# Optimizing a Trainium2 kernel written in Bass

```python
import numpy as np
import jax
import jax.numpy as jnp

def _softmax(x, axis=-1):
    return jax.nn.softmax(x, axis=axis)

def _gelu(x):
    return jax.nn.gelu(x, approximate=True)

def _silu(x):
    return jax.nn.silu(x)

def _sigmoid(x):
    return jax.nn.sigmoid(x)

def _layernorm(x, axis=-1, eps=1e-05):
    m = jnp.mean(x, axis=axis, keepdims=True)
    v = jnp.var(x, axis=axis, keepdims=True)
    return (x - m) / jnp.sqrt(v + eps)

def _scatter_add(tgt, idx, src, axis=0):
    return tgt.at[idx].add(src)

def _segment_sum(src, seg, n):
    return jax.ops.segment_sum(src, seg, n)
kernel_name = 'mk_adj_preln_d4_adj_r2_39b4b2'

def setup_inputs(seed: int=0):
    np.random.seed(seed)
    _w = jnp.asarray

    def _rec_inputs():
        import jax
        import jax.numpy as jnp
        _gk = jax.random.key(seed)
        x = -0.0005207 + 1.001 * jax.random.normal(jax.random.fold_in(_gk, 1), (2048, 256), jnp.float32)
        _w = (1.0 + jnp.arange(2048, dtype=jnp.float32)) ** (-0.5)
        _w = _w / _w.mean()
        _pij = jnp.clip(0.0078125 * _w[:, None] * _w[None, :], 0.0, 1.0)
        _a = jax.random.uniform(jax.random.fold_in(_gk, 2), (2048, 2048)) < _pij
        _af = _a.astype(jnp.float32)
        adj = _af
        return (x, adj)
    x, adj = _rec_inputs()

    def _L0_gnn_setup():
        import jax, jax.numpy as jnp
        import numpy as np
        N = 2048
        INPUT_DIM = 256
        KEY_DIM = 64
        OUT_DIM = 256
        N_HEADS = 8
        IDENTITY_BIAS = 0.01
        MASK_VAL = 1e+16

        def _xavier(key, shape, gain=np.sqrt(2.0)):
            std = gain * np.sqrt(2.0 / (shape[-2] + shape[-1]))
            return jax.random.normal(key, shape, dtype=jnp.float32) * np.float32(std)
        key = jax.random.key(seed)
        kx, ka, kk, kq, kv, ko = jax.random.split(key, 6)
        node_matrix = jax.random.normal(kx, (N, INPUT_DIM), dtype=jnp.float32)
        adjacency_matrix = jax.random.bernoulli(ka, 0.01, (N, N)).astype(jnp.float32)
        Wks = _xavier(kk, (N_HEADS, INPUT_DIM, KEY_DIM))
        Wqs = _xavier(kq, (N_HEADS, INPUT_DIM, KEY_DIM))
        Wvs = _xavier(kv, (N_HEADS, INPUT_DIM, KEY_DIM))
        Wo = _xavier(ko, (N_HEADS, KEY_DIM, OUT_DIM))
        return {'node_matrix': node_matrix, 'adjacency_matrix': adjacency_matrix, 'Wks': Wks, 'Wqs': Wqs, 'Wvs': Wvs, 'Wo': Wo}
    _L0_gnn_all = _L0_gnn_setup()
    _L0_gnn_in = {k: v for k, v in _L0_gnn_all.items() if k in ('Wks', 'Wqs', 'Wvs', 'Wo')}
    del _L0_gnn_all

    def _L1_gnn_setup():
        import jax, jax.numpy as jnp
        import numpy as np
        N = 4096
        F_IN = 256
        F_OUT = 256
        DENSITY = 0.01
        key = jax.random.key(seed)
        k_x, k_adj, k_w, k_b = jax.random.split(key, 4)
        input_features = jax.random.normal(k_x, (N, F_IN), dtype=jnp.float32)
        adj = (jax.random.uniform(k_adj, (N, N)) < DENSITY).astype(jnp.float32)
        idx = jnp.arange(N)
        adj = adj.at[idx, idx].set(1.0)
        W = jax.random.normal(k_w, (F_IN, F_OUT), dtype=jnp.float32) / np.sqrt(F_IN)
        b = jax.random.normal(k_b, (F_OUT,), dtype=jnp.float32) * 0.01
        return {'input_features': input_features, 'adj': adj, 'W': W, 'b': b}
    _L1_gnn_all = _L1_gnn_setup()
    _L1_gnn_in = {k: v for k, v in _L1_gnn_all.items() if k in ('W', 'b')}
    del _L1_gnn_all

    def _L2_gnn_setup():
        import jax, jax.numpy as jnp
        import numpy as np
        N, IN_F, OUT_F = (4096, 256, 256)
        HID = OUT_F // 2
        key = jax.random.key(seed)
        ks = jax.random.split(key, 6)
        x = jax.random.normal(ks[0], (N, IN_F), dtype=jnp.float32)
        adj = jax.random.uniform(ks[1], (N, N), dtype=jnp.float32)
        W1 = jax.random.normal(ks[2], (HID, IN_F), dtype=jnp.float32) * np.sqrt(2.0 / IN_F)
        b1 = jnp.zeros((HID,), dtype=jnp.float32)
        W2 = jax.random.normal(ks[3], (OUT_F, HID), dtype=jnp.float32) * np.sqrt(2.0 / HID)
        b2 = jnp.zeros((OUT_F,), dtype=jnp.float32)
        return {'x': x, 'adj': adj, 'W1': W1, 'b1': b1, 'W2': W2, 'b2': b2}
    _L2_gnn_all = _L2_gnn_setup()
    _L2_gnn_in = {k: v for k, v in _L2_gnn_all.items() if k in ('W1', 'b1', 'W2', 'b2')}
    del _L2_gnn_all

    def _L3_gnn_setup():
        import jax, jax.numpy as jnp
        import numpy as np
        N = 2048
        D = 256
        H = 4
        NEG = -10000000000.0
        ALPHA = 0.3
        key = jax.random.key(seed)
        ks = jax.random.split(key, 8)
        nodes = jax.random.normal(ks[0], (N, D), dtype=jnp.float32)
        adj = (jax.random.uniform(ks[1], (N, N)) < 0.01).astype(jnp.float32)
        adj = jnp.maximum(adj, jnp.eye(N, dtype=jnp.float32))
        s = 0.05
        W_node = jax.random.normal(ks[2], (D, D), dtype=jnp.float32) * s
        b_node = jnp.zeros((D,), dtype=jnp.float32)
        K = jax.random.normal(ks[3], (H, D, D), dtype=jnp.float32) * s
        A_self = jax.random.normal(ks[4], (H, D), dtype=jnp.float32) * s
        A_neigh = jax.random.normal(ks[5], (H, D), dtype=jnp.float32) * s
        return {'nodes': nodes, 'adj': adj, 'W_node': W_node, 'b_node': b_node, 'K': K, 'A_self': A_self, 'A_neigh': A_neigh, 'num_heads': H}
    _L3_gnn_all = _L3_gnn_setup()
    _L3_gnn_in = {k: v for k, v in _L3_gnn_all.items() if k in ('W_node', 'b_node', 'K', 'A_self', 'A_neigh')}
    del _L3_gnn_all
    return {'x': x, 'adj': adj, 'L0_gnn_Wks': _L0_gnn_in['Wks'], 'L0_gnn_Wqs': _L0_gnn_in['Wqs'], 'L0_gnn_Wvs': _L0_gnn_in['Wvs'], 'L0_gnn_Wo': _L0_gnn_in['Wo'], 'L1_gnn_W': _L1_gnn_in['W'], 'L1_gnn_b': _L1_gnn_in['b'], 'L2_gnn_W1': _L2_gnn_in['W1'], 'L2_gnn_b1': _L2_gnn_in['b1'], 'L2_gnn_W2': _L2_gnn_in['W2'], 'L2_gnn_b2': _L2_gnn_in['b2'], 'L3_gnn_W_node': _L3_gnn_in['W_node'], 'L3_gnn_b_node': _L3_gnn_in['b_node'], 'L3_gnn_K': _L3_gnn_in['K'], 'L3_gnn_A_self': _L3_gnn_in['A_self'], 'L3_gnn_A_neigh': _L3_gnn_in['A_neigh']}

def reference(x, adj, L0_gnn_Wks, L0_gnn_Wqs, L0_gnn_Wvs, L0_gnn_Wo, L1_gnn_W, L1_gnn_b, L2_gnn_W1, L2_gnn_b1, L2_gnn_W2, L2_gnn_b2, L3_gnn_W_node, L3_gnn_b_node, L3_gnn_K, L3_gnn_A_self, L3_gnn_A_neigh):
    import jax
    import jax.numpy as jnp

    def _L0_gnn_ref(node_matrix, adjacency_matrix, Wks, Wqs, Wvs, Wo):
        import jax, jax.numpy as jnp
        import numpy as np
        N = 2048
        INPUT_DIM = 256
        KEY_DIM = 64
        OUT_DIM = 256
        N_HEADS = 8
        IDENTITY_BIAS = 0.01
        MASK_VAL = 1e+16

        def _xavier(key, shape, gain=np.sqrt(2.0)):
            std = gain * np.sqrt(2.0 / (shape[-2] + shape[-1]))
            return jax.random.normal(key, shape, dtype=jnp.float32) * np.float32(std)
        n = node_matrix.shape[0]
        kd = Wks.shape[-1]
        eye = jnp.eye(n, dtype=node_matrix.dtype)
        adj = jnp.maximum(adjacency_matrix, eye)
        q = jnp.einsum('nd,hdk->hnk', node_matrix, Wqs)
        k = jnp.einsum('nd,hdk->hnk', node_matrix, Wks)
        v = jnp.einsum('nd,hdk->hnk', node_matrix, Wvs)
        scores = jnp.einsum('hqk,hmk->hqm', q, k) * kd ** (-0.5)
        scores = scores + IDENTITY_BIAS * eye - MASK_VAL * (1.0 - adj)
        att = jax.nn.softmax(scores, axis=-1)
        return jnp.einsum('hqm,hmk,hko->qo', att, v, Wo)

    def _L1_gnn_ref(input_features, adj, W, b):
        import jax, jax.numpy as jnp
        import numpy as np
        N = 4096
        F_IN = 256
        F_OUT = 256
        DENSITY = 0.01
        A = (adj != 0).astype(input_features.dtype)
        hidden = input_features @ W + b
        deg = jnp.sum(A, axis=0)
        return A @ hidden / deg[:, None]

    def _L2_gnn_ref(x, adj, W1, b1, W2, b2):
        import jax, jax.numpy as jnp
        import numpy as np
        N, IN_F, OUT_F = (4096, 256, 256)
        HID = OUT_F // 2
        h = x @ W1.T + b1
        h = h @ W2.T + b2
        A = adj + jnp.eye(adj.shape[0], dtype=adj.dtype)
        rowsum = A.sum(axis=1)
        r_inv_sqrt = jnp.power(rowsum, -0.5)
        r_inv_sqrt = jnp.where(jnp.isinf(r_inv_sqrt), 0.0, r_inv_sqrt)
        A = r_inv_sqrt[:, None] * A * r_inv_sqrt[None, :]
        return A.astype(jnp.float32) @ h.astype(jnp.float32)

    def _L3_gnn_ref(nodes, adj, W_node, b_node, K, A_self, A_neigh, num_heads):
        import jax, jax.numpy as jnp
        import numpy as np
        N = 2048
        D = 256
        H = 4
        NEG = -10000000000.0
        ALPHA = 0.3
        x = nodes @ W_node + b_node
        feats = jnp.einsum('nd,hdf->hnf', x, K)
        s = jnp.einsum('hnf,hf->hn', feats, A_self) + jnp.einsum('hnf,hf->hn', feats, A_neigh)
        s = jnp.where(s > 0, s, ALPHA * s)
        logits = s[:, :, None] + NEG * (1.0 - adj)[None]
        attn = jax.nn.softmax(logits, axis=-1)
        out = jnp.einsum('hij,hjf->hif', attn, feats)
        out = jnp.mean(out, axis=0)
        return jax.nn.relu(out)
    h = jnp.maximum(_layernorm(x, axis=-1), 0.0)
    x = x + _L0_gnn_ref(h, adj, L0_gnn_Wks, L0_gnn_Wqs, L0_gnn_Wvs, L0_gnn_Wo)
    h = jnp.maximum(_layernorm(x, axis=-1), 0.0)
    x = x + _L1_gnn_ref(h, adj, L1_gnn_W, L1_gnn_b)
    h = jnp.maximum(_layernorm(x, axis=-1), 0.0)
    x = x + _L2_gnn_ref(h, adj, L2_gnn_W1, L2_gnn_b1, L2_gnn_W2, L2_gnn_b2)
    h = jnp.maximum(_layernorm(x, axis=-1), 0.0)
    x = x + _L3_gnn_ref(h, adj, L3_gnn_W_node, L3_gnn_b_node, L3_gnn_K, L3_gnn_A_self, L3_gnn_A_neigh, 4)
    return x

_drawn_inputs = setup_inputs


def setup_inputs(seed=0):
    import zlib

    import numpy as np

    out = dict(_drawn_inputs(seed))
    spreads = {'L2_gnn_b1': (0.0, 0.1), 'L2_gnn_b2': (0.0, 0.1), 'L3_gnn_b_node': (0.0, 0.743)}
    factors = {'L1_gnn_b': 8.0}
    for name, (base, spread) in spreads.items():
        noise = np.random.default_rng([zlib.crc32(name.encode()), seed]).standard_normal(out[name].shape)
        drawn = base * np.exp(spread * noise) if base else spread * noise
        out[name] = jnp.asarray(drawn.astype(out[name].dtype))
    for name, factor in factors.items():
        out[name] = (out[name] * factor).astype(out[name].dtype)
    return out
```

```python
from contextlib import ExitStack

import concourse.bass as bass
from concourse import mybir

F32 = mybir.dt.float32
F32R = mybir.dt.float32r
BF16 = mybir.dt.bfloat16
U8 = mybir.dt.uint8
ALU = mybir.AluOpType
ACT = mybir.ActivationFunctionType
AX = mybir.AxisListType

P = 128
N = 2048
D = 256
HEADS = 8
HD = 64
PAIRS = HEADS // 2
TILES = N // P
DC = D // P
BANK = 512
QUARTERS = N // BANK
CHUNKS = HEADS * QUARTERS
GAT_HEADS = 4
DX = D + GAT_HEADS
EPS = 1e-5
SCORE_SCALE = float(HD) ** -0.5
IDENTITY_BIAS = 0.01
MASK_VAL = 1e16
NEG = -1e10
ALPHA = 0.3
HUGE = 3.0e38


def ds(i, size):
    return bass.ds(i * size, size)


def wait(eng, sem, value):
    if isinstance(value, int) and value <= 0:
        return
    eng.wait_ge(sem, value)


def wait_apart(eng, sem, value, passed):
    wait(eng, sem, value)
    if not isinstance(value, int):
        eng.sem_inc(passed, 1)


def project_keys_values(nc, x, k_stack, v, w, ident, eps, mv, rstd, dram):
    with ExitStack() as ctx:
        def sb(name, shape, dt=F32):
            return ctx.enter_context(nc.sbuf_tensor(name, shape, dt))

        def sem(name):
            return ctx.enter_context(nc.semaphore(name))

        wk = sb("wk", [P, DC, HEADS * HD])
        wv = sb("wv", [P, DC, HEADS * HD])
        stats = sb("a_stats", [P, TILES, 6])
        std = sb("a_std", [P, TILES])
        xc = sb("a_xc", [P, 2, D])
        hT = sb("a_hT", [P, 2, DC, BANK])
        k_hi = sb("k_hi", [P, 2, BANK], F32R)
        k_lo = sb("k_lo", [P, 2, BANK], F32R)
        turn_ps = [ctx.enter_context(nc.psum_tensor(f"a_turn{i}", [P, BANK], F32)) for i in range(2)]
        v_ps = [ctx.enter_context(nc.psum_tensor(f"a_v{i}", [P, BANK], F32)) for i in range(2)]
        k_ps = [ctx.enter_context(nc.psum_tensor(f"a_k{i}", [P, BANK], F32)) for i in range(PAIRS)]

        x_loaded = [sem(f"x_loaded{c}") for c in range(QUARTERS)]
        kv_weights = sem("kv_weights")
        const_loaded = sem("const_loaded")
        ident_cleared = sem("ident_cleared")
        ident_ready = sem("ident_ready")
        ln_step = sem("a_ln_step")
        stats_ready = sem("a_stats_ready")
        std_ready = sem("a_std_ready")
        rstd_ready = sem("a_rstd_ready")
        centred = sem("a_centred")
        turned = sem("a_turned")
        relu_done = sem("a_relu_done")
        v_ready = sem("v_ready")
        v_copied = sem("v_copied")
        k_ready = sem("k_ready")
        k_high = sem("k_high")
        k_split = sem("k_split")
        k_stacked = [sem(f"k_stacked{i}") for i in range(2)]
        consts_built = sem("consts_built")
        TPC = TILES // QUARTERS

        with nc.Block() as block:

            @block.sync
            def _(sp):
                x_view = dram["x"].rearrange("(t p) d -> p t d", p=P)
                for c in range(QUARTERS):
                    sp.dma_start(x[:, c * TPC:(c + 1) * TPC, :], x_view[:, c * TPC:(c + 1) * TPC, :])\
                        .then_inc(x_loaded[c], 16)
                    if c == 0:
                        for dst, name in ((wk, "L0_gnn_Wks"), (wv, "L0_gnn_Wvs")):
                            for d in range(DC):
                                sp.dma_start(dst[:, d, :].rearrange("p (h k) -> p h k", h=HEADS),
                                             dram[name][:, d * P:(d + 1) * P, :].rearrange("h p k -> p h k"))\
                                    .then_inc(kv_weights, 16)
                for d in range(DC):
                    sp.dma_start(w["q"][:, d, :].rearrange("p (h k) -> p h k", h=HEADS),
                                 dram["L0_gnn_Wqs"][:, d * P:(d + 1) * P, :].rearrange("h p k -> p h k"))\
                        .then_inc(const_loaded, 16)
                sp.dma_start(w["o"][:, :, :], dram["L0_gnn_Wo"].rearrange("(r a) k o -> (a k) r o", a=2))\
                    .then_inc(const_loaded, 16)
                for n in range(QUARTERS * PAIRS):
                    c, p = divmod(n, PAIRS)
                    cols = slice(c * BANK, (c + 1) * BANK)
                    sp.wait_ge(k_split, n + 1)
                    for half in range(2):
                        src = slice(half * HD, (half + 1) * HD)
                        sp.dma_start(k_stack[0:HD, 2 * p + half, cols].bitcast(F32), k_hi[src, n % 2, :].bitcast(F32))\
                            .then_inc(k_stacked[n % 2], 16)
                        sp.dma_start(k_stack[HD:P, 2 * p + half, cols].bitcast(F32), k_lo[src, n % 2, :].bitcast(F32))\
                            .then_inc(k_stacked[n % 2], 16)
                for i in range(2):
                    sp.wait_ge(k_stacked[i], 64 * QUARTERS * PAIRS // 2)
                sp.wait_ge(const_loaded, 16 * (DC + 1))

            @block.gpsimd
            def _(pool):
                nc.gpsimd.memset(ident["i"][:, :], 0.0).then_inc(ident_cleared, 1)
                nc.gpsimd.memset(ident["not"][:, :], 1.0).then_inc(ident_cleared, 1)
                nc.gpsimd.memset(ident["bias"][:, :], 0.0).then_inc(ident_cleared, 1)
                nc.gpsimd.memset(eps[:, :], EPS).then_inc(ident_cleared, 1)
                pool.wait_ge(ident_cleared, 4)
                for name, fill in (("i", 1.0), ("not", 0.0), ("bias", -IDENTITY_BIAS)):
                    nc.gpsimd.affine_select(out=ident[name][:, :], in_=ident[name][:, :],
                                            compare_op=ALU.not_equal, fill=fill, base=0,
                                            pattern=[[-1, P]], channel_multiplier=1)\
                        .then_inc(ident_ready, 1)
                pool.wait_ge(ident_ready, 3)

            @block.vector
            def _(dve):
                def layer_norm(t):
                    dve.wait_ge(std_ready, t + 1)
                    nc.vector.reciprocal(rstd[:, t:t + 1], std[:, t:t + 1]).then_inc(rstd_ready, 1)
                    dve.wait_ge(rstd_ready, t + 1)
                    wait(dve, turned, t - 1)
                    nc.vector.tensor_scalar(xc[:, t % 2, :], x[:, t, :], mv[:, t, 0:1], rstd[:, t:t + 1],
                                            ALU.subtract, ALU.mult).then_inc(centred, 1)

                def statistics(t):
                    if t % TPC == 0:
                        dve.wait_ge(x_loaded[t // TPC], 16)
                    nc.vector.bn_stats(stats[:, t, :], x[:, t, :]).then_inc(ln_step, 1)
                    dve.wait_ge(ln_step, t + 1)
                    nc.vector.bn_aggr(mv[:, t, :], stats[:, t, :]).then_inc(stats_ready, 1)

                statistics(0)
                statistics(1)
                for t in range(TPC):
                    statistics(t + 2)
                    layer_norm(t)
                for c in range(QUARTERS):
                    if c + 1 < QUARTERS:
                        for t in range((c + 1) * TPC, (c + 2) * TPC):
                            if t + 2 < TILES:
                                statistics(t + 2)
                            layer_norm(t)
                    for p in range(PAIRS):
                        n = c * PAIRS + p
                        dve.wait_ge(k_ready, n + 1)
                        wait(dve, k_stacked[n % 2], 64 * (n // 2))
                        nc.vector.tensor_copy(k_hi[:, n % 2, :], k_ps[p][:, :]).then_inc(k_high, 1)
                        dve.wait_ge(k_high, n + 1)
                        nc.vector.tensor_tensor(k_lo[:, n % 2, :], k_ps[p][:, :],
                                                k_hi[:, n % 2, :].bitcast(F32), ALU.subtract)\
                            .then_inc(k_split, 1)

            @block.scalar
            def _(act):
                def relu(t):
                    act.wait_ge(turned, t + 1)
                    c = t // TPC
                    wait(act, k_ready, PAIRS * (c - 1))
                    nc.scalar.activation(hT[:, c % 2, :, (t % TPC) * P:(t % TPC + 1) * P],
                                         turn_ps[t % 2][:, 0:D].rearrange("p (c n) -> p c n", c=DC),
                                         ACT.Relu).then_inc(relu_done, 1)

                def deviation(t):
                    act.wait_ge(stats_ready, t + 1)
                    nc.scalar.activation(std[:, t:t + 1], mv[:, t, 1:2], ACT.Sqrt, bias=eps[:, :])\
                        .then_inc(std_ready, 1)

                act.wait_ge(ident_cleared, 4)
                deviation(0)
                deviation(1)
                for t in range(TPC):
                    deviation(t + 2)
                    relu(t)
                for c in range(QUARTERS):
                    if c + 1 < QUARTERS:
                        for t in range((c + 1) * TPC, (c + 2) * TPC):
                            if t + 2 < TILES:
                                deviation(t + 2)
                            relu(t)
                    for t in range(c * TPC, (c + 1) * TPC):
                        act.wait_ge(v_ready, t + 1)
                        nc.scalar.activation(v[:, t, :], v_ps[t % 2][:, :], ACT.Copy).then_inc(v_copied, 1)
                act.wait_ge(v_copied, TILES)

            @block.tensor
            def _(pe):
                def turn(t):
                    pe.wait_ge(centred, t + 1)
                    wait(pe, relu_done, t - 1)
                    for d in range(DC):
                        last = nc.tensor.transpose(turn_ps[t % 2][:, d * P:(d + 1) * P],
                                                   xc[:, t % 2, d * P:(d + 1) * P], ident["i"][:, :])
                    last.then_inc(turned, 1)

                pe.wait_ge(ident_ready, 3)
                for t in range(TPC):
                    turn(t)
                pe.wait_ge(kv_weights, 16 * 2 * DC)
                for c in range(QUARTERS):
                    if c + 1 < QUARTERS:
                        for t in range((c + 1) * TPC, (c + 2) * TPC):
                            turn(t)
                    for t in range(c * TPC, (c + 1) * TPC):
                        pe.wait_ge(relu_done, t + 1)
                        wait(pe, v_copied, t - 1)
                        for d in range(DC):
                            last = nc.tensor.matmul(v_ps[t % 2][:, :],
                                                    hT[:, c % 2, d, (t % TPC) * P:(t % TPC + 1) * P],
                                                    wv[:, d, :], start=(d == 0), stop=(d == DC - 1))
                        last.then_inc(v_ready, 1)
                    for p in range(PAIRS):
                        wait(pe, k_split, (c - 1) * PAIRS + p + 1)
                        for d in range(DC):
                            last = nc.tensor.matmul(k_ps[p][:, :], wk[:, d, p * P:(p + 1) * P],
                                                    hT[:, c % 2, d, :], start=(d == 0), stop=(d == DC - 1))
                        last.then_inc(k_ready, 1)


def attend(nc, x, k_stack, v, w, ident, mv, rstd, col_count, dram):
    with ExitStack() as ctx:
        def sb(name, shape, dt=F32):
            return ctx.enter_context(nc.sbuf_tensor(name, shape, dt))

        def sem(name):
            return ctx.enter_context(nc.semaphore(name))

        def ps(name):
            return ctx.enter_context(nc.psum_tensor(name, [P, BANK], F32))

        adj = sb("adj_tile", [P, N])
        mask = sb("mask", [P, N])
        probs = sb("probs", [P, 4, N])
        probs_T = sb("probs_T", [P, 2, 2, BANK])
        q_hi = sb("q_hi", [P, PAIRS, P], F32R)
        q_lo = sb("q_lo", [P, PAIRS, P], F32R)
        q_stack = sb("q_stack", [P, HEADS, 2, P], F32R)
        xc = sb("b_xc", [P, D])
        hT = sb("b_hT", [P, DC, P])
        chunk_min = sb("chunk_min", [P, 2, QUARTERS])
        head_min = sb("head_min", [P, HEADS])
        prob_sum = sb("prob_sum", [P, HEADS])
        inv_cols = sb("inv_cols", [P, 2, HD])
        inv_rows = sb("inv_rows", [P, 2, P])
        heads_T = sb("heads_T", [P, PAIRS, P])
        S = [ps(f"scores{i}") for i in range(3)]
        T = [ps(f"turn{i}") for i in range(2)]
        O = [ps(f"heads{i}") for i in range(2)]
        M = ps("misc")

        adj_loaded = sem("adj_loaded")
        sp_passed = sem("b_sp_passed")
        dve_passed = sem("b_dve_passed")
        mask_step = sem("mask_step")
        count_cleared = sem("count_cleared")
        counted = sem("counted")
        centred = sem("b_centred")
        x_turned = sem("b_x_turned")
        relu_done = sem("b_relu_done")
        q_ready = sem("q_ready")
        q_high = sem("q_high")
        q_split = sem("q_split")
        q_stacked = [sem(f"q_stacked{p}") for p in range(PAIRS)]
        scores_ready = sem("scores_ready")
        scores_read = sem("scores_read")
        head_masked = sem("head_masked")
        probs_ready = sem("probs_ready")
        turned = [sem("even_turned"), sem("odd_turned")]
        copied = [sem("even_copied"), sem("odd_copied")]
        quarter_used = sem("quarter_used")
        inv_ready = sem("inv_ready")
        inv_turned = sem("inv_turned")
        inv_copied = sem("inv_copied")
        pair_normed = sem("pair_normed")
        out_ready = sem("out_ready")
        x_added = sem("x_added")

        def chunk_bank(j):
            return S[j % 3]

        def over_tiles(eng, body):
            body(0, False, True, True)
            with eng.Fori(1, TILES - 1) as t:
                body(t, True, True, True)
            body(TILES - 1, True, True, False)
            body(TILES, True, False, False)

        with nc.Block() as block:

            @block.sync
            def _(sp):
                adj_rows = dram["adj"].rearrange("(t p) n -> t p n", p=P)

                def load_adj(n):
                    wait_apart(sp, mask_step, 3 * (n - 1) + 1, sp_passed)
                    wait_apart(sp, counted, n, sp_passed)
                    sp.dma_start(adj[:, :], adj_rows[ds(n, 1), :, :].rearrange("a p n -> (a p) n"))\
                        .then_inc(adj_loaded, 16)

                def stack_queries(n, p):
                    wait_apart(sp, q_split, n + 1, sp_passed)
                    wait_apart(sp, scores_ready, CHUNKS * (n - 1) + 2 * QUARTERS * (p + 1), sp_passed)
                    for half in range(2):
                        src = slice(half * HD, (half + 1) * HD)
                        for part, (low, high) in enumerate(((q_hi, q_lo), (q_lo, q_hi))):
                            sp.dma_start(q_stack[0:HD, 2 * p + half, part, :].bitcast(F32), low[src, p, :].bitcast(F32))\
                                .then_inc(q_stacked[p], 16)
                            sp.dma_start(q_stack[HD:P, 2 * p + half, part, :].bitcast(F32), high[src, p, :].bitcast(F32))\
                                .then_inc(q_stacked[p], 16)

                sp.dma_start(adj[:, :], adj_rows[0, :, :]).then_inc(adj_loaded, 16)
                for p in range(PAIRS):
                    stack_queries(0, p)

                def body(t, has_prev, has_cur, has_next):
                    if has_next:
                        load_adj(t + 1)
                        for p in range(PAIRS):
                            stack_queries(t + 1, p)

                over_tiles(sp, body)

            @block.gpsimd
            def _(pool):
                nc.gpsimd.memset(col_count[:, :], 0.0).then_inc(count_cleared, 1)
                pool.wait_ge(count_cleared, 1)

                def body(n):
                    pool.wait_ge(adj_loaded, 16 * (n + 1))
                    wait(pool, counted, n)
                    nc.gpsimd.tensor_tensor(col_count[:, :], adj[:, :], col_count[:, :], ALU.add)\
                        .then_inc(counted, 1)

                body(0)
                with pool.Fori(1, TILES) as n:
                    body(n)
                pool.wait_ge(counted, TILES)

            @block.vector
            def _(dve):
                def build_mask(n):
                    dve.wait_ge(adj_loaded, 16 * (n + 1))
                    nc.vector.tensor_scalar(mask[:, :], adj[:, :], -MASK_VAL, MASK_VAL,
                                            ALU.mult, ALU.add).then_inc(mask_step, 1)
                    dve.wait_ge(mask_step, 3 * n + 1)
                    own = mask[:, ds(n, P)]
                    nc.vector.tensor_tensor(own, own, ident["not"][:, :], ALU.mult).then_inc(mask_step, 1)
                    dve.wait_ge(mask_step, 3 * n + 2)
                    nc.vector.tensor_tensor(own, own, ident["bias"][:, :], ALU.add).then_inc(mask_step, 1)
                    dve.wait_ge(mask_step, 3 * n + 3)

                def layer_norm(n):
                    own = x[:, ds(n, 1), :].rearrange("p a d -> p (a d)")
                    wait(dve, x_turned, n)
                    nc.vector.tensor_scalar(xc[:, :], own, mv[:, ds(n, 1), 0], rstd[:, ds(n, 1)],
                                            ALU.subtract, ALU.mult).then_inc(centred, 1)

                def split_queries(n):
                    dve.wait_ge(q_high, n + 1)
                    nc.vector.scalar_tensor_tensor(
                        out=q_lo[:, :, :], in0=M[:, :].rearrange("p (a n) -> p a n", a=PAIRS),
                        scalar=-SCORE_SCALE, in1=q_hi[:, :, :].bitcast(F32),
                        op0=ALU.mult, op1=ALU.subtract).then_inc(q_split, 1)

                def mask_scores(t, pair, j):
                    half, c = divmod(j, QUARTERS)
                    h = 2 * pair + half
                    i = h * QUARTERS + c
                    wait_apart(dve, scores_ready, CHUNKS * t + i + 1, dve_passed)
                    if c == 0:
                        wait_apart(dve, turned[half], QUARTERS * PAIRS * t + QUARTERS * (pair - 1), dve_passed)
                    nc.vector.tensor_tensor_reduce(
                        probs[:, h % 4, c * BANK:(c + 1) * BANK], chunk_bank(i)[:, :],
                        mask[:, c * BANK:(c + 1) * BANK], 1.0, HUGE, ALU.add, ALU.min,
                        chunk_min[:, half, c:c + 1]).then_inc(scores_read, 1)
                    if c == QUARTERS - 1:
                        dve.wait_ge(scores_read, CHUNKS * t + i + 1)
                        nc.vector.tensor_reduce(head_min[:, h:h + 1], chunk_min[:, half, :], AX.X, ALU.min)\
                            .then_inc(head_masked, 1)

                build_mask(0)
                layer_norm(0)
                split_queries(0)

                def body(t, has_prev, has_cur, has_next):
                    for pair in range(PAIRS):
                        g = PAIRS * t + pair
                        for k in range(QUARTERS):
                            if has_cur:
                                mask_scores(t, pair, 2 * k)
                                mask_scores(t, pair, 2 * k + 1)
                            turn_prev = (has_cur or pair == 0) and (has_prev or pair >= 1)
                            if turn_prev:
                                q = QUARTERS * (g - 1) + k
                                dve.wait_ge(turned[1], q + 1)
                                wait(dve, quarter_used, q - 1)
                                nc.vector.tensor_copy(probs_T[:, k % 2, 1, :], T[1][:, :])\
                                    .then_inc(copied[1], 1)
                            if turn_prev and k == 0:
                                prev = (pair - 1) % PAIRS
                                dve.wait_ge(probs_ready, 2 * g)
                                wait(dve, inv_turned, g - 1)
                                nc.vector.reciprocal(
                                    inv_cols[:, :, :],
                                    prob_sum[:, 2 * prev:2 * prev + 2].unsqueeze(2).to_broadcast([P, 2, HD]))\
                                    .then_inc(inv_ready, 1)
                            norm_prev = (has_cur or pair <= 1) and (has_prev or pair >= 2)
                            if norm_prev and k == 1:
                                prev = (pair - 2) % PAIRS
                                dve.wait_ge(quarter_used, QUARTERS * (g - 1))
                                dve.wait_ge(inv_copied, g - 1)
                                nc.vector.tensor_tensor(heads_T[:, prev, :], O[pair % 2][:, 0:P],
                                                        inv_rows[:, pair % 2, :], ALU.mult)\
                                    .then_inc(pair_normed, 1)
                            if has_next and pair == 1 and k == 2:
                                layer_norm(t + 1)
                            if has_prev and pair == 2 and k == 0:
                                dve.wait_ge(out_ready, t)
                                own = x[:, ds(t - 1, 1), :].rearrange("p a d -> p (a d)")
                                nc.vector.tensor_tensor(own, M[:, 0:D], own, ALU.add).then_inc(x_added, 1)
                            if has_next and pair == 3 and k == 0:
                                split_queries(t + 1)
                    if has_next:
                        build_mask(t + 1)

                over_tiles(dve, body)
                dve.wait_ge(x_added, TILES)

            @block.scalar
            def _(act):
                def relu(n):
                    act.wait_ge(x_turned, n + 1)
                    wait(act, q_ready, n)
                    nc.scalar.activation(hT[:, :, :], M[:, 0:D].rearrange("p (c n) -> p c n", c=DC),
                                         ACT.Relu).then_inc(relu_done, 1)

                def round_queries(n):
                    act.wait_ge(q_ready, n + 1)
                    for p in range(PAIRS):
                        wait(act, q_stacked[p], 128 * n)
                    nc.scalar.activation(q_hi[:, :, :], M[:, :].rearrange("p (a n) -> p a n", a=PAIRS),
                                         ACT.Copy, scale=-SCORE_SCALE).then_inc(q_high, 1)

                relu(0)
                round_queries(0)

                def body(t, has_prev, has_cur, has_next):
                    for pair in range(PAIRS):
                        g = PAIRS * t + pair
                        for k in range(QUARTERS):
                            turn_prev = (has_cur or pair == 0) and (has_prev or pair >= 1)
                            if turn_prev:
                                q = QUARTERS * (g - 1) + k
                                act.wait_ge(turned[0], q + 1)
                                wait(act, quarter_used, q - 1)
                                nc.scalar.activation(probs_T[:, k % 2, 0, :], T[0][:, :], ACT.Copy)\
                                    .then_inc(copied[0], 1)
                            if turn_prev and k == 1:
                                act.wait_ge(inv_turned, g)
                                wait(act, pair_normed, g - 2)
                                nc.scalar.activation(inv_rows[:, (pair - 1) % 2, :], M[:, 0:P], ACT.Copy)\
                                    .then_inc(inv_copied, 1)
                            if has_next and pair == 2 and k == 0:
                                relu(t + 1)
                            if has_next and pair == 2 and k == 3:
                                round_queries(t + 1)
                            if has_cur and k % 2 == 1:
                                h = 2 * pair + k // 2
                                act.wait_ge(head_masked, HEADS * t + h + 1)
                                nc.scalar.activation(probs[:, h % 4, :], probs[:, h % 4, :], ACT.Exp,
                                                     bias=head_min[:, h:h + 1], scale=-1.0,
                                                     accum_out=prob_sum[:, h:h + 1]).then_inc(probs_ready, 1)

                over_tiles(act, body)

            @block.tensor
            def _(pe):
                def turn_x(n):
                    pe.wait_ge(centred, n + 1)
                    for d in range(DC):
                        last = nc.tensor.transpose(M[:, d * P:(d + 1) * P], xc[:, d * P:(d + 1) * P],
                                                   ident["i"][:, :])
                    last.then_inc(x_turned, 1)

                def project_queries(n):
                    pe.wait_ge(relu_done, n + 1)
                    for p in range(PAIRS):
                        for d in range(DC):
                            last = nc.tensor.matmul(M[:, p * P:(p + 1) * P], w["q"][:, d, p * P:(p + 1) * P],
                                                    hT[:, d, :], start=(d == 0), stop=(d == DC - 1))
                    last.then_inc(q_ready, 1)

                turn_x(0)
                project_queries(0)

                def scores(t, pair, j):
                    half, c = divmod(j, QUARTERS)
                    h = 2 * pair + half
                    i = h * QUARTERS + c
                    if j == 0:
                        pe.wait_ge(q_stacked[pair], 128 * (t + 1))
                    if i >= 3:
                        pe.wait_ge(scores_read, CHUNKS * t + i - 2)
                    else:
                        wait(pe, scores_read, CHUNKS * t - (1, 0, 2)[i])
                    keys = k_stack[:, h, c * BANK:(c + 1) * BANK]
                    for part in range(2):
                        last = nc.tensor.matmul(chunk_bank(i)[:, :], q_stack[:, h, part, :], keys,
                                                start=(part == 0), stop=(part == 1))
                    last.then_inc(scores_ready, 1)

                def turn_probs(pair, g, k):
                    for half in range(2):
                        slot = (2 * pair + half) % 4
                        if k == 0:
                            pe.wait_ge(probs_ready, 2 * g + half + 1)
                        wait(pe, copied[half], QUARTERS * g + k)
                        for b in range(BANK // P):
                            m = k * (BANK // P) + b
                            last = nc.tensor.transpose(T[half][:, b * P:(b + 1) * P],
                                                       probs[:, slot, m * P:(m + 1) * P], ident["i"][:, :])
                        last.then_inc(turned[half], 1)

                def weigh_values(pair, g, k):
                    for half in range(2):
                        pe.wait_ge(copied[half], QUARTERS * g + k + 1)
                    if k == 0:
                        wait(pe, pair_normed, g - 1)
                    for b in range(BANK // P):
                        m = k * (BANK // P) + b
                        for half in range(2):
                            h = 2 * pair + half
                            last = nc.tensor.matmul(O[pair % 2][half * HD:(half + 1) * HD, 0:P],
                                                    v[:, m, h * HD:(h + 1) * HD],
                                                    probs_T[:, k % 2, half, b * P:(b + 1) * P],
                                                    start=(m == 0), stop=(m == TILES - 1))
                    last.then_inc(quarter_used, 1)

                def body(t, has_prev, has_cur, has_next):
                    for pair in range(PAIRS):
                        g = PAIRS * t + pair
                        turn_prev = (has_cur or pair == 0) and (has_prev or pair >= 1)
                        last_prev = (has_cur or pair <= 1) and (has_prev or pair >= 2)
                        for k in range(QUARTERS):
                            if has_cur:
                                scores(t, pair, 2 * k)
                                scores(t, pair, 2 * k + 1)
                            if turn_prev:
                                turn_probs((pair - 1) % PAIRS, g - 1, k)
                            if k == 0 and last_prev:
                                weigh_values((pair - 2) % PAIRS, g - 2, QUARTERS - 1)
                            if k >= 1 and turn_prev:
                                weigh_values((pair - 1) % PAIRS, g - 1, k - 1)
                            if k == 1 and turn_prev:
                                pe.wait_ge(inv_ready, g)
                                wait(pe, inv_copied, g - 1)
                                if pair == 2 and has_next:
                                    pe.wait_ge(relu_done, t + 2)
                                if pair == 2 and has_prev:
                                    wait(pe, x_added, t)
                                if pair == 3 and has_next:
                                    pe.wait_ge(q_split, t + 2)
                                nc.tensor.transpose(M[:, 0:P], inv_cols[:, :, :].rearrange("p a n -> p (a n)"),
                                                    ident["i"][:, :]).then_inc(inv_turned, 1)
                            if k == 3 and pair == 1 and has_prev:
                                pe.wait_ge(pair_normed, g - 1)
                                wait(pe, inv_copied, g if has_cur else g - 1)
                                for p in range(PAIRS):
                                    last = nc.tensor.matmul(M[:, 0:D], heads_T[:, p, :], w["o"][:, p, :],
                                                            start=(p == 0), stop=(p == PAIRS - 1))
                                last.then_inc(out_ready, 1)
                            if k == 0 and pair == 2 and has_next:
                                wait(pe, x_added, t)
                                pe.wait_ge(inv_copied, g - 1)
                                turn_x(t + 1)
                            if k == 3 and pair == 2 and has_next:
                                pe.wait_ge(inv_copied, g)
                                project_queries(t + 1)

                over_tiles(pe, body)


def graph_layers(nc, x, ident, eps, col_count, dram, out):
    with ExitStack() as ctx:
        def sb(name, shape, dt=F32):
            return ctx.enter_context(nc.sbuf_tensor(name, shape, dt))

        def sem(name):
            return ctx.enter_context(nc.semaphore(name))

        def ps(name):
            return ctx.enter_context(nc.psum_tensor(name, [P, BANK], F32))

        adj = sb("adj_in", [P, 2, N])
        adj_T = sb("adj_T", [P, TILES, N], U8)
        block_T = sb("block_T", [P, 2, N], F32R)
        parts = [sb(f"parts{i}", [P, TILES, 2, D], F32R) for i in range(2)]
        xc = sb("c_xc", [P, 2, D])
        hT = sb("c_hT", [P, 2, DC, P])
        y = sb("y", [P, 2, DX])
        yr = sb("yr", [P, D])
        stats = sb("c_stats", [P, 6])
        mv = sb("c_mv", [P, 2, 2])
        std = sb("c_std", [P, 2])
        rstd = sb("c_rstd", [P, 2])
        deg1 = sb("deg1", [P, TILES])
        w1 = sb("w1", [P, DC, D])
        w2 = sb("w2", [P, DC, D])
        w3 = sb("w3", [P, DC, DX])
        bias = sb("bias", [P, 3, DX])
        gat_k = sb("gat_k", [P, DC, GAT_HEADS, D])
        ones = sb("ones", [P, P])
        ident_r = sb("ident_r", [P, P], F32R)
        ones_b = sb("ones_b", [P, 1], BF16)
        in_deg_inv = sb("in_deg_inv", [P, TILES])
        r = sb("r", [P, TILES])
        row_sum = sb("row_sum", [P, TILES])
        adj_copy = sb("adj_copy", [P, N], U8)
        r_any = sb("r_any", [P, TILES])
        scores = sb("gat_scores", [P, TILES, GAT_HEADS])
        w_adj = sb("w_adj", [P, TILES, GAT_HEADS])
        w_all = sb("w_all", [P, TILES, GAT_HEADS])
        g_tmp = sb("g_tmp", [P, 4, TILES, GAT_HEADS])
        y_sum = sb("y_sum", [P, D])
        all_sum_T = sb("all_sum_T", [P, DC, P])
        all_k = sb("all_k", [P, GAT_HEADS, D])
        u = sb("u", [P, 2, D])
        acc = sb("acc", [P, 2, D])
        w2a = sb("w2a", [P, D])
        w2b = sb("w2b", [P, DC, P])
        w2b_T = sb("w2b_T", [P, D])
        wn_T = sb("wn_T", [P, DC, D])
        a_bc = sb("a_bc", [P, 2, GAT_HEADS, D])
        va = sb("va", [P, DC, GAT_HEADS])
        va_junk = sb("va_junk", [P, D])
        b_col = sb("b_col", [P, 1 + DC])
        b_bc = sb("b_bc", [P, 1 + DC, P])

        turn_ps = [ps("c_turn0"), ps("c_turn1")]
        sum_ps = [ps("sum0"), ps("sum1")]
        small_ps = ps("small")
        dense_ps = [ps("dense0"), ps("dense1")]
        z_ps = [[dense_ps[0], dense_ps[1]], [turn_ps[1], ps("z3")]]

        loaded = sem("weights_loaded")
        sp_passed = sem("c_sp_passed")
        dve_passed = sem("c_dve_passed")
        adj_in = [sem("adj_in0"), sem("adj_in1")]
        prep_pool = sem("prep_pool")
        prep_dve = sem("prep_dve")
        prep_pe = sem("prep_pe")
        prep_act = sem("prep_act")
        ln_step = sem("c_ln_step")
        stats_ready = sem("c_stats_ready")
        std_ready = sem("c_std_ready")
        rstd_ready = sem("c_rstd_ready")
        deg_ready = sem("deg_ready")
        deg_root = sem("deg_root")
        x_step = sem("x_step")
        centred = sem("c_centred")
        x_turned = sem("c_x_turned")
        h_ready = sem("h_ready")
        dense_ready = sem("dense_ready")
        y_step = sem("y_step")
        y_split = sem("y_split")
        y_summed = sem("y_summed")
        adj_turned = sem("adj_turned")
        adj_kept_even = sem("adj_kept_even")
        adj_kept_odd = sem("adj_kept_odd")
        rows_summed = sem("rows_summed")
        block_ready = sem("block_ready")
        sums_ready = sem("sums_ready")
        gat_step = sem("gat_step")
        gat_exp = sem("gat_exp")
        z_ready = sem("z_ready")
        z_step = sem("z_step")
        out_ready = sem("tile_out_ready")
        out_stored = [sem("out_stored0"), sem("out_stored1")]

        QB = BANK // P
        LOADS = 14
        VECTORS = 3 + 1 + DC * GAT_HEADS + 1 + DC
        YS = 3
        XS = 2

        def one(ap):
            return ap.rearrange("p a d -> p (a d)")

        def over_ticks(eng, tick, first=2, lead=0):
            def peeled(t):
                tick(t, t % 2, lambda lag: 0 <= t - lag < TILES)
            for t in range(first):
                peeled(t)
            with eng.Fori(first // 2, TILES // 2 - lead) as i:
                for s in range(2):
                    tick(2 * i + s, s, lambda lag: True)
            for t in range(TILES - 2 * lead, TILES + 2):
                peeled(t)

        with nc.Block() as block:

            @block.sync
            def _(sp):
                adj_rows = dram["adj"].rearrange("(t p) n -> t p n", p=P)

                def flat_bc(ap, n):
                    return ap.rearrange("(a n) -> a n", a=1).broadcast_to([P, n])

                def load_adj(t, s):
                    sp.dma_start(adj[:, s, :], adj_rows[ds(t, 1), :, :].rearrange("a p n -> (a p) n"))\
                        .then_inc(adj_in[s], 16)

                sp.dma_start(w1[:, :, :], dram["L1_gnn_W"].rearrange("(c p) o -> p c o", p=P)).then_inc(loaded, 16)
                sp.dma_start(bias[:, 0, 0:D], flat_bc(dram["L1_gnn_b"], D)).then_inc(loaded, 16)
                load_adj(0, 0)
                load_adj(1, 1)
                sp.dma_start(w2a[:, :], dram["L2_gnn_W1"]).then_inc(loaded, 16)
                sp.dma_start(w2b[:, :, :], dram["L2_gnn_W2"].rearrange("(c p) m -> p c m", p=P)).then_inc(loaded, 16)
                sp.dma_start(bias[:, 1, 0:D], flat_bc(dram["L2_gnn_b2"], D)).then_inc(loaded, 16)
                sp.dma_start(w3[:, :, 0:D], dram["L3_gnn_W_node"].rearrange("(c p) o -> p c o", p=P)).then_inc(loaded, 16)
                sp.dma_start(bias[:, 2, 0:D], flat_bc(dram["L3_gnn_b_node"], D)).then_inc(loaded, 16)
                for c in range(DC):
                    sp.dma_start(gat_k[:, c, :, :],
                                 dram["L3_gnn_K"][:, c * P:(c + 1) * P, :].rearrange("h p f -> p h f"))\
                        .then_inc(loaded, 16)
                for i, name in enumerate(("L3_gnn_A_self", "L3_gnn_A_neigh")):
                    sp.dma_start(a_bc[:, i, :, :].rearrange("p h f -> p (h f)"),
                                 flat_bc(dram[name].rearrange("h f -> (h f)"), GAT_HEADS * D)).then_inc(loaded, 16)
                sp.dma_start(b_col[:, 0:1], dram["L2_gnn_b1"].rearrange("(p a) -> p a", a=1)).then_inc(loaded, 16)
                for c in range(DC):
                    sp.dma_start(b_col[:, 1 + c:2 + c],
                                 dram["L3_gnn_b_node"][c * P:(c + 1) * P].rearrange("(p a) -> p a", a=1))\
                        .then_inc(loaded, 16)
                with sp.Fori(1, TILES // 2) as i:
                    for s in range(2):
                        t = 2 * i + s
                        wait_apart(sp, adj_turned, QUARTERS * (t - 1), sp_passed)
                        wait_apart(sp, rows_summed, t - 1, sp_passed)
                        load_adj(t, s)
                out_rows = out.rearrange("(t p) d -> t p d", p=P)

                def store(t, s):
                    wait_apart(sp, out_ready, t + 1, sp_passed)
                    sp.dma_start(out_rows[ds(t, 1), :, :].rearrange("a p d -> (a p) d"), acc[:, s, :])\
                        .then_inc(out_stored[s], 16)

                with sp.Fori(0, TILES // 2) as i:
                    for s in range(2):
                        store(2 * i + s, s)
                for s in range(2):
                    wait_apart(sp, out_stored[s], 16 * TILES // 2, sp_passed)

            @block.gpsimd
            def _(pool):
                nc.gpsimd.memset(ones[:, :], 1.0).then_inc(prep_pool, 1)
                nc.gpsimd.memset(ones_b[:, :], 1.0).then_inc(prep_pool, 1)
                nc.gpsimd.memset(y_sum[:, :], 0.0).then_inc(prep_pool, 1)
                pool.wait_ge(prep_pool, 3)

                def add_y(t, s):
                    pool.wait_ge(y_step, YS * (2 * TILES + t) + 1)
                    wait(pool, y_summed, t)
                    nc.gpsimd.tensor_tensor(y_sum[:, :], y[:, s, 0:D], y_sum[:, :], ALU.add)\
                        .then_inc(y_summed, 1)

                add_y(0, 0)
                add_y(1, 1)
                with pool.Fori(1, TILES // 2) as i:
                    for s in range(2):
                        add_y(2 * i + s, s)

            @block.vector
            def _(dve):
                def statistics(n, t, s):
                    nc.vector.bn_stats(stats[:, :], one(x[:, ds(t, 1), :])).then_inc(ln_step, 1)
                    wait_apart(dve, ln_step, n + 1, dve_passed)
                    nc.vector.bn_aggr(mv[:, s, :], stats[:, :]).then_inc(stats_ready, 1)

                def center(n, t, s):
                    own = one(x[:, ds(t, 1), :])
                    dve.wait_ge(std_ready, n + 1)
                    nc.vector.reciprocal(rstd[:, s:s + 1], std[:, s:s + 1]).then_inc(rstd_ready, 1)
                    dve.wait_ge(rstd_ready, n + 1)
                    wait(dve, x_turned, n - 1)
                    nc.vector.tensor_scalar(xc[:, s, :], own, mv[:, s, 0:1], rstd[:, s:s + 1],
                                            ALU.subtract, ALU.mult).then_inc(centred, 1)

                def finish_y(layer, t, s):
                    n = (layer - 1) * TILES + t
                    width = DX if layer == 3 else D
                    dve.wait_ge(dense_ready, n + 1)
                    if layer == 3:
                        wait(dve, y_summed, t - 1)
                    nc.vector.tensor_tensor(y[:, s, 0:width], dense_ps[s][:, 0:width], bias[:, layer - 1, 0:width],
                                            ALU.add).then_inc(y_step, 1)
                    dve.wait_ge(y_step, YS * n + 1)
                    if layer == 2:
                        nc.vector.tensor_scalar(yr[:, :], y[:, s, 0:D], r[:, ds(t, 1)], None, ALU.mult)\
                            .then_inc(y_step, 1)
                        full = yr[:, :]
                    elif layer == 3:
                        nc.vector.tensor_copy(one(scores[:, ds(t, 1), :]), y[:, s, D:DX]).then_inc(y_step, 1)
                        full = y[:, s, 0:D]
                    else:
                        dve.sem_inc(y_step, 1)
                        full = y[:, s, 0:D]
                    dve.wait_ge(y_step, YS * n + 2)
                    to = parts[layer % 2]
                    hi = to[:, ds(t, 1), 0, :].rearrange("p a d -> p (a d)")
                    lo = to[:, ds(t, 1), 1, :].rearrange("p a d -> p (a d)")
                    nc.vector.tensor_copy(hi, full).then_inc(y_step, 1)
                    dve.wait_ge(y_step, YS * n + 3)
                    nc.vector.tensor_tensor(lo, full, hi.bitcast(F32), ALU.subtract).then_inc(y_split, 1)

                nc.vector.tensor_copy(ident_r[:, :], ident["i"][:, :]).then_inc(prep_dve, 1)
                dve.wait_ge(loaded, 16 * LOADS)
                dve.wait_ge(prep_pe, 1)
                nc.vector.reciprocal(in_deg_inv[:, :], small_ps[:, 0:TILES]).then_inc(prep_dve, 1)

                def first_tick(t, s, live):
                    if live(0):
                        statistics(t, t, s)
                        for q in range(2):
                            n = QUARTERS * t + 2 * q + 1
                            dve.wait_ge(adj_turned, n + 1)
                            nc.vector.tensor_copy(adj_T[:, ds(t, 1), (2 * q + 1) * BANK:(2 * q + 2) * BANK]
                                                  .rearrange("p a n -> p (a n)"), sum_ps[1][:, :])\
                                .then_inc(adj_kept_odd, 1)
                    if live(2):
                        finish_y(1, t - 2, s)
                    if live(0):
                        center(t, t, s)

                over_ticks(dve, first_tick, first=4)

                dve.wait_ge(prep_pool, 3)
                dve.wait_ge(rows_summed, TILES)
                nc.vector.tensor_scalar(deg1[:, :], row_sum[:, :], 1.0, 1.0 / HUGE, ALU.add, ALU.max)\
                    .then_inc(deg_ready, 1)
                dve.wait_ge(deg_root, 1)
                nc.vector.reciprocal(deg1[:, :], r_any[:, :]).then_inc(deg_ready, 1)
                dve.wait_ge(deg_ready, 2)
                nc.vector.scalar_tensor_tensor(out=r[:, :], in0=row_sum[:, :], scalar=-1.0, in1=deg1[:, :],
                                               op0=ALU.is_gt, op1=ALU.mult).then_inc(prep_dve, 1)
                dve.wait_ge(prep_dve, 3)
                at = 3
                nc.vector.tensor_tensor(a_bc[:, 0, :, :], a_bc[:, 0, :, :], a_bc[:, 1, :, :], ALU.add)\
                    .then_inc(prep_dve, 1)
                dve.wait_ge(prep_dve, at + 1)
                for c in range(DC):
                    for h in range(GAT_HEADS):
                        nc.vector.tensor_tensor_reduce(va_junk[:, :], gat_k[:, c, h, :], a_bc[:, 0, h, :],
                                                       1.0, 0.0, ALU.mult, ALU.add, va[:, c, h:h + 1])\
                            .then_inc(prep_dve, 1)
                        dve.wait_ge(prep_dve, at + 2 + c * GAT_HEADS + h)
                for i in range(1 + DC):
                    nc.vector.tensor_scalar(b_bc[:, i, :], ones[:, :], b_col[:, i:i + 1], None, ALU.mult)\
                        .then_inc(prep_dve, 1)
                dve.wait_ge(prep_pe, 3)
                nc.vector.tensor_tensor(bias[:, 1, 0:D], small_ps[:, 0:D], bias[:, 1, 0:D], ALU.add)\
                    .then_inc(prep_dve, 1)
                dve.wait_ge(prep_pe, 6)
                nc.vector.tensor_copy(bias[:, 2, D:DX], small_ps[:, 0:GAT_HEADS]).then_inc(prep_dve, 1)
                dve.wait_ge(prep_dve, VECTORS + 2)

                def layer_tick(layer):
                    def tick(t, s, live):
                        n = (layer - 1) * TILES + t
                        if live(0):
                            scale = in_deg_inv if layer == 1 else r
                            own = one(x[:, ds(t, 1), :])
                            dve.wait_ge(sums_ready, n + 1)
                            nc.vector.scalar_tensor_tensor(out=own, in0=sum_ps[s][:, 0:D], scalar=scale[:, ds(t, 1)],
                                                           in1=own, op0=ALU.mult, op1=ALU.add).then_inc(x_step, 1)
                            dve.wait_ge(x_step, XS * n + 1)
                            nc.vector.scalar_tensor_tensor(out=own, in0=sum_ps[s][:, D:2 * D],
                                                           scalar=scale[:, ds(t, 1)],
                                                           in1=own, op0=ALU.mult, op1=ALU.add).then_inc(x_step, 1)
                            wait_apart(dve, x_step, XS * n + 2, dve_passed)
                            statistics(n + TILES, t, s)
                        if live(2):
                            finish_y(layer + 1, t - 2, s)
                        if live(0):
                            center(n + TILES, t, s)
                    return tick

                over_ticks(dve, layer_tick(1))
                over_ticks(dve, layer_tick(2), first=4)

                dve.wait_ge(y_split, 3 * TILES)
                step = [0]

                def link(ins):
                    step[0] += 1
                    ins.then_inc(gat_step, 1)
                    dve.wait_ge(gat_step, step[0])

                deg = row_sum[:, :].unsqueeze(2).to_broadcast([P, TILES, GAT_HEADS])
                lrelu, top, e_adj, e_all = (g_tmp[:, i, :, :] for i in range(4))
                link(nc.vector.scalar_tensor_tensor(out=lrelu, in0=scores[:, :, :], scalar=ALPHA,
                                                    in1=scores[:, :, :], op0=ALU.mult, op1=ALU.max))
                link(nc.vector.tensor_scalar(top, deg, 1.0, -NEG, ALU.min, ALU.mult))
                link(nc.vector.scalar_tensor_tensor(out=top, in0=top, scalar=NEG, in1=lrelu,
                                                    op0=ALU.add, op1=ALU.add))
                link(nc.vector.tensor_tensor(e_adj, lrelu, top, ALU.subtract))
                link(nc.vector.tensor_scalar(e_adj, e_adj, 0.0, None, ALU.min))
                link(nc.vector.scalar_tensor_tensor(out=e_all, in0=lrelu, scalar=NEG, in1=top,
                                                    op0=ALU.add, op1=ALU.subtract))
                dve.wait_ge(gat_exp, 2)
                link(nc.vector.tensor_scalar(lrelu, deg, -1.0, float(N), ALU.mult, ALU.add))
                link(nc.vector.tensor_tensor(lrelu, lrelu, e_all, ALU.mult))
                link(nc.vector.tensor_tensor(top, deg, e_adj, ALU.mult))
                link(nc.vector.tensor_tensor(top, top, lrelu, ALU.add))
                link(nc.vector.reciprocal(lrelu, top))
                link(nc.vector.tensor_scalar(lrelu, lrelu, 1.0 / GAT_HEADS, None, ALU.mult))
                link(nc.vector.tensor_tensor(e_adj, e_adj, e_all, ALU.subtract))
                link(nc.vector.tensor_tensor(w_adj[:, :, :], e_adj, lrelu, ALU.mult))
                link(nc.vector.tensor_tensor(w_all[:, :, :], e_all, lrelu, ALU.mult))

                def out_tick(t, s, live):
                    if live(0):
                        n = 2 * TILES + t
                        dve.wait_ge(sums_ready, n + 1)
                        wait(dve, x_turned, n + TILES - 1)
                        nc.vector.tensor_copy(u[:, s, :], sum_ps[s][:, 0:D]).then_inc(x_step, 1)
                        dve.wait_ge(x_step, XS * n + 1)
                        nc.vector.tensor_tensor(u[:, s, :], sum_ps[s][:, D:2 * D], u[:, s, :], ALU.add)\
                            .then_inc(x_step, 1)
                    if live(2):
                        o = t - 2
                        to = acc[:, s, :]
                        if isinstance(o, int):
                            wait(dve, out_stored[s], 16 * (o // 2))
                        else:
                            dve.wait_ge(out_stored[s], (o - s) * 8)
                        k = 0
                        for h in range(GAT_HEADS):
                            src = all_k[:, h, :]
                            wgt = w_all[:, ds(o, 1), h]
                            if h == 0:
                                nc.vector.tensor_scalar(to, src, wgt, None, ALU.mult).then_inc(z_step, 1)
                            else:
                                nc.vector.scalar_tensor_tensor(out=to, in0=src, scalar=wgt, in1=to,
                                                               op0=ALU.mult, op1=ALU.add).then_inc(z_step, 1)
                            k += 1
                            dve.wait_ge(z_step, 2 * GAT_HEADS * o + k)
                        dve.wait_ge(z_ready, o + 1)
                        for h in range(GAT_HEADS):
                            z = z_ps[s][h // 2][:, (h % 2) * D:(h % 2 + 1) * D]
                            nc.vector.scalar_tensor_tensor(out=to, in0=z, scalar=w_adj[:, ds(o, 1), h], in1=to,
                                                           op0=ALU.mult, op1=ALU.add).then_inc(z_step, 1)
                            k += 1
                            dve.wait_ge(z_step, 2 * GAT_HEADS * o + k)
                        nc.vector.scalar_tensor_tensor(out=to, in0=to, scalar=0.0, in1=one(x[:, ds(o, 1), :]),
                                                       op0=ALU.max, op1=ALU.add).then_inc(out_ready, 1)

                over_ticks(dve, out_tick, first=4)

            @block.scalar
            def _(act):
                def relu(n, s, func=ACT.Relu):
                    act.wait_ge(x_turned, n + 1)
                    if func == ACT.Relu:
                        wait(act, dense_ready, n - 1)
                    else:
                        act.wait_ge(dense_ready, 3 * TILES)
                        wait(act, z_ready, n - 1 - 3 * TILES)
                    nc.scalar.activation(hT[:, s, :, :], turn_ps[0][:, 0:D].rearrange("p (c n) -> p c n", c=DC),
                                         func).then_inc(h_ready, 1)

                def deviation(n, s):
                    act.wait_ge(stats_ready, n + 1)
                    nc.scalar.activation(std[:, s:s + 1], mv[:, s, 1:2], ACT.Sqrt, bias=eps[:, :])\
                        .then_inc(std_ready, 1)

                def widen(n, t, s):
                    wait(act, sums_ready, n - 1)
                    nc.scalar.activation(block_T[:, s, :], one(adj_T[:, ds(t, 1), :]), ACT.Copy)\
                        .then_inc(block_ready, 1)

                def first_tick(t, s, live):
                    if live(0):
                        for q in range(2):
                            n = QUARTERS * t + 2 * q
                            act.wait_ge(adj_turned, n + 1)
                            nc.scalar.activation(adj_T[:, ds(t, 1), 2 * q * BANK:(2 * q + 1) * BANK]
                                                 .rearrange("p a n -> p (a n)"), sum_ps[0][:, :], ACT.Copy)\
                                .then_inc(adj_kept_even, 1)
                        wait(act, rows_summed, t)
                        nc.scalar.activation(adj_copy[:, :], adj[:, s, :], ACT.Copy,
                                             accum_out=row_sum[:, ds(t, 1)]).then_inc(rows_summed, 1)
                    if live(1):
                        relu(t - 1, 1 - s)
                    if live(0):
                        deviation(t, s)

                over_ticks(act, first_tick, first=4)
                act.wait_ge(adj_kept_even, 2 * TILES)
                act.wait_ge(adj_kept_odd, 2 * TILES)

                act.wait_ge(deg_ready, 1)
                nc.scalar.activation(r_any[:, :], deg1[:, :], ACT.Sqrt).then_inc(deg_root, 1)

                act.wait_ge(prep_pe, 2)
                nc.scalar.activation(w2b_T[:, :], turn_ps[1][:, 0:D], ACT.Copy).then_inc(prep_act, 1)
                for d in range(DC):
                    act.wait_ge(prep_pe, 4 + d)
                    if d == 0:
                        nc.scalar.activation(w2[:, :, :].rearrange("p c o -> p (c o)"), dense_ps[0][:, :], ACT.Copy)\
                            .then_inc(prep_act, 1)
                    nc.scalar.activation(wn_T[:, d, :], sum_ps[d][:, 0:D], ACT.Copy).then_inc(prep_act, 1)
                act.wait_ge(prep_pe, 7)
                nc.scalar.activation(w3[:, :, D:DX], dense_ps[1][:, 0:DC * GAT_HEADS]
                                     .rearrange("p (c h) -> p c h", c=DC), ACT.Copy).then_inc(prep_act, 1)

                def layer_tick(layer):
                    def tick(t, s, live):
                        n = (layer - 1) * TILES + t
                        if live(-1):
                            widen(n + 1, t + 1, 1 - s)
                        if live(1):
                            relu(n - 1 + TILES, 1 - s, ACT.Relu if layer < 3 else ACT.Copy)
                        if live(0) and layer < 3:
                            deviation(n + TILES, s)
                    return tick

                def run_layer(layer):
                    widen((layer - 1) * TILES, 0, 0)
                    over_ticks(act, layer_tick(layer), lead=1)

                run_layer(1)
                run_layer(2)
                widen(2 * TILES, 0, 0)
                act.wait_ge(gat_step, 6)
                for i in (2, 3):
                    nc.scalar.activation(g_tmp[:, i, :, :], g_tmp[:, i, :, :], ACT.Exp).then_inc(gat_exp, 1)
                act.wait_ge(prep_pe, 8)
                nc.scalar.activation(all_sum_T[:, :, :], small_ps[:, 0:D].rearrange("p (c n) -> p c n", c=DC),
                                     ACT.Copy).then_inc(prep_act, 1)
                act.wait_ge(prep_pe, 9)
                for i in range(2):
                    nc.scalar.activation(all_k[:, 2 * i:2 * i + 2, :].rearrange("p h f -> p (h f)"),
                                         dense_ps[i][:, :], ACT.Copy).then_inc(prep_act, 1)
                over_ticks(act, layer_tick(3), first=4, lead=1)

            @block.tensor
            def _(pe):
                def turn(n, s, src):
                    pe.wait_ge(centred, n + 1) if src is xc else pe.wait_ge(x_step, XS * (n - TILES) + 2)
                    wait(pe, h_ready, n)
                    for d in range(DC):
                        last = nc.tensor.transpose(turn_ps[0][:, d * P:(d + 1) * P],
                                                   src[:, s, d * P:(d + 1) * P], ident["i"][:, :])
                    last.then_inc(x_turned, 1)

                def dense(layer, n, s):
                    pe.wait_ge(h_ready, n + 1)
                    wait(pe, y_step, YS * (n - 2) + 1)
                    weights, width = ((w1, D), (w2, D), (w3, DX))[layer - 1]
                    for d in range(DC):
                        last = nc.tensor.matmul(dense_ps[s][:, 0:width], hT[:, s, d, :], weights[:, d, :],
                                                start=(d == 0), stop=(d == DC - 1))
                    last.then_inc(dense_ready, 1)

                def sums(layer, n, t, s):
                    pe.wait_ge(block_ready, n + 1)
                    wait(pe, x_step, XS * (n - 1))
                    src = parts[layer % 2]
                    if layer == 2:
                        nc.tensor.matmul(sum_ps[s][:, :], ident_r[:, :], src[:, ds(t, 1), :, :],
                                         start=True, stop=False)
                    for j in range(TILES):
                        last = nc.tensor.matmul(sum_ps[s][:, :], block_T[:, s, j * P:(j + 1) * P],
                                                src[:, j, :, :], start=(j == 0 and layer != 2),
                                                stop=(j == TILES - 1))
                    last.then_inc(sums_ready, 1)

                pe.wait_ge(prep_pool, 3)
                for t in range(TILES):
                    last = nc.tensor.matmul(small_ps[:, t:t + 1], col_count[:, t * P:(t + 1) * P], ones_b[:, :],
                                            start=True, stop=True)
                last.then_inc(prep_pe, 1)
                pe.wait_ge(loaded, 16 * LOADS)

                def first_tick(t, s, live):
                    if live(0):
                        pe.wait_ge(adj_in[s], (t - s) * 8 + 16)
                        for q in range(QUARTERS):
                            if q % 2 == 0:
                                wait(pe, adj_kept_even, 2 * t + q // 2)
                            else:
                                wait(pe, adj_kept_odd, 2 * t + q // 2)
                            for b in range(QB):
                                m = q * QB + b
                                last = nc.tensor.transpose(sum_ps[q % 2][:, b * P:(b + 1) * P],
                                                           adj[:, s, m * P:(m + 1) * P], ident["i"][:, :])
                            last.then_inc(adj_turned, 1)
                    if live(1):
                        turn(t - 1, 1 - s, xc)
                    if live(2):
                        dense(1, t - 2, s)

                over_ticks(pe, first_tick, first=4)

                pe.wait_ge(prep_dve, VECTORS)
                pe.wait_ge(adj_kept_even, 2 * TILES)
                pe.wait_ge(adj_kept_odd, 2 * TILES)
                pe.wait_ge(y_split, TILES)
                for c in range(DC):
                    last = nc.tensor.transpose(turn_ps[1][:, c * P:(c + 1) * P], w2b[:, c, :], ident["i"][:, :])
                last.then_inc(prep_pe, 1)
                pe.wait_ge(prep_act, 1)
                nc.tensor.matmul(small_ps[:, 0:D], b_bc[:, 0, :], w2b_T[:, :], start=True, stop=True)\
                    .then_inc(prep_pe, 1)
                for c in range(DC):
                    nc.tensor.matmul(dense_ps[0][:, c * D:(c + 1) * D], w2a[:, c * P:(c + 1) * P], w2b_T[:, :],
                                     start=True, stop=True)
                for d in range(DC):
                    for c in range(DC):
                        last = nc.tensor.transpose(sum_ps[d][:, c * P:(c + 1) * P],
                                                   w3[:, c, d * P:(d + 1) * P], ident["i"][:, :])
                    last.then_inc(prep_pe, 1)
                pe.wait_ge(prep_dve, VECTORS + 1)
                for d in range(DC):
                    last = nc.tensor.matmul(small_ps[:, 0:GAT_HEADS], b_bc[:, 1 + d, :], va[:, d, :],
                                            start=(d == 0), stop=(d == DC - 1))
                last.then_inc(prep_pe, 1)
                pe.wait_ge(prep_act, 4)
                for c in range(DC):
                    for d in range(DC):
                        last = nc.tensor.matmul(dense_ps[1][:, c * GAT_HEADS:(c + 1) * GAT_HEADS],
                                                wn_T[:, d, c * P:(c + 1) * P], va[:, d, :],
                                                start=(d == 0), stop=(d == DC - 1))
                last.then_inc(prep_pe, 1)
                pe.wait_ge(prep_act, 5)
                pe.wait_ge(prep_dve, VECTORS + 2)

                def layer_tick(layer):
                    def tick(t, s, live):
                        n = (layer - 1) * TILES + t
                        if live(0):
                            sums(layer, n, t, s)
                        if live(1):
                            turn(n - 1 + TILES, 1 - s, xc)
                        if live(2):
                            dense(layer + 1, n - 2 + TILES, s)
                    return tick

                for layer in (1, 2):
                    pe.wait_ge(y_split, layer * TILES)
                    over_ticks(pe, layer_tick(layer))
                pe.wait_ge(y_split, 3 * TILES)
                pe.wait_ge(y_summed, TILES)
                for c in range(DC):
                    last = nc.tensor.matmul(small_ps[:, c * P:(c + 1) * P], y_sum[:, c * P:(c + 1) * P], ones[:, :],
                                            start=True, stop=True)
                last.then_inc(prep_pe, 1)
                pe.wait_ge(prep_act, 6)
                pe.wait_ge(y_step, YS * 3 * TILES)
                for i in range(2):
                    for c in range(DC):
                        last = nc.tensor.matmul(dense_ps[i][:, :], all_sum_T[:, c, :],
                                                gat_k[:, c, 2 * i:2 * i + 2, :],
                                                start=(c == 0), stop=(c == DC - 1))
                last.then_inc(prep_pe, 1)
                pe.wait_ge(prep_act, 8)

                def out_tick(t, s, live):
                    n = 2 * TILES + t
                    if live(0):
                        sums(3, n, t, s)
                    if live(1):
                        turn(n - 1 + TILES, 1 - s, u)
                    if live(2):
                        o = t - 2
                        pe.wait_ge(h_ready, n - 2 + TILES + 1)
                        wait(pe, z_step, 2 * GAT_HEADS * (o - 1))
                        for i in range(2):
                            for c in range(DC):
                                last = nc.tensor.matmul(z_ps[s][i][:, :], hT[:, s, c, :],
                                                        gat_k[:, c, 2 * i:2 * i + 2, :],
                                                        start=(c == 0), stop=(c == DC - 1))
                        last.then_inc(z_ready, 1)

                over_ticks(pe, out_tick, first=4)


def build(nc, dram, out):
    with ExitStack() as ctx:
        def sb(name, shape, dt=F32):
            return ctx.enter_context(nc.sbuf_tensor(name, shape, dt))

        x = sb("x", [P, TILES, D])
        ident = {name: sb("ident_" + name, [P, P]) for name in ("i", "not", "bias")}
        eps = sb("eps", [P, 1])
        col_count = sb("col_count", [P, N], BF16)
        with ExitStack() as heads:
            k_stack = heads.enter_context(nc.sbuf_tensor("k_stack", [P, HEADS, N], F32R))
            v = heads.enter_context(nc.sbuf_tensor("v", [P, TILES, HEADS * HD], F32))
            w = {"q": heads.enter_context(nc.sbuf_tensor("wq", [P, DC, HEADS * HD], F32)),
                 "o": heads.enter_context(nc.sbuf_tensor("wo", [P, PAIRS, D], F32))}
            mv = heads.enter_context(nc.sbuf_tensor("mean_var", [P, TILES, 2], F32))
            rstd = heads.enter_context(nc.sbuf_tensor("rstd", [P, TILES], F32))
            project_keys_values(nc, x, k_stack, v, w, ident, eps, mv, rstd, dram)
            attend(nc, x, k_stack, v, w, ident, mv, rstd, col_count, dram)
        graph_layers(nc, x, ident, eps, col_count, dram, out)


_INS = ["x", "adj", "L0_gnn_Wks", "L0_gnn_Wqs", "L0_gnn_Wvs", "L0_gnn_Wo", "L1_gnn_W", "L1_gnn_b",
        "L2_gnn_W1", "L2_gnn_b1", "L2_gnn_W2", "L2_gnn_b2", "L3_gnn_W_node", "L3_gnn_b_node",
        "L3_gnn_K", "L3_gnn_A_self", "L3_gnn_A_neigh"]


def kernel(**inputs):
    import numpy as _np
    import concourse.bacc as _bacc
    from concourse import mybir as _mybir
    from concourse.bass_utils import run_bass_kernel_spmd as _run

    nc = _bacc.Bacc("TRN2", target_bir_lowering=False, num_devices=1)
    arrays, dram = {}, {}
    for name in _INS:
        a = _np.ascontiguousarray(inputs[name])
        arrays[f"in_{name}_dram"] = a
        dram[name] = nc.dram_tensor(f"in_{name}_dram", a.shape, _mybir.dt.from_np(a.dtype),
                                    kind="ExternalInput").ap()
    out = nc.dram_tensor("out_dram", (N, D), _mybir.dt.float32, kind="ExternalOutput").ap()
    build(nc, dram, out)
    r = _run(nc, [arrays], core_ids=[0])
    return r.results[0]["out_dram"]
```

```python
from contextlib import ExitStack

import concourse.bass as bass
from concourse import mybir

F32 = mybir.dt.float32
F32R = mybir.dt.float32r
BF16 = mybir.dt.bfloat16
U8 = mybir.dt.uint8
ALU = mybir.AluOpType
ACT = mybir.ActivationFunctionType
AX = mybir.AxisListType

P = 128
N = 2048
D = 256
HEADS = 8
HD = 64
PAIRS = HEADS // 2
TILES = N // P
DC = D // P
BANK = 512
QUARTERS = N // BANK
CHUNKS = HEADS * QUARTERS
GAT_HEADS = 4
DX = D + GAT_HEADS
EPS = 1e-5
SCORE_SCALE = float(HD) ** -0.5
IDENTITY_BIAS = 0.01
MASK_VAL = 1e16
NEG = -1e10
ALPHA = 0.3
HUGE = 3.0e38


def ds(i, size):
    return bass.ds(i * size, size)


def wait(eng, sem, value):
    if isinstance(value, int) and value <= 0:
        return
    eng.wait_ge(sem, value)


def wait_apart(eng, sem, value, passed):
    wait(eng, sem, value)
    if not isinstance(value, int):
        eng.sem_inc(passed, 1)


def stack_queries(eng, q_hi, q_lo, q_stack, p, stacked):
    for half in range(2):
        src = slice(half * HD, (half + 1) * HD)
        for part, (low, high) in enumerate(((q_hi, q_lo), (q_lo, q_hi))):
            eng.dma_start(q_stack[0:HD, 2 * p + half, part, :].bitcast(F32), low[src, p, :].bitcast(F32))\
                .then_inc(stacked, 16)
            eng.dma_start(q_stack[HD:P, 2 * p + half, part, :].bitcast(F32), high[src, p, :].bitcast(F32))\
                .then_inc(stacked, 16)


def project_keys_values(nc, x, adj, q_hi, q_lo, q_stack, k_stack, v, w, ident, eps, mv, rstd, row_sum,
                        col_count, dram):
    with ExitStack() as ctx:
        def sb(name, shape, dt=F32):
            return ctx.enter_context(nc.sbuf_tensor(name, shape, dt))

        def sem(name):
            return ctx.enter_context(nc.semaphore(name))

        wk = sb("wk", [P, DC, HEADS * HD])
        wv = sb("wv", [P, DC, HEADS * HD])
        adj_copy = sb("a_adj_copy", [P, N], U8)
        stats = sb("a_stats", [P, TILES, 6])
        std = sb("a_std", [P, TILES])
        xc = sb("a_xc", [P, 2, D])
        hT = sb("a_hT", [P, 2, DC, BANK])
        turn_ps = [ctx.enter_context(nc.psum_tensor(f"a_turn{i}", [P, BANK], F32)) for i in range(2)]
        v_ps = [ctx.enter_context(nc.psum_tensor(f"a_v{i}", [P, BANK], F32)) for i in range(2)]
        k_ps = [ctx.enter_context(nc.psum_tensor(f"a_k{i}", [P, BANK], F32)) for i in range(PAIRS)]

        x_loaded = [sem(f"x_loaded{c}") for c in range(QUARTERS)]
        kv_weights = sem("kv_weights")
        const_loaded = sem("const_loaded")
        ident_cleared = sem("ident_cleared")
        ident_ready = sem("ident_ready")
        ln_step = sem("a_ln_step")
        stats_ready = sem("a_stats_ready")
        std_ready = sem("a_std_ready")
        rstd_ready = sem("a_rstd_ready")
        centred = sem("a_centred")
        turned = sem("a_turned")
        relu_done = sem("a_relu_done")
        v_ready = sem("v_ready")
        v_copied = sem("v_copied")
        k_ready = sem("k_ready")
        k_high = sem("k_high")
        k_split = sem("k_split")
        q0_ready = sem("q0_ready")
        q0_high = sem("q0_high")
        q0_split = sem("q0_split")
        q0_stacked = sem("q0_stacked")
        adj0_loaded = sem("adj0_loaded")
        count_cleared = sem("count_cleared")
        counted = sem("tile0_counted")
        rows_summed = sem("tile0_summed")
        mask_step = sem("a_mask_step")
        TPC = TILES // QUARTERS

        with nc.Block() as block:

            @block.sync
            def _(sp):
                x_view = dram["x"].rearrange("(t p) d -> p t d", p=P)
                for c in range(QUARTERS):
                    sp.dma_start(x[:, c * TPC:(c + 1) * TPC, :], x_view[:, c * TPC:(c + 1) * TPC, :])\
                        .then_inc(x_loaded[c], 16)
                    if c == 0:
                        for dst, name in ((wv, "L0_gnn_Wvs"), (wk, "L0_gnn_Wks")):
                            for d in range(DC):
                                sp.dma_start(dst[:, d, :].rearrange("p (h k) -> p h k", h=HEADS),
                                             dram[name][:, d * P:(d + 1) * P, :].rearrange("h p k -> p h k"))\
                                    .then_inc(kv_weights, 16)
                for d in range(DC):
                    sp.dma_start(w["q"][:, d, :].rearrange("p (h k) -> p h k", h=HEADS),
                                 dram["L0_gnn_Wqs"][:, d * P:(d + 1) * P, :].rearrange("h p k -> p h k"))\
                        .then_inc(const_loaded, 16)
                sp.dma_start(w["o"][:, :, :], dram["L0_gnn_Wo"].rearrange("(r a) k o -> (a k) r o", a=2))\
                    .then_inc(const_loaded, 16)
                sp.dma_start(adj[:, 0, :], dram["adj"][0:P, :]).then_inc(adj0_loaded, 16)
                sp.wait_ge(q0_split, 1)
                for p in range(PAIRS):
                    stack_queries(sp, q_hi, q_lo, q_stack, p, q0_stacked)
                sp.wait_ge(q0_stacked, 128 * PAIRS)

            @block.gpsimd
            def _(pool):
                nc.gpsimd.memset(ident["i"][:, :], 0.0).then_inc(ident_cleared, 1)
                nc.gpsimd.memset(ident["not"][:, :], 1.0).then_inc(ident_cleared, 1)
                nc.gpsimd.memset(ident["bias"][:, :], 0.0).then_inc(ident_cleared, 1)
                nc.gpsimd.memset(eps[:, :], EPS).then_inc(ident_cleared, 1)
                pool.wait_ge(ident_cleared, 4)
                for name, fill in (("i", 1.0), ("not", 0.0), ("bias", -IDENTITY_BIAS)):
                    nc.gpsimd.affine_select(out=ident[name][:, :], in_=ident[name][:, :],
                                            compare_op=ALU.not_equal, fill=fill, base=0,
                                            pattern=[[-1, P]], channel_multiplier=1)\
                        .then_inc(ident_ready, 1)
                pool.wait_ge(ident_ready, 3)
                nc.gpsimd.memset(col_count[:, :], 0.0).then_inc(count_cleared, 1)
                pool.wait_ge(count_cleared, 1)
                pool.wait_ge(adj0_loaded, 16)
                nc.gpsimd.tensor_tensor(col_count[:, :], adj[:, 0, :], col_count[:, :], ALU.add)\
                    .then_inc(counted, 1)
                pool.wait_ge(counted, 1)

            @block.vector
            def _(dve):
                def layer_norm(t):
                    dve.wait_ge(std_ready, t + 1)
                    nc.vector.reciprocal(rstd[:, t:t + 1], std[:, t:t + 1]).then_inc(rstd_ready, 1)
                    dve.wait_ge(rstd_ready, t + 1)
                    wait(dve, turned, t - 1)
                    nc.vector.tensor_scalar(xc[:, t % 2, :], x[:, t, :], mv[:, t, 0:1], rstd[:, t:t + 1],
                                            ALU.subtract, ALU.mult).then_inc(centred, 1)

                def statistics(t):
                    if t % TPC == 0:
                        dve.wait_ge(x_loaded[t // TPC], 16)
                    nc.vector.bn_stats(stats[:, t, :], x[:, t, :]).then_inc(ln_step, 1)
                    dve.wait_ge(ln_step, t + 1)
                    nc.vector.bn_aggr(mv[:, t, :], stats[:, t, :]).then_inc(stats_ready, 1)

                def split_keys(n):
                    c, p = divmod(n, PAIRS)
                    cols = slice(c * BANK, (c + 1) * BANK)
                    for half in range(2):
                        own = slice(half * HD, (half + 1) * HD)
                        other = slice((1 - half) * HD, (2 - half) * HD)
                        dve.wait_ge(k_high, 2 * n + half + 1)
                        nc.vector.tensor_tensor(k_stack[other, 2 * p + half, cols], k_ps[p][own, :],
                                                k_stack[own, 2 * p + half, cols].bitcast(F32), ALU.subtract)\
                            .then_inc(k_split, 1)

                statistics(0)
                statistics(1)
                for t in range(TPC + 1):
                    statistics(t + 2)
                    layer_norm(t)
                for n in range(TILES):
                    if n + TPC + 3 < TILES:
                        statistics(n + TPC + 3)
                    if n + TPC + 1 < TILES:
                        layer_norm(n + TPC + 1)
                    split_keys(n)
                    if n == PAIRS - 1:
                        dve.wait_ge(q0_high, 1)
                        nc.vector.scalar_tensor_tensor(
                            out=q_lo[:, :, :], in0=v_ps[1][:, :].rearrange("p (a n) -> p a n", a=PAIRS),
                            scalar=-SCORE_SCALE, in1=q_hi[:, :, :].bitcast(F32),
                            op0=ALU.mult, op1=ALU.subtract).then_inc(q0_split, 1)
                dve.wait_ge(counted, 1)
                dve.wait_ge(rows_summed, 1)
                build_mask(nc, dve, adj[:, 0, :], adj[:, 0, 0:P], ident, mask_step, 0)
                dve.wait_ge(k_split, 2 * TILES)

            @block.scalar
            def _(act):
                def relu(t):
                    act.wait_ge(turned, t + 1)
                    c = t // TPC
                    wait(act, k_ready, PAIRS * (c - 1))
                    nc.scalar.activation(hT[:, c % 2, :, (t % TPC) * P:(t % TPC + 1) * P],
                                         turn_ps[t % 2][:, 0:D].rearrange("p (c n) -> p c n", c=DC),
                                         ACT.Relu).then_inc(relu_done, 1)

                def deviation(t):
                    act.wait_ge(stats_ready, t + 1)
                    nc.scalar.activation(std[:, t:t + 1], mv[:, t, 1:2], ACT.Sqrt, bias=eps[:, :])\
                        .then_inc(std_ready, 1)

                def copy_out(n):
                    act.wait_ge(v_ready, n + 1)
                    nc.scalar.activation(v[:, n, :], v_ps[n % 2][:, :], ACT.Copy).then_inc(v_copied, 1)
                    c, p = divmod(n, PAIRS)
                    act.wait_ge(k_ready, n + 1)
                    for half in range(2):
                        own = slice(half * HD, (half + 1) * HD)
                        nc.scalar.activation(k_stack[own, 2 * p + half, c * BANK:(c + 1) * BANK], k_ps[p][own, :],
                                             ACT.Copy).then_inc(k_high, 1)

                act.wait_ge(ident_cleared, 4)
                deviation(0)
                deviation(1)
                for t in range(TPC):
                    deviation(t + 2)
                    relu(t)
                deviation(TPC + 2)
                for n in range(TILES):
                    if n + TPC + 3 < TILES:
                        deviation(n + TPC + 3)
                    if n + TPC < TILES:
                        relu(n + TPC)
                    copy_out(n)
                    if n == PAIRS - 1:
                        act.wait_ge(q0_ready, 1)
                        nc.scalar.activation(q_hi[:, :, :], v_ps[1][:, :].rearrange("p (a n) -> p a n", a=PAIRS),
                                             ACT.Copy, scale=-SCORE_SCALE).then_inc(q0_high, 1)
                    if n == 2 * PAIRS:
                        act.wait_ge(adj0_loaded, 16)
                        nc.scalar.activation(adj_copy[:, :], adj[:, 0, :], ACT.Copy, accum_out=row_sum[:, 0:1])\
                            .then_inc(rows_summed, 1)
                act.wait_ge(v_copied, TILES)

            @block.tensor
            def _(pe):
                def turn(t):
                    pe.wait_ge(centred, t + 1)
                    wait(pe, relu_done, t - 1)
                    for d in range(DC):
                        last = nc.tensor.transpose(turn_ps[t % 2][:, d * P:(d + 1) * P],
                                                   xc[:, t % 2, d * P:(d + 1) * P], ident["i"][:, :])
                    last.then_inc(turned, 1)

                pe.wait_ge(ident_ready, 3)
                for t in range(TPC):
                    turn(t)
                pe.wait_ge(kv_weights, 16 * 2 * DC)
                for n in range(TILES):
                    c, p = divmod(n, PAIRS)
                    if n + TPC < TILES:
                        turn(n + TPC)
                    pe.wait_ge(relu_done, n + 1)
                    wait(pe, v_copied, n - 1)
                    if n == PAIRS + 1:
                        pe.wait_ge(q0_split, 1)
                    for d in range(DC):
                        last = nc.tensor.matmul(v_ps[n % 2][:, :], hT[:, c % 2, d, p * P:(p + 1) * P],
                                                wv[:, d, :], start=(d == 0), stop=(d == DC - 1))
                    last.then_inc(v_ready, 1)
                    pe.wait_ge(relu_done, (c + 1) * TPC)
                    wait(pe, k_split, 2 * (n - PAIRS + 1))
                    for d in range(DC):
                        last = nc.tensor.matmul(k_ps[p][:, :], wk[:, d, p * P:(p + 1) * P],
                                                hT[:, c % 2, d, :], start=(d == 0), stop=(d == DC - 1))
                    last.then_inc(k_ready, 1)
                    if n == PAIRS - 1:
                        pe.wait_ge(const_loaded, 16 * (DC + 1))
                        pe.wait_ge(v_copied, PAIRS)
                        for a in range(PAIRS):
                            for d in range(DC):
                                last = nc.tensor.matmul(v_ps[1][:, a * P:(a + 1) * P],
                                                        w["q"][:, d, a * P:(a + 1) * P], hT[:, 0, d, 0:P],
                                                        start=(d == 0), stop=(d == DC - 1))
                        last.then_inc(q0_ready, 1)


def build_mask(nc, dve, adj, own, ident, mask_step, done):
    nc.vector.tensor_scalar(adj, adj, -MASK_VAL, MASK_VAL, ALU.mult, ALU.add).then_inc(mask_step, 1)
    dve.wait_ge(mask_step, done + 1)
    nc.vector.tensor_tensor(own, own, ident["not"][:, :], ALU.mult).then_inc(mask_step, 1)
    dve.wait_ge(mask_step, done + 2)
    nc.vector.tensor_tensor(own, own, ident["bias"][:, :], ALU.add).then_inc(mask_step, 1)
    dve.wait_ge(mask_step, done + 3)


def attend(nc, x, mask, q_hi, q_lo, q_stack, k_stack, v, w, ident, mv, rstd, row_sum, col_count, dram):
    with ExitStack() as ctx:
        def sb(name, shape, dt=F32):
            return ctx.enter_context(nc.sbuf_tensor(name, shape, dt))

        def sem(name):
            return ctx.enter_context(nc.semaphore(name))

        def ps(name):
            return ctx.enter_context(nc.psum_tensor(name, [P, BANK], F32))

        probs = sb("probs", [P, 4, N])
        probs_T = sb("probs_T", [P, 2, 2, BANK])
        xc = sb("b_xc", [P, D])
        hT = sb("b_hT", [P, DC, P])
        chunk_min = sb("chunk_min", [P, 2, QUARTERS])
        head_min = sb("head_min", [P, HEADS])
        adj_copy = sb("adj_copy", [P, N], U8)
        prob_sum = sb("prob_sum", [P, HEADS])
        inv_sum = sb("inv_sum", [P, 2])
        inv_cols = sb("inv_cols", [P, 2, HD])
        inv_rows = sb("inv_rows", [P, 2, P])
        heads_T = sb("heads_T", [P, PAIRS, P])
        S = [ps(f"scores{i}") for i in range(3)]
        T = [ps(f"turn{i}") for i in range(2)]
        O = [ps(f"heads{i}") for i in range(2)]
        M = ps("misc")

        adj_loaded = sem("adj_loaded")
        sp_passed = sem("b_sp_passed")
        dve_passed = sem("b_dve_passed")
        mask_step = sem("mask_step")
        counted = sem("counted")
        rows_summed = sem("rows_summed")
        centred = sem("b_centred")
        x_turned = sem("b_x_turned")
        relu_done = sem("b_relu_done")
        q_ready = sem("q_ready")
        q_high = sem("q_high")
        q_split = sem("q_split")
        q_stacked = [sem(f"q_stacked{p}") for p in range(PAIRS)]
        scores_ready = sem("scores_ready")
        scores_read = sem("scores_read")
        head_masked = sem("head_masked")
        probs_ready = sem("probs_ready")
        turned = [sem("even_turned"), sem("odd_turned")]
        copied = [sem("even_copied"), sem("odd_copied")]
        quarter_used = sem("quarter_used")
        inv_known = sem("inv_known")
        inv_ready = sem("inv_ready")
        inv_turned = sem("inv_turned")
        inv_copied = sem("inv_copied")
        pair_normed = sem("pair_normed")
        out_ready = sem("out_ready")
        x_added = sem("x_added")

        def chunk_bank(j):
            return S[j % 3]

        def over_tiles(eng, body):
            body(0, 0, False, True, True)
            with eng.Fori(0, TILES // 2 - 1) as i:
                for s in (1, 0):
                    body(2 * i + (2 - s), s, True, True, True)
            body(TILES - 1, 1, True, True, False)
            body(TILES, 0, True, False, False)

        with nc.Block() as block:

            @block.sync
            def _(sp):
                adj_rows = dram["adj"].rearrange("(t p) n -> t p n", p=P)

                def body(t, s, has_prev, has_cur, has_next):
                    if has_next:
                        wait_apart(sp, scores_read, CHUNKS * t, sp_passed)
                        sp.dma_start(mask[:, 1 - s, :], adj_rows[ds(t + 1, 1), :, :].rearrange("a p n -> (a p) n"))\
                            .then_inc(adj_loaded, 16)
                        for p in range(PAIRS):
                            wait_apart(sp, q_split, t + 1, sp_passed)
                            wait_apart(sp, scores_ready, CHUNKS * t + 2 * QUARTERS * (p + 1), sp_passed)
                            stack_queries(sp, q_hi, q_lo, q_stack, p, q_stacked[p])

                over_tiles(sp, body)

            @block.gpsimd
            def _(pool):
                def body(t, s, has_prev, has_cur, has_next):
                    if has_next:
                        pool.wait_ge(adj_loaded, 16 * (t + 1))
                        wait(pool, counted, t)
                        nc.gpsimd.tensor_tensor(col_count[:, :], mask[:, 1 - s, :], col_count[:, :], ALU.add)\
                            .then_inc(counted, 1)

                over_tiles(pool, body)
                pool.wait_ge(counted, TILES - 1)

            @block.vector
            def _(dve):
                def layer_norm(n):
                    own = x[:, ds(n, 1), :].rearrange("p a d -> p (a d)")
                    wait(dve, x_turned, n - 1)
                    nc.vector.tensor_scalar(xc[:, :], own, mv[:, ds(n, 1), 0], rstd[:, ds(n, 1)],
                                            ALU.subtract, ALU.mult).then_inc(centred, 1)

                def split_queries(n):
                    dve.wait_ge(q_high, n)
                    nc.vector.scalar_tensor_tensor(
                        out=q_lo[:, :, :], in0=M[:, :].rearrange("p (a n) -> p a n", a=PAIRS),
                        scalar=-SCORE_SCALE, in1=q_hi[:, :, :].bitcast(F32),
                        op0=ALU.mult, op1=ALU.subtract).then_inc(q_split, 1)

                def mask_scores(t, s, pair, j):
                    half, c = divmod(j, QUARTERS)
                    h = 2 * pair + half
                    i = h * QUARTERS + c
                    wait_apart(dve, scores_ready, CHUNKS * t + i + 1, dve_passed)
                    if c == 0:
                        wait_apart(dve, turned[half], QUARTERS * PAIRS * t + QUARTERS * (pair - 1), dve_passed)
                    nc.vector.tensor_tensor_reduce(
                        probs[:, h % 4, c * BANK:(c + 1) * BANK], chunk_bank(i)[:, :],
                        mask[:, s, c * BANK:(c + 1) * BANK], 1.0, HUGE, ALU.add, ALU.min,
                        chunk_min[:, half, c:c + 1]).then_inc(scores_read, 1)
                    if c == QUARTERS - 1:
                        dve.wait_ge(scores_read, CHUNKS * t + i + 1)
                        nc.vector.tensor_reduce(head_min[:, h:h + 1], chunk_min[:, half, :], AX.X, ALU.min)\
                            .then_inc(head_masked, 1)

                def body(t, s, has_prev, has_cur, has_next):
                    for pair in range(PAIRS):
                        g = PAIRS * t + pair
                        for k in range(QUARTERS):
                            if has_cur:
                                mask_scores(t, s, pair, 2 * k)
                                mask_scores(t, s, pair, 2 * k + 1)
                            turn_prev = (has_cur or pair == 0) and (has_prev or pair >= 1)
                            if turn_prev:
                                q = QUARTERS * (g - 1) + k
                                dve.wait_ge(turned[1], q + 1)
                                wait(dve, quarter_used, q - 1)
                                nc.vector.tensor_copy(probs_T[:, k % 2, 1, :], T[1][:, :])\
                                    .then_inc(copied[1], 1)
                            if turn_prev and k == 0:
                                prev = (pair - 1) % PAIRS
                                dve.wait_ge(probs_ready, 2 * g)
                                wait(dve, inv_turned, g - 1)
                                nc.vector.reciprocal(inv_sum[:, :], prob_sum[:, 2 * prev:2 * prev + 2])\
                                    .then_inc(inv_known, 1)
                                dve.wait_ge(inv_known, g)
                                nc.vector.tensor_copy(inv_cols[:, :, :],
                                                      inv_sum[:, :].unsqueeze(2).to_broadcast([P, 2, HD]))\
                                    .then_inc(inv_ready, 1)
                            norm_prev = (has_cur or pair <= 1) and (has_prev or pair >= 2)
                            if norm_prev and k == 1:
                                prev = (pair - 2) % PAIRS
                                dve.wait_ge(quarter_used, QUARTERS * (g - 1))
                                dve.wait_ge(inv_copied, g - 1)
                                nc.vector.tensor_tensor(heads_T[:, prev, :], O[pair % 2][:, 0:P],
                                                        inv_rows[:, pair % 2, :], ALU.mult)\
                                    .then_inc(pair_normed, 1)
                            if has_next and pair == 1 and k == 2:
                                layer_norm(t + 1)
                            if has_prev and pair == 1 and k == 3:
                                dve.wait_ge(out_ready, t)
                                own = x[:, ds(t - 1, 1), :].rearrange("p a d -> p (a d)")
                                nc.vector.tensor_tensor(own, M[:, 0:D], own, ALU.add).then_inc(x_added, 1)
                            if has_next and pair == 2 and k == 2:
                                dve.wait_ge(counted, t + 1)
                                dve.wait_ge(rows_summed, t + 1)
                                build_mask(nc, dve, mask[:, 1 - s, :], mask[:, 1 - s, ds(t + 1, P)], ident,
                                           mask_step, 3 * t)
                            if has_next and pair == 3 and k == 0:
                                split_queries(t + 1)

                over_tiles(dve, body)
                dve.wait_ge(x_added, TILES)

            @block.scalar
            def _(act):
                def relu(n):
                    act.wait_ge(x_turned, n)
                    wait(act, q_ready, n - 1)
                    nc.scalar.activation(hT[:, :, :], M[:, 0:D].rearrange("p (c n) -> p c n", c=DC),
                                         ACT.Relu).then_inc(relu_done, 1)

                def round_queries(n):
                    act.wait_ge(q_ready, n)
                    for p in range(PAIRS):
                        wait(act, q_stacked[p], 128 * (n - 1))
                    nc.scalar.activation(q_hi[:, :, :], M[:, :].rearrange("p (a n) -> p a n", a=PAIRS),
                                         ACT.Copy, scale=-SCORE_SCALE).then_inc(q_high, 1)

                def sum_rows(n, s):
                    act.wait_ge(adj_loaded, 16 * n)
                    wait(act, rows_summed, n - 1)
                    nc.scalar.activation(adj_copy[:, :], mask[:, s, :], ACT.Copy,
                                         accum_out=row_sum[:, ds(n, 1)]).then_inc(rows_summed, 1)

                def body(t, s, has_prev, has_cur, has_next):
                    for pair in range(PAIRS):
                        g = PAIRS * t + pair
                        for k in range(QUARTERS):
                            turn_prev = (has_cur or pair == 0) and (has_prev or pair >= 1)
                            if turn_prev:
                                q = QUARTERS * (g - 1) + k
                                act.wait_ge(turned[0], q + 1)
                                wait(act, quarter_used, q - 1)
                                nc.scalar.activation(probs_T[:, k % 2, 0, :], T[0][:, :], ACT.Copy)\
                                    .then_inc(copied[0], 1)
                            if turn_prev and k == 1:
                                act.wait_ge(inv_turned, g)
                                wait(act, pair_normed, g - 2)
                                nc.scalar.activation(inv_rows[:, (pair - 1) % 2, :], M[:, 0:P], ACT.Copy)\
                                    .then_inc(inv_copied, 1)
                            if has_next and pair == 1 and k == 2:
                                sum_rows(t + 1, 1 - s)
                            if has_next and pair == 2 and k == 0:
                                relu(t + 1)
                            if has_next and pair == 2 and k == 3:
                                round_queries(t + 1)
                            if has_cur and k % 2 == 1:
                                h = 2 * pair + k // 2
                                act.wait_ge(head_masked, HEADS * t + h + 1)
                                nc.scalar.activation(probs[:, h % 4, :], probs[:, h % 4, :], ACT.Exp,
                                                     bias=head_min[:, h:h + 1], scale=-1.0,
                                                     accum_out=prob_sum[:, h:h + 1]).then_inc(probs_ready, 1)

                over_tiles(act, body)

            @block.tensor
            def _(pe):
                def turn_x(n):
                    pe.wait_ge(centred, n)
                    for d in range(DC):
                        last = nc.tensor.transpose(M[:, d * P:(d + 1) * P], xc[:, d * P:(d + 1) * P],
                                                   ident["i"][:, :])
                    last.then_inc(x_turned, 1)

                def project_queries(n):
                    pe.wait_ge(relu_done, n)
                    for p in range(PAIRS):
                        for d in range(DC):
                            last = nc.tensor.matmul(M[:, p * P:(p + 1) * P], w["q"][:, d, p * P:(p + 1) * P],
                                                    hT[:, d, :], start=(d == 0), stop=(d == DC - 1))
                    last.then_inc(q_ready, 1)

                def scores(t, pair, j):
                    half, c = divmod(j, QUARTERS)
                    h = 2 * pair + half
                    i = h * QUARTERS + c
                    if j == 0:
                        wait(pe, q_stacked[pair], 128 * t)
                    if i >= 3:
                        pe.wait_ge(scores_read, CHUNKS * t + i - 2)
                    else:
                        wait(pe, scores_read, CHUNKS * t - (1, 0, 2)[i])
                    keys = k_stack[:, h, c * BANK:(c + 1) * BANK]
                    for part in range(2):
                        last = nc.tensor.matmul(chunk_bank(i)[:, :], q_stack[:, h, part, :], keys,
                                                start=(part == 0), stop=(part == 1))
                    last.then_inc(scores_ready, 1)

                def turn_probs(pair, g, k):
                    for half in range(2):
                        slot = (2 * pair + half) % 4
                        if k == 0:
                            pe.wait_ge(probs_ready, 2 * g + half + 1)
                        wait(pe, copied[half], QUARTERS * g + k)
                        for b in range(BANK // P):
                            m = k * (BANK // P) + b
                            last = nc.tensor.transpose(T[half][:, b * P:(b + 1) * P],
                                                       probs[:, slot, m * P:(m + 1) * P], ident["i"][:, :])
                        last.then_inc(turned[half], 1)

                def weigh_values(pair, g, k):
                    for half in range(2):
                        pe.wait_ge(copied[half], QUARTERS * g + k + 1)
                    if k == 0:
                        wait(pe, pair_normed, g - 1)
                    for b in range(BANK // P):
                        m = k * (BANK // P) + b
                        for half in range(2):
                            h = 2 * pair + half
                            last = nc.tensor.matmul(O[pair % 2][half * HD:(half + 1) * HD, 0:P],
                                                    v[:, m, h * HD:(h + 1) * HD],
                                                    probs_T[:, k % 2, half, b * P:(b + 1) * P],
                                                    start=(m == 0), stop=(m == TILES - 1))
                    last.then_inc(quarter_used, 1)

                def body(t, s, has_prev, has_cur, has_next):
                    for pair in range(PAIRS):
                        g = PAIRS * t + pair
                        turn_prev = (has_cur or pair == 0) and (has_prev or pair >= 1)
                        last_prev = (has_cur or pair <= 1) and (has_prev or pair >= 2)
                        for k in range(QUARTERS):
                            if has_cur:
                                scores(t, pair, 2 * k)
                                scores(t, pair, 2 * k + 1)
                            if turn_prev:
                                turn_probs((pair - 1) % PAIRS, g - 1, k)
                            if k == 0 and last_prev:
                                weigh_values((pair - 2) % PAIRS, g - 2, QUARTERS - 1)
                            if k >= 1 and turn_prev:
                                weigh_values((pair - 1) % PAIRS, g - 1, k - 1)
                            if k == 1 and turn_prev:
                                pe.wait_ge(inv_ready, g)
                                wait(pe, inv_copied, g - 1)
                                if pair == 2 and has_next:
                                    pe.wait_ge(relu_done, t + 1)
                                if pair == 2 and has_prev:
                                    wait(pe, x_added, t)
                                if pair == 3 and has_next:
                                    pe.wait_ge(q_split, t + 1)
                                nc.tensor.transpose(M[:, 0:P], inv_cols[:, :, :].rearrange("p a n -> p (a n)"),
                                                    ident["i"][:, :]).then_inc(inv_turned, 1)
                            if k == 2 and pair == 1 and has_prev:
                                pe.wait_ge(pair_normed, g - 1)
                                wait(pe, inv_copied, g if has_cur else g - 1)
                                for p in range(PAIRS):
                                    last = nc.tensor.matmul(M[:, 0:D], heads_T[:, p, :], w["o"][:, p, :],
                                                            start=(p == 0), stop=(p == PAIRS - 1))
                                last.then_inc(out_ready, 1)
                            if k == 0 and pair == 2 and has_next:
                                wait(pe, x_added, t)
                                pe.wait_ge(inv_copied, g - 1)
                                turn_x(t + 1)
                            if k == 2 and pair == 2 and has_next:
                                pe.wait_ge(inv_copied, g)
                                project_queries(t + 1)

                over_tiles(pe, body)


def graph_layers(nc, x, ident, eps, row_sum, col_count, dram, out):
    with ExitStack() as ctx:
        def sb(name, shape, dt=F32):
            return ctx.enter_context(nc.sbuf_tensor(name, shape, dt))

        def sem(name):
            return ctx.enter_context(nc.semaphore(name))

        def ps(name):
            return ctx.enter_context(nc.psum_tensor(name, [P, BANK], F32))

        adj = sb("adj_in", [P, 2, N])
        adj_T = sb("adj_T", [P, TILES, N], U8)
        block_T = sb("block_T", [P, 2, N], F32R)
        parts = [sb(f"parts{i}", [P, TILES, 2, D], F32R) for i in range(2)]
        xc = sb("c_xc", [P, 2, D])
        hT = sb("c_hT", [P, 2, DC, P])
        y = sb("y", [P, 2, DX])
        yr = sb("yr", [P, D])
        stats = sb("c_stats", [P, 6])
        mv = sb("c_mv", [P, 2, 2])
        std = sb("c_std", [P, 2])
        rstd = sb("c_rstd", [P, 2])
        deg1 = sb("deg1", [P, TILES])
        w1 = sb("w1", [P, DC, D])
        w2 = sb("w2", [P, DC, D])
        w3 = sb("w3", [P, DC, DX])
        bias = sb("bias", [P, 3, DX])
        gat_k = sb("gat_k", [P, DC, GAT_HEADS, D])
        ones = sb("ones", [P, P])
        ident_r = sb("ident_r", [P, P], F32R)
        ones_b = sb("ones_b", [P, 1], BF16)
        in_deg_inv = sb("in_deg_inv", [P, TILES])
        r = sb("r", [P, TILES])
        r_any = sb("r_any", [P, TILES])
        scores = sb("gat_scores", [P, TILES, GAT_HEADS])
        w_adj = sb("w_adj", [P, TILES, GAT_HEADS])
        w_all = sb("w_all", [P, TILES, GAT_HEADS])
        g_tmp = sb("g_tmp", [P, 4, TILES, GAT_HEADS])
        y_sum = sb("y_sum", [P, D])
        all_sum_T = sb("all_sum_T", [P, DC, P])
        all_k = sb("all_k", [P, GAT_HEADS, D])
        u = sb("u", [P, 2, D])
        acc = sb("acc", [P, 2, D])
        w2a = sb("w2a", [P, D])
        w2b = sb("w2b", [P, DC, P])
        w2b_T = sb("w2b_T", [P, D])
        wn_T = sb("wn_T", [P, DC, D])
        a_bc = sb("a_bc", [P, 2, GAT_HEADS, D])
        va = sb("va", [P, DC, GAT_HEADS])
        va_junk = sb("va_junk", [P, D])
        b_col = sb("b_col", [P, 1 + DC])
        b_bc = sb("b_bc", [P, 1 + DC, P])

        turn_ps = [ps("c_turn0"), ps("c_turn1")]
        sum_ps = [ps("sum0"), ps("sum1")]
        small_ps = ps("small")
        dense_ps = [ps("dense0"), ps("dense1")]
        z_ps = [[dense_ps[0], dense_ps[1]], [turn_ps[1], ps("z3")]]

        loaded = sem("weights_loaded")
        sp_passed = sem("c_sp_passed")
        dve_passed = sem("c_dve_passed")
        adj_in = [sem("adj_in0"), sem("adj_in1")]
        prep_pool = sem("prep_pool")
        prep_dve = sem("prep_dve")
        prep_pe = sem("prep_pe")
        prep_act = sem("prep_act")
        ln_step = sem("c_ln_step")
        stats_ready = sem("c_stats_ready")
        std_ready = sem("c_std_ready")
        rstd_ready = sem("c_rstd_ready")
        deg_ready = sem("deg_ready")
        deg_root = sem("deg_root")
        x_step = sem("x_step")
        centred = sem("c_centred")
        x_turned = sem("c_x_turned")
        h_ready = sem("h_ready")
        dense_ready = sem("dense_ready")
        y_step = sem("y_step")
        y_split = sem("y_split")
        y_summed = sem("y_summed")
        adj_turned = sem("adj_turned")
        adj_kept_even = sem("adj_kept_even")
        adj_kept_odd = sem("adj_kept_odd")
        block_ready = sem("block_ready")
        sums_ready = sem("sums_ready")
        gat_step = sem("gat_step")
        gat_exp = sem("gat_exp")
        z_ready = sem("z_ready")
        z_step = sem("z_step")
        out_ready = sem("tile_out_ready")
        out_stored = [sem("out_stored0"), sem("out_stored1")]

        QB = BANK // P
        LOADS = 14
        VECTORS = 3 + 1 + DC * GAT_HEADS + 1 + DC
        YS = 3
        XS = 2

        def one(ap):
            return ap.rearrange("p a d -> p (a d)")

        def over_ticks(eng, tick, first=2, lead=0):
            def peeled(t):
                tick(t, t % 2, lambda lag: 0 <= t - lag < TILES)
            for t in range(first):
                peeled(t)
            with eng.Fori(first // 2, TILES // 2 - lead) as i:
                for s in range(2):
                    tick(2 * i + s, s, lambda lag: True)
            for t in range(TILES - 2 * lead, TILES + 2):
                peeled(t)

        with nc.Block() as block:

            @block.sync
            def _(sp):
                adj_rows = dram["adj"].rearrange("(t p) n -> t p n", p=P)

                def flat_bc(ap, n):
                    return ap.rearrange("(a n) -> a n", a=1).broadcast_to([P, n])

                def load_adj(t, s):
                    sp.dma_start(adj[:, s, :], adj_rows[ds(t, 1), :, :].rearrange("a p n -> (a p) n"))\
                        .then_inc(adj_in[s], 16)

                sp.dma_start(w1[:, :, :], dram["L1_gnn_W"].rearrange("(c p) o -> p c o", p=P)).then_inc(loaded, 16)
                sp.dma_start(bias[:, 0, 0:D], flat_bc(dram["L1_gnn_b"], D)).then_inc(loaded, 16)
                load_adj(0, 0)
                load_adj(1, 1)
                sp.dma_start(w2a[:, :], dram["L2_gnn_W1"]).then_inc(loaded, 16)
                sp.dma_start(w2b[:, :, :], dram["L2_gnn_W2"].rearrange("(c p) m -> p c m", p=P)).then_inc(loaded, 16)
                sp.dma_start(bias[:, 1, 0:D], flat_bc(dram["L2_gnn_b2"], D)).then_inc(loaded, 16)
                sp.dma_start(w3[:, :, 0:D], dram["L3_gnn_W_node"].rearrange("(c p) o -> p c o", p=P)).then_inc(loaded, 16)
                sp.dma_start(bias[:, 2, 0:D], flat_bc(dram["L3_gnn_b_node"], D)).then_inc(loaded, 16)
                for c in range(DC):
                    sp.dma_start(gat_k[:, c, :, :],
                                 dram["L3_gnn_K"][:, c * P:(c + 1) * P, :].rearrange("h p f -> p h f"))\
                        .then_inc(loaded, 16)
                for i, name in enumerate(("L3_gnn_A_self", "L3_gnn_A_neigh")):
                    sp.dma_start(a_bc[:, i, :, :].rearrange("p h f -> p (h f)"),
                                 flat_bc(dram[name].rearrange("h f -> (h f)"), GAT_HEADS * D)).then_inc(loaded, 16)
                sp.dma_start(b_col[:, 0:1], dram["L2_gnn_b1"].rearrange("(p a) -> p a", a=1)).then_inc(loaded, 16)
                for c in range(DC):
                    sp.dma_start(b_col[:, 1 + c:2 + c],
                                 dram["L3_gnn_b_node"][c * P:(c + 1) * P].rearrange("(p a) -> p a", a=1))\
                        .then_inc(loaded, 16)
                with sp.Fori(1, TILES // 2) as i:
                    for s in range(2):
                        t = 2 * i + s
                        wait_apart(sp, adj_turned, QUARTERS * (t - 1), sp_passed)
                        load_adj(t, s)
                out_rows = out.rearrange("(t p) d -> t p d", p=P)

                def store(t, s):
                    wait_apart(sp, out_ready, t + 1, sp_passed)
                    sp.dma_start(out_rows[ds(t, 1), :, :].rearrange("a p d -> (a p) d"), acc[:, s, :])\
                        .then_inc(out_stored[s], 16)

                with sp.Fori(0, TILES // 2) as i:
                    for s in range(2):
                        store(2 * i + s, s)
                for s in range(2):
                    wait_apart(sp, out_stored[s], 16 * TILES // 2, sp_passed)

            @block.gpsimd
            def _(pool):
                nc.gpsimd.memset(ones[:, :], 1.0).then_inc(prep_pool, 1)
                nc.gpsimd.memset(ones_b[:, :], 1.0).then_inc(prep_pool, 1)
                nc.gpsimd.memset(y_sum[:, :], 0.0).then_inc(prep_pool, 1)
                pool.wait_ge(prep_pool, 3)

                def add_y(t, s):
                    pool.wait_ge(y_step, YS * (2 * TILES + t) + 1)
                    wait(pool, y_summed, t)
                    nc.gpsimd.tensor_tensor(y_sum[:, :], y[:, s, 0:D], y_sum[:, :], ALU.add)\
                        .then_inc(y_summed, 1)

                add_y(0, 0)
                add_y(1, 1)
                with pool.Fori(1, TILES // 2) as i:
                    for s in range(2):
                        add_y(2 * i + s, s)

            @block.vector
            def _(dve):
                def statistics(n, t, s):
                    nc.vector.bn_stats(stats[:, :], one(x[:, ds(t, 1), :])).then_inc(ln_step, 1)
                    wait_apart(dve, ln_step, n + 1, dve_passed)
                    nc.vector.bn_aggr(mv[:, s, :], stats[:, :]).then_inc(stats_ready, 1)

                def center(n, t, s):
                    own = one(x[:, ds(t, 1), :])
                    dve.wait_ge(std_ready, n + 1)
                    nc.vector.reciprocal(rstd[:, s:s + 1], std[:, s:s + 1]).then_inc(rstd_ready, 1)
                    dve.wait_ge(rstd_ready, n + 1)
                    wait(dve, x_turned, n - 1)
                    nc.vector.tensor_scalar(xc[:, s, :], own, mv[:, s, 0:1], rstd[:, s:s + 1],
                                            ALU.subtract, ALU.mult).then_inc(centred, 1)

                def finish_y(layer, t, s):
                    n = (layer - 1) * TILES + t
                    width = DX if layer == 3 else D
                    dve.wait_ge(dense_ready, n + 1)
                    if layer == 3:
                        wait(dve, y_summed, t - 1)
                    nc.vector.tensor_tensor(y[:, s, 0:width], dense_ps[s][:, 0:width], bias[:, layer - 1, 0:width],
                                            ALU.add).then_inc(y_step, 1)
                    dve.wait_ge(y_step, YS * n + 1)
                    if layer == 2:
                        nc.vector.tensor_scalar(yr[:, :], y[:, s, 0:D], r[:, ds(t, 1)], None, ALU.mult)\
                            .then_inc(y_step, 1)
                        full = yr[:, :]
                    elif layer == 3:
                        nc.vector.tensor_copy(one(scores[:, ds(t, 1), :]), y[:, s, D:DX]).then_inc(y_step, 1)
                        full = y[:, s, 0:D]
                    else:
                        dve.sem_inc(y_step, 1)
                        full = y[:, s, 0:D]
                    dve.wait_ge(y_step, YS * n + 2)
                    to = parts[layer % 2]
                    hi = to[:, ds(t, 1), 0, :].rearrange("p a d -> p (a d)")
                    lo = to[:, ds(t, 1), 1, :].rearrange("p a d -> p (a d)")
                    nc.vector.tensor_copy(hi, full).then_inc(y_step, 1)
                    dve.wait_ge(y_step, YS * n + 3)
                    nc.vector.tensor_tensor(lo, full, hi.bitcast(F32), ALU.subtract).then_inc(y_split, 1)

                nc.vector.tensor_copy(ident_r[:, :], ident["i"][:, :]).then_inc(prep_dve, 1)
                dve.wait_ge(loaded, 16 * LOADS)
                dve.wait_ge(prep_pe, 1)
                nc.vector.reciprocal(in_deg_inv[:, :], small_ps[:, 0:TILES]).then_inc(prep_dve, 1)

                def first_tick(t, s, live):
                    if live(0):
                        statistics(t, t, s)
                        for q in range(2):
                            n = QUARTERS * t + 2 * q + 1
                            dve.wait_ge(adj_turned, n + 1)
                            nc.vector.tensor_copy(adj_T[:, ds(t, 1), (2 * q + 1) * BANK:(2 * q + 2) * BANK]
                                                  .rearrange("p a n -> p (a n)"), sum_ps[1][:, :])\
                                .then_inc(adj_kept_odd, 1)
                    if live(2):
                        finish_y(1, t - 2, s)
                    if live(0):
                        center(t, t, s)

                over_ticks(dve, first_tick, first=4)

                dve.wait_ge(prep_pool, 3)
                nc.vector.tensor_scalar(deg1[:, :], row_sum[:, :], 1.0, 1.0 / HUGE, ALU.add, ALU.max)\
                    .then_inc(deg_ready, 1)
                dve.wait_ge(deg_root, 1)
                nc.vector.reciprocal(deg1[:, :], r_any[:, :]).then_inc(deg_ready, 1)
                dve.wait_ge(deg_ready, 2)
                nc.vector.scalar_tensor_tensor(out=r[:, :], in0=row_sum[:, :], scalar=-1.0, in1=deg1[:, :],
                                               op0=ALU.is_gt, op1=ALU.mult).then_inc(prep_dve, 1)
                dve.wait_ge(prep_dve, 3)
                at = 3
                nc.vector.tensor_tensor(a_bc[:, 0, :, :], a_bc[:, 0, :, :], a_bc[:, 1, :, :], ALU.add)\
                    .then_inc(prep_dve, 1)
                dve.wait_ge(prep_dve, at + 1)
                for c in range(DC):
                    for h in range(GAT_HEADS):
                        nc.vector.tensor_tensor_reduce(va_junk[:, :], gat_k[:, c, h, :], a_bc[:, 0, h, :],
                                                       1.0, 0.0, ALU.mult, ALU.add, va[:, c, h:h + 1])\
                            .then_inc(prep_dve, 1)
                        dve.wait_ge(prep_dve, at + 2 + c * GAT_HEADS + h)
                for i in range(1 + DC):
                    nc.vector.tensor_scalar(b_bc[:, i, :], ones[:, :], b_col[:, i:i + 1], None, ALU.mult)\
                        .then_inc(prep_dve, 1)
                dve.wait_ge(prep_pe, 3)
                nc.vector.tensor_tensor(bias[:, 1, 0:D], small_ps[:, 0:D], bias[:, 1, 0:D], ALU.add)\
                    .then_inc(prep_dve, 1)
                dve.wait_ge(prep_pe, 6)
                nc.vector.tensor_copy(bias[:, 2, D:DX], small_ps[:, 0:GAT_HEADS]).then_inc(prep_dve, 1)
                dve.wait_ge(prep_dve, VECTORS + 2)

                def layer_tick(layer):
                    def tick(t, s, live):
                        n = (layer - 1) * TILES + t
                        if live(0):
                            scale = in_deg_inv if layer == 1 else r
                            own = one(x[:, ds(t, 1), :])
                            dve.wait_ge(sums_ready, n + 1)
                            nc.vector.scalar_tensor_tensor(out=own, in0=sum_ps[s][:, 0:D], scalar=scale[:, ds(t, 1)],
                                                           in1=own, op0=ALU.mult, op1=ALU.add).then_inc(x_step, 1)
                            dve.wait_ge(x_step, XS * n + 1)
                            nc.vector.scalar_tensor_tensor(out=own, in0=sum_ps[s][:, D:2 * D],
                                                           scalar=scale[:, ds(t, 1)],
                                                           in1=own, op0=ALU.mult, op1=ALU.add).then_inc(x_step, 1)
                            wait_apart(dve, x_step, XS * n + 2, dve_passed)
                            statistics(n + TILES, t, s)
                        if live(2):
                            finish_y(layer + 1, t - 2, s)
                        if live(0):
                            center(n + TILES, t, s)
                    return tick

                over_ticks(dve, layer_tick(1))
                over_ticks(dve, layer_tick(2), first=4)

                dve.wait_ge(y_split, 3 * TILES)
                step = [0]

                def link(ins):
                    step[0] += 1
                    ins.then_inc(gat_step, 1)
                    dve.wait_ge(gat_step, step[0])

                deg = row_sum[:, :].unsqueeze(2).to_broadcast([P, TILES, GAT_HEADS])
                lrelu, top, e_adj, e_all = (g_tmp[:, i, :, :] for i in range(4))
                link(nc.vector.scalar_tensor_tensor(out=lrelu, in0=scores[:, :, :], scalar=ALPHA,
                                                    in1=scores[:, :, :], op0=ALU.mult, op1=ALU.max))
                link(nc.vector.tensor_scalar(top, deg, 1.0, -NEG, ALU.min, ALU.mult))
                link(nc.vector.scalar_tensor_tensor(out=top, in0=top, scalar=NEG, in1=lrelu,
                                                    op0=ALU.add, op1=ALU.add))
                link(nc.vector.tensor_tensor(e_adj, lrelu, top, ALU.subtract))
                link(nc.vector.tensor_scalar(e_adj, e_adj, 0.0, None, ALU.min))
                link(nc.vector.scalar_tensor_tensor(out=e_all, in0=lrelu, scalar=NEG, in1=top,
                                                    op0=ALU.add, op1=ALU.subtract))
                dve.wait_ge(gat_exp, 2)
                link(nc.vector.tensor_scalar(lrelu, deg, -1.0, float(N), ALU.mult, ALU.add))
                link(nc.vector.tensor_tensor(lrelu, lrelu, e_all, ALU.mult))
                link(nc.vector.tensor_tensor(top, deg, e_adj, ALU.mult))
                link(nc.vector.tensor_tensor(top, top, lrelu, ALU.add))
                link(nc.vector.reciprocal(lrelu, top))
                link(nc.vector.tensor_scalar(lrelu, lrelu, 1.0 / GAT_HEADS, None, ALU.mult))
                link(nc.vector.tensor_tensor(e_adj, e_adj, e_all, ALU.subtract))
                link(nc.vector.tensor_tensor(w_adj[:, :, :], e_adj, lrelu, ALU.mult))
                link(nc.vector.tensor_tensor(w_all[:, :, :], e_all, lrelu, ALU.mult))

                def out_tick(t, s, live):
                    if live(0):
                        n = 2 * TILES + t
                        dve.wait_ge(sums_ready, n + 1)
                        wait(dve, x_turned, n + TILES - 1)
                        nc.vector.tensor_copy(u[:, s, :], sum_ps[s][:, 0:D]).then_inc(x_step, 1)
                        dve.wait_ge(x_step, XS * n + 1)
                        nc.vector.tensor_tensor(u[:, s, :], sum_ps[s][:, D:2 * D], u[:, s, :], ALU.add)\
                            .then_inc(x_step, 1)
                    if live(2):
                        o = t - 2
                        to = acc[:, s, :]
                        if isinstance(o, int):
                            wait(dve, out_stored[s], 16 * (o // 2))
                        else:
                            dve.wait_ge(out_stored[s], (o - s) * 8)
                        k = 0
                        for h in range(GAT_HEADS):
                            src = all_k[:, h, :]
                            wgt = w_all[:, ds(o, 1), h]
                            if h == 0:
                                nc.vector.tensor_scalar(to, src, wgt, None, ALU.mult).then_inc(z_step, 1)
                            else:
                                nc.vector.scalar_tensor_tensor(out=to, in0=src, scalar=wgt, in1=to,
                                                               op0=ALU.mult, op1=ALU.add).then_inc(z_step, 1)
                            k += 1
                            dve.wait_ge(z_step, 2 * GAT_HEADS * o + k)
                        dve.wait_ge(z_ready, o + 1)
                        for h in range(GAT_HEADS):
                            z = z_ps[s][h // 2][:, (h % 2) * D:(h % 2 + 1) * D]
                            nc.vector.scalar_tensor_tensor(out=to, in0=z, scalar=w_adj[:, ds(o, 1), h], in1=to,
                                                           op0=ALU.mult, op1=ALU.add).then_inc(z_step, 1)
                            k += 1
                            dve.wait_ge(z_step, 2 * GAT_HEADS * o + k)
                        nc.vector.scalar_tensor_tensor(out=to, in0=to, scalar=0.0, in1=one(x[:, ds(o, 1), :]),
                                                       op0=ALU.max, op1=ALU.add).then_inc(out_ready, 1)

                over_ticks(dve, out_tick, first=4)

            @block.scalar
            def _(act):
                def relu(n, s, func=ACT.Relu):
                    act.wait_ge(x_turned, n + 1)
                    if func == ACT.Relu:
                        wait(act, dense_ready, n - 1)
                    else:
                        act.wait_ge(dense_ready, 3 * TILES)
                        wait(act, z_ready, n - 1 - 3 * TILES)
                    nc.scalar.activation(hT[:, s, :, :], turn_ps[0][:, 0:D].rearrange("p (c n) -> p c n", c=DC),
                                         func).then_inc(h_ready, 1)

                def deviation(n, s):
                    act.wait_ge(stats_ready, n + 1)
                    nc.scalar.activation(std[:, s:s + 1], mv[:, s, 1:2], ACT.Sqrt, bias=eps[:, :])\
                        .then_inc(std_ready, 1)

                def widen(n, t, s):
                    wait(act, sums_ready, n - 1)
                    nc.scalar.activation(block_T[:, s, :], one(adj_T[:, ds(t, 1), :]), ACT.Copy)\
                        .then_inc(block_ready, 1)

                def first_tick(t, s, live):
                    if live(0):
                        for q in range(2):
                            n = QUARTERS * t + 2 * q
                            act.wait_ge(adj_turned, n + 1)
                            nc.scalar.activation(adj_T[:, ds(t, 1), 2 * q * BANK:(2 * q + 1) * BANK]
                                                 .rearrange("p a n -> p (a n)"), sum_ps[0][:, :], ACT.Copy)\
                                .then_inc(adj_kept_even, 1)
                    if live(1):
                        relu(t - 1, 1 - s)
                    if live(0):
                        deviation(t, s)

                over_ticks(act, first_tick, first=4)
                act.wait_ge(adj_kept_even, 2 * TILES)
                act.wait_ge(adj_kept_odd, 2 * TILES)

                act.wait_ge(deg_ready, 1)
                nc.scalar.activation(r_any[:, :], deg1[:, :], ACT.Sqrt).then_inc(deg_root, 1)

                act.wait_ge(prep_pe, 2)
                nc.scalar.activation(w2b_T[:, :], turn_ps[1][:, 0:D], ACT.Copy).then_inc(prep_act, 1)
                for d in range(DC):
                    act.wait_ge(prep_pe, 4 + d)
                    if d == 0:
                        nc.scalar.activation(w2[:, :, :].rearrange("p c o -> p (c o)"), dense_ps[0][:, :], ACT.Copy)\
                            .then_inc(prep_act, 1)
                    nc.scalar.activation(wn_T[:, d, :], sum_ps[d][:, 0:D], ACT.Copy).then_inc(prep_act, 1)
                act.wait_ge(prep_pe, 7)
                nc.scalar.activation(w3[:, :, D:DX], dense_ps[1][:, 0:DC * GAT_HEADS]
                                     .rearrange("p (c h) -> p c h", c=DC), ACT.Copy).then_inc(prep_act, 1)

                def layer_tick(layer):
                    def tick(t, s, live):
                        n = (layer - 1) * TILES + t
                        if live(-1):
                            widen(n + 1, t + 1, 1 - s)
                        if live(1):
                            relu(n - 1 + TILES, 1 - s, ACT.Relu if layer < 3 else ACT.Copy)
                        if live(0) and layer < 3:
                            deviation(n + TILES, s)
                    return tick

                def run_layer(layer):
                    widen((layer - 1) * TILES, 0, 0)
                    over_ticks(act, layer_tick(layer), lead=1)

                run_layer(1)
                run_layer(2)
                widen(2 * TILES, 0, 0)
                act.wait_ge(gat_step, 6)
                for i in (2, 3):
                    nc.scalar.activation(g_tmp[:, i, :, :], g_tmp[:, i, :, :], ACT.Exp).then_inc(gat_exp, 1)
                act.wait_ge(prep_pe, 8)
                nc.scalar.activation(all_sum_T[:, :, :], small_ps[:, 0:D].rearrange("p (c n) -> p c n", c=DC),
                                     ACT.Copy).then_inc(prep_act, 1)
                act.wait_ge(prep_pe, 9)
                for i in range(2):
                    nc.scalar.activation(all_k[:, 2 * i:2 * i + 2, :].rearrange("p h f -> p (h f)"),
                                         dense_ps[i][:, :], ACT.Copy).then_inc(prep_act, 1)
                over_ticks(act, layer_tick(3), first=4, lead=1)

            @block.tensor
            def _(pe):
                def turn(n, s, src):
                    pe.wait_ge(centred, n + 1) if src is xc else pe.wait_ge(x_step, XS * (n - TILES) + 2)
                    wait(pe, h_ready, n)
                    for d in range(DC):
                        last = nc.tensor.transpose(turn_ps[0][:, d * P:(d + 1) * P],
                                                   src[:, s, d * P:(d + 1) * P], ident["i"][:, :])
                    last.then_inc(x_turned, 1)

                def dense(layer, n, s):
                    pe.wait_ge(h_ready, n + 1)
                    wait(pe, y_step, YS * (n - 2) + 1)
                    weights, width = ((w1, D), (w2, D), (w3, DX))[layer - 1]
                    for d in range(DC):
                        last = nc.tensor.matmul(dense_ps[s][:, 0:width], hT[:, s, d, :], weights[:, d, :],
                                                start=(d == 0), stop=(d == DC - 1))
                    last.then_inc(dense_ready, 1)

                def sums(layer, n, t, s):
                    pe.wait_ge(block_ready, n + 1)
                    wait(pe, x_step, XS * (n - 1))
                    src = parts[layer % 2]
                    if layer == 2:
                        nc.tensor.matmul(sum_ps[s][:, :], ident_r[:, :], src[:, ds(t, 1), :, :],
                                         start=True, stop=False)
                    for j in range(TILES):
                        last = nc.tensor.matmul(sum_ps[s][:, :], block_T[:, s, j * P:(j + 1) * P],
                                                src[:, j, :, :], start=(j == 0 and layer != 2),
                                                stop=(j == TILES - 1))
                    last.then_inc(sums_ready, 1)

                pe.wait_ge(prep_pool, 3)
                for t in range(TILES):
                    last = nc.tensor.matmul(small_ps[:, t:t + 1], col_count[:, t * P:(t + 1) * P], ones_b[:, :],
                                            start=True, stop=True)
                last.then_inc(prep_pe, 1)
                pe.wait_ge(loaded, 16 * LOADS)

                def first_tick(t, s, live):
                    if live(0):
                        pe.wait_ge(adj_in[s], (t - s) * 8 + 16)
                        for q in range(QUARTERS):
                            if q % 2 == 0:
                                wait(pe, adj_kept_even, 2 * t + q // 2)
                            else:
                                wait(pe, adj_kept_odd, 2 * t + q // 2)
                            for b in range(QB):
                                m = q * QB + b
                                last = nc.tensor.transpose(sum_ps[q % 2][:, b * P:(b + 1) * P],
                                                           adj[:, s, m * P:(m + 1) * P], ident["i"][:, :])
                            last.then_inc(adj_turned, 1)
                    if live(1):
                        turn(t - 1, 1 - s, xc)
                    if live(2):
                        dense(1, t - 2, s)

                over_ticks(pe, first_tick, first=4)

                pe.wait_ge(prep_dve, VECTORS)
                pe.wait_ge(adj_kept_even, 2 * TILES)
                pe.wait_ge(adj_kept_odd, 2 * TILES)
                pe.wait_ge(y_split, TILES)
                for c in range(DC):
                    last = nc.tensor.transpose(turn_ps[1][:, c * P:(c + 1) * P], w2b[:, c, :], ident["i"][:, :])
                last.then_inc(prep_pe, 1)
                pe.wait_ge(prep_act, 1)
                nc.tensor.matmul(small_ps[:, 0:D], b_bc[:, 0, :], w2b_T[:, :], start=True, stop=True)\
                    .then_inc(prep_pe, 1)
                for c in range(DC):
                    nc.tensor.matmul(dense_ps[0][:, c * D:(c + 1) * D], w2a[:, c * P:(c + 1) * P], w2b_T[:, :],
                                     start=True, stop=True)
                for d in range(DC):
                    for c in range(DC):
                        last = nc.tensor.transpose(sum_ps[d][:, c * P:(c + 1) * P],
                                                   w3[:, c, d * P:(d + 1) * P], ident["i"][:, :])
                    last.then_inc(prep_pe, 1)
                pe.wait_ge(prep_dve, VECTORS + 1)
                for d in range(DC):
                    last = nc.tensor.matmul(small_ps[:, 0:GAT_HEADS], b_bc[:, 1 + d, :], va[:, d, :],
                                            start=(d == 0), stop=(d == DC - 1))
                last.then_inc(prep_pe, 1)
                pe.wait_ge(prep_act, 4)
                for c in range(DC):
                    for d in range(DC):
                        last = nc.tensor.matmul(dense_ps[1][:, c * GAT_HEADS:(c + 1) * GAT_HEADS],
                                                wn_T[:, d, c * P:(c + 1) * P], va[:, d, :],
                                                start=(d == 0), stop=(d == DC - 1))
                last.then_inc(prep_pe, 1)
                pe.wait_ge(prep_act, 5)
                pe.wait_ge(prep_dve, VECTORS + 2)

                def layer_tick(layer):
                    def tick(t, s, live):
                        n = (layer - 1) * TILES + t
                        if live(0):
                            sums(layer, n, t, s)
                        if live(1):
                            turn(n - 1 + TILES, 1 - s, xc)
                        if live(2):
                            dense(layer + 1, n - 2 + TILES, s)
                    return tick

                for layer in (1, 2):
                    pe.wait_ge(y_split, layer * TILES)
                    over_ticks(pe, layer_tick(layer))
                pe.wait_ge(y_split, 3 * TILES)
                pe.wait_ge(y_summed, TILES)
                for c in range(DC):
                    last = nc.tensor.matmul(small_ps[:, c * P:(c + 1) * P], y_sum[:, c * P:(c + 1) * P], ones[:, :],
                                            start=True, stop=True)
                last.then_inc(prep_pe, 1)
                pe.wait_ge(prep_act, 6)
                pe.wait_ge(y_step, YS * 3 * TILES)
                for i in range(2):
                    for c in range(DC):
                        last = nc.tensor.matmul(dense_ps[i][:, :], all_sum_T[:, c, :],
                                                gat_k[:, c, 2 * i:2 * i + 2, :],
                                                start=(c == 0), stop=(c == DC - 1))
                last.then_inc(prep_pe, 1)
                pe.wait_ge(prep_act, 8)

                def out_tick(t, s, live):
                    n = 2 * TILES + t
                    if live(0):
                        sums(3, n, t, s)
                    if live(1):
                        turn(n - 1 + TILES, 1 - s, u)
                    if live(2):
                        o = t - 2
                        pe.wait_ge(h_ready, n - 2 + TILES + 1)
                        wait(pe, z_step, 2 * GAT_HEADS * (o - 1))
                        for i in range(2):
                            for c in range(DC):
                                last = nc.tensor.matmul(z_ps[s][i][:, :], hT[:, s, c, :],
                                                        gat_k[:, c, 2 * i:2 * i + 2, :],
                                                        start=(c == 0), stop=(c == DC - 1))
                        last.then_inc(z_ready, 1)

                over_ticks(pe, out_tick, first=4)


def build(nc, dram, out):
    with ExitStack() as ctx:
        def sb(name, shape, dt=F32):
            return ctx.enter_context(nc.sbuf_tensor(name, shape, dt))

        x = sb("x", [P, TILES, D])
        ident = {name: sb("ident_" + name, [P, P]) for name in ("i", "not", "bias")}
        eps = sb("eps", [P, 1])
        col_count = sb("col_count", [P, N], BF16)
        row_sum = sb("row_sum", [P, TILES])
        with ExitStack() as heads:
            k_stack = heads.enter_context(nc.sbuf_tensor("k_stack", [P, HEADS, N], F32R))
            v = heads.enter_context(nc.sbuf_tensor("v", [P, TILES, HEADS * HD], F32))
            w = {"q": heads.enter_context(nc.sbuf_tensor("wq", [P, DC, HEADS * HD], F32)),
                 "o": heads.enter_context(nc.sbuf_tensor("wo", [P, PAIRS, D], F32))}
            mv = heads.enter_context(nc.sbuf_tensor("mean_var", [P, TILES, 2], F32))
            rstd = heads.enter_context(nc.sbuf_tensor("rstd", [P, TILES], F32))
            mask = heads.enter_context(nc.sbuf_tensor("mask", [P, 2, N], F32))
            q_hi = heads.enter_context(nc.sbuf_tensor("q_hi", [P, PAIRS, P], F32R))
            q_lo = heads.enter_context(nc.sbuf_tensor("q_lo", [P, PAIRS, P], F32R))
            q_stack = heads.enter_context(nc.sbuf_tensor("q_stack", [P, HEADS, 2, P], F32R))
            project_keys_values(nc, x, mask, q_hi, q_lo, q_stack, k_stack, v, w, ident, eps, mv, rstd,
                                row_sum, col_count, dram)
            attend(nc, x, mask, q_hi, q_lo, q_stack, k_stack, v, w, ident, mv, rstd, row_sum, col_count, dram)
        graph_layers(nc, x, ident, eps, row_sum, col_count, dram, out)


_INS = ["x", "adj", "L0_gnn_Wks", "L0_gnn_Wqs", "L0_gnn_Wvs", "L0_gnn_Wo", "L1_gnn_W", "L1_gnn_b",
        "L2_gnn_W1", "L2_gnn_b1", "L2_gnn_W2", "L2_gnn_b2", "L3_gnn_W_node", "L3_gnn_b_node",
        "L3_gnn_K", "L3_gnn_A_self", "L3_gnn_A_neigh"]


def kernel(**inputs):
    import numpy as _np
    import concourse.bacc as _bacc
    from concourse import mybir as _mybir
    from concourse.bass_utils import run_bass_kernel_spmd as _run

    nc = _bacc.Bacc("TRN2", target_bir_lowering=False, num_devices=1)
    arrays, dram = {}, {}
    for name in _INS:
        a = _np.ascontiguousarray(inputs[name])
        arrays[f"in_{name}_dram"] = a
        dram[name] = nc.dram_tensor(f"in_{name}_dram", a.shape, _mybir.dt.from_np(a.dtype),
                                    kind="ExternalInput").ap()
    out = nc.dram_tensor("out_dram", (N, D), _mybir.dt.float32, kind="ExternalOutput").ap()
    build(nc, dram, out)
    r = _run(nc, [arrays], core_ids=[0])
    return r.results[0]["out_dram"]
```

```python
from contextlib import ExitStack

import concourse.bass as bass
from concourse import mybir

F32 = mybir.dt.float32
F32R = mybir.dt.float32r
BF16 = mybir.dt.bfloat16
U8 = mybir.dt.uint8
ALU = mybir.AluOpType
ACT = mybir.ActivationFunctionType
AX = mybir.AxisListType

P = 128
N = 2048
D = 256
HEADS = 8
HD = 64
PAIRS = HEADS // 2
TILES = N // P
DC = D // P
BANK = 512
QUARTERS = N // BANK
CHUNKS = HEADS * QUARTERS
GAT_HEADS = 4
DX = D + GAT_HEADS
EPS = 1e-5
SCORE_SCALE = float(HD) ** -0.5
IDENTITY_BIAS = 0.01
MASK_VAL = 1e16
NEG = -1e10
ALPHA = 0.3
HUGE = 3.0e38


def ds(i, size):
    return bass.ds(i * size, size)


def wait(eng, sem, value):
    if isinstance(value, int) and value <= 0:
        return
    eng.wait_ge(sem, value)


def wait_apart(eng, sem, value, passed):
    wait(eng, sem, value)
    if not isinstance(value, int):
        eng.sem_inc(passed, 1)


def stack_queries(eng, q_hi, q_lo, q_stack, p, stacked):
    for half in range(2):
        src = slice(half * HD, (half + 1) * HD)
        for part, (low, high) in enumerate(((q_hi, q_lo), (q_lo, q_hi))):
            eng.dma_start(q_stack[0:HD, 2 * p + half, part, :].bitcast(F32), low[src, p, :].bitcast(F32))\
                .then_inc(stacked, 16)
            eng.dma_start(q_stack[HD:P, 2 * p + half, part, :].bitcast(F32), high[src, p, :].bitcast(F32))\
                .then_inc(stacked, 16)


def project_keys_values(nc, x, adj, q_hi, q_lo, q_stack, k_stack, v, w, ident, eps, mv, rstd, row_sum,
                        col_count, dram):
    with ExitStack() as ctx:
        def sb(name, shape, dt=F32):
            return ctx.enter_context(nc.sbuf_tensor(name, shape, dt))

        def sem(name):
            return ctx.enter_context(nc.semaphore(name))

        wk = sb("wk", [P, DC, HEADS * HD])
        wv = sb("wv", [P, DC, HEADS * HD])
        adj_copy = sb("a_adj_copy", [P, N], U8)
        stats = sb("a_stats", [P, TILES, 6])
        std = sb("a_std", [P, TILES])
        xc = sb("a_xc", [P, 2, D])
        hT = sb("a_hT", [P, 2, DC, BANK])
        turn_ps = [ctx.enter_context(nc.psum_tensor(f"a_turn{i}", [P, BANK], F32)) for i in range(2)]
        v_ps = [ctx.enter_context(nc.psum_tensor(f"a_v{i}", [P, BANK], F32)) for i in range(2)]
        k_ps = [ctx.enter_context(nc.psum_tensor(f"a_k{i}", [P, BANK], F32)) for i in range(PAIRS)]

        x_loaded = [sem(f"x_loaded{c}") for c in range(QUARTERS)]
        kv_weights = sem("kv_weights")
        const_loaded = sem("const_loaded")
        ident_cleared = sem("ident_cleared")
        ident_ready = sem("ident_ready")
        ln_step = sem("a_ln_step")
        stats_ready = sem("a_stats_ready")
        std_ready = sem("a_std_ready")
        rstd_ready = sem("a_rstd_ready")
        centred = sem("a_centred")
        turned = sem("a_turned")
        relu_done = sem("a_relu_done")
        v_ready = sem("v_ready")
        v_copied = sem("v_copied")
        k_ready = sem("k_ready")
        k_high = sem("k_high")
        k_split = sem("k_split")
        q0_ready = sem("q0_ready")
        q0_high = sem("q0_high")
        q0_split = sem("q0_split")
        q0_stacked = sem("q0_stacked")
        adj0_loaded = sem("adj0_loaded")
        count_cleared = sem("count_cleared")
        counted = sem("tile0_counted")
        rows_summed = sem("tile0_summed")
        mask_step = sem("a_mask_step")
        TPC = TILES // QUARTERS

        with nc.Block() as block:

            @block.sync
            def _(sp):
                x_view = dram["x"].rearrange("(t p) d -> p t d", p=P)
                for c in range(QUARTERS):
                    sp.dma_start(x[:, c * TPC:(c + 1) * TPC, :], x_view[:, c * TPC:(c + 1) * TPC, :])\
                        .then_inc(x_loaded[c], 16)
                    if c == 0:
                        for dst, name in ((wv, "L0_gnn_Wvs"), (wk, "L0_gnn_Wks")):
                            for d in range(DC):
                                sp.dma_start(dst[:, d, :].rearrange("p (h k) -> p h k", h=HEADS),
                                             dram[name][:, d * P:(d + 1) * P, :].rearrange("h p k -> p h k"))\
                                    .then_inc(kv_weights, 16)
                for d in range(DC):
                    sp.dma_start(w["q"][:, d, :].rearrange("p (h k) -> p h k", h=HEADS),
                                 dram["L0_gnn_Wqs"][:, d * P:(d + 1) * P, :].rearrange("h p k -> p h k"))\
                        .then_inc(const_loaded, 16)
                sp.dma_start(w["o"][:, :, :], dram["L0_gnn_Wo"].rearrange("(r a) k o -> (a k) r o", a=2))\
                    .then_inc(const_loaded, 16)
                sp.dma_start(adj[:, 0, :], dram["adj"][0:P, :]).then_inc(adj0_loaded, 16)
                sp.wait_ge(q0_split, 1)
                for p in range(PAIRS):
                    stack_queries(sp, q_hi, q_lo, q_stack, p, q0_stacked)
                sp.wait_ge(q0_stacked, 128 * PAIRS)

            @block.gpsimd
            def _(pool):
                nc.gpsimd.memset(ident["i"][:, :], 0.0).then_inc(ident_cleared, 1)
                nc.gpsimd.memset(ident["not"][:, :], 1.0).then_inc(ident_cleared, 1)
                nc.gpsimd.memset(ident["bias"][:, :], 0.0).then_inc(ident_cleared, 1)
                nc.gpsimd.memset(eps[:, :], EPS).then_inc(ident_cleared, 1)
                pool.wait_ge(ident_cleared, 4)
                for name, fill in (("i", 1.0), ("not", 0.0), ("bias", -IDENTITY_BIAS)):
                    nc.gpsimd.affine_select(out=ident[name][:, :], in_=ident[name][:, :],
                                            compare_op=ALU.not_equal, fill=fill, base=0,
                                            pattern=[[-1, P]], channel_multiplier=1)\
                        .then_inc(ident_ready, 1)
                pool.wait_ge(ident_ready, 3)
                nc.gpsimd.memset(col_count[:, :], 0.0).then_inc(count_cleared, 1)
                pool.wait_ge(count_cleared, 1)
                pool.wait_ge(adj0_loaded, 16)
                nc.gpsimd.tensor_tensor(col_count[:, :], adj[:, 0, :], col_count[:, :], ALU.add)\
                    .then_inc(counted, 1)
                pool.wait_ge(counted, 1)

            @block.vector
            def _(dve):
                def layer_norm(t):
                    dve.wait_ge(std_ready, t + 1)
                    nc.vector.reciprocal(rstd[:, t:t + 1], std[:, t:t + 1]).then_inc(rstd_ready, 1)
                    dve.wait_ge(rstd_ready, t + 1)
                    wait(dve, turned, t - 1)
                    nc.vector.tensor_scalar(xc[:, t % 2, :], x[:, t, :], mv[:, t, 0:1], rstd[:, t:t + 1],
                                            ALU.subtract, ALU.mult).then_inc(centred, 1)

                def statistics(t):
                    if t % TPC == 0:
                        dve.wait_ge(x_loaded[t // TPC], 16)
                    nc.vector.bn_stats(stats[:, t, :], x[:, t, :]).then_inc(ln_step, 1)
                    dve.wait_ge(ln_step, t + 1)
                    nc.vector.bn_aggr(mv[:, t, :], stats[:, t, :]).then_inc(stats_ready, 1)

                def split_keys(n):
                    c, p = divmod(n, PAIRS)
                    cols = slice(c * BANK, (c + 1) * BANK)
                    for half in range(2):
                        own = slice(half * HD, (half + 1) * HD)
                        other = slice((1 - half) * HD, (2 - half) * HD)
                        dve.wait_ge(k_high, 2 * n + half + 1)
                        nc.vector.tensor_tensor(k_stack[other, 2 * p + half, cols], k_ps[p][own, :],
                                                k_stack[own, 2 * p + half, cols].bitcast(F32), ALU.subtract)\
                            .then_inc(k_split, 1)

                statistics(0)
                statistics(1)
                for t in range(TPC + 1):
                    statistics(t + 2)
                    layer_norm(t)
                for n in range(TILES):
                    if n + TPC + 3 < TILES:
                        statistics(n + TPC + 3)
                    if n + TPC + 1 < TILES:
                        layer_norm(n + TPC + 1)
                    split_keys(n)
                    if n == PAIRS - 1:
                        dve.wait_ge(q0_high, 1)
                        nc.vector.scalar_tensor_tensor(
                            out=q_lo[:, :, :], in0=v_ps[1][:, :].rearrange("p (a n) -> p a n", a=PAIRS),
                            scalar=-SCORE_SCALE, in1=q_hi[:, :, :].bitcast(F32),
                            op0=ALU.mult, op1=ALU.subtract).then_inc(q0_split, 1)
                dve.wait_ge(counted, 1)
                dve.wait_ge(rows_summed, 1)
                for half in range(2):
                    mask_half(nc, adj[:, 0, :], half, mask_step)
                mask_own(nc, dve, adj[:, 0, 0:P], ident, mask_step, 0)
                dve.wait_ge(k_split, 2 * TILES)

            @block.scalar
            def _(act):
                def relu(t):
                    act.wait_ge(turned, t + 1)
                    c = t // TPC
                    wait(act, k_ready, PAIRS * (c - 1))
                    nc.scalar.activation(hT[:, c % 2, :, (t % TPC) * P:(t % TPC + 1) * P],
                                         turn_ps[t % 2][:, 0:D].rearrange("p (c n) -> p c n", c=DC),
                                         ACT.Relu).then_inc(relu_done, 1)

                def deviation(t):
                    act.wait_ge(stats_ready, t + 1)
                    nc.scalar.activation(std[:, t:t + 1], mv[:, t, 1:2], ACT.Sqrt, bias=eps[:, :])\
                        .then_inc(std_ready, 1)

                def copy_out(n):
                    act.wait_ge(v_ready, n + 1)
                    nc.scalar.activation(v[:, n, :], v_ps[n % 2][:, :], ACT.Copy).then_inc(v_copied, 1)
                    c, p = divmod(n, PAIRS)
                    act.wait_ge(k_ready, n + 1)
                    for half in range(2):
                        own = slice(half * HD, (half + 1) * HD)
                        nc.scalar.activation(k_stack[own, 2 * p + half, c * BANK:(c + 1) * BANK], k_ps[p][own, :],
                                             ACT.Copy).then_inc(k_high, 1)

                act.wait_ge(ident_cleared, 4)
                deviation(0)
                deviation(1)
                for t in range(TPC):
                    deviation(t + 2)
                    relu(t)
                deviation(TPC + 2)
                for n in range(TILES):
                    if n + TPC + 3 < TILES:
                        deviation(n + TPC + 3)
                    if n + TPC < TILES:
                        relu(n + TPC)
                    copy_out(n)
                    if n == PAIRS - 1:
                        act.wait_ge(q0_ready, 1)
                        nc.scalar.activation(q_hi[:, :, :], v_ps[1][:, :].rearrange("p (a n) -> p a n", a=PAIRS),
                                             ACT.Copy, scale=-SCORE_SCALE).then_inc(q0_high, 1)
                    if n == 2 * PAIRS:
                        act.wait_ge(adj0_loaded, 16)
                        nc.scalar.activation(adj_copy[:, :], adj[:, 0, :], ACT.Copy, accum_out=row_sum[:, 0:1])\
                            .then_inc(rows_summed, 1)
                act.wait_ge(v_copied, TILES)

            @block.tensor
            def _(pe):
                def turn(t):
                    pe.wait_ge(centred, t + 1)
                    wait(pe, relu_done, t - 1)
                    for d in range(DC):
                        last = nc.tensor.transpose(turn_ps[t % 2][:, d * P:(d + 1) * P],
                                                   xc[:, t % 2, d * P:(d + 1) * P], ident["i"][:, :])
                    last.then_inc(turned, 1)

                pe.wait_ge(ident_ready, 3)
                for t in range(TPC):
                    turn(t)
                pe.wait_ge(kv_weights, 16 * 2 * DC)
                for n in range(TILES):
                    c, p = divmod(n, PAIRS)
                    if n + TPC < TILES:
                        turn(n + TPC)
                    pe.wait_ge(relu_done, n + 1)
                    wait(pe, v_copied, n - 1)
                    if n == PAIRS + 1:
                        pe.wait_ge(q0_split, 1)
                    for d in range(DC):
                        last = nc.tensor.matmul(v_ps[n % 2][:, :], hT[:, c % 2, d, p * P:(p + 1) * P],
                                                wv[:, d, :], start=(d == 0), stop=(d == DC - 1))
                    last.then_inc(v_ready, 1)
                    pe.wait_ge(relu_done, (c + 1) * TPC)
                    wait(pe, k_split, 2 * (n - PAIRS + 1))
                    for d in range(DC):
                        last = nc.tensor.matmul(k_ps[p][:, :], wk[:, d, p * P:(p + 1) * P],
                                                hT[:, c % 2, d, :], start=(d == 0), stop=(d == DC - 1))
                    last.then_inc(k_ready, 1)
                    if n == PAIRS - 1:
                        pe.wait_ge(const_loaded, 16 * (DC + 1))
                        pe.wait_ge(v_copied, PAIRS)
                        for a in range(PAIRS):
                            for d in range(DC):
                                last = nc.tensor.matmul(v_ps[1][:, a * P:(a + 1) * P],
                                                        w["q"][:, d, a * P:(a + 1) * P], hT[:, 0, d, 0:P],
                                                        start=(d == 0), stop=(d == DC - 1))
                        last.then_inc(q0_ready, 1)


def mask_half(nc, adj, half, mask_step):
    cols = adj[:, half * N // 2:(half + 1) * N // 2]
    nc.vector.tensor_scalar(cols, cols, -MASK_VAL, MASK_VAL, ALU.mult, ALU.add).then_inc(mask_step, 1)


def mask_own(nc, dve, own, ident, mask_step, done):
    dve.wait_ge(mask_step, done + 2)
    nc.vector.tensor_tensor(own, own, ident["not"][:, :], ALU.mult).then_inc(mask_step, 1)
    dve.wait_ge(mask_step, done + 3)
    nc.vector.tensor_tensor(own, own, ident["bias"][:, :], ALU.add).then_inc(mask_step, 1)
    dve.wait_ge(mask_step, done + 4)


def attend(nc, x, mask, q_hi, q_lo, q_stack, k_stack, v, w, ident, mv, rstd, row_sum, col_count,
           w1, bias1, dram):
    with ExitStack() as ctx:
        def sb(name, shape, dt=F32):
            return ctx.enter_context(nc.sbuf_tensor(name, shape, dt))

        def sem(name):
            return ctx.enter_context(nc.semaphore(name))

        def ps(name):
            return ctx.enter_context(nc.psum_tensor(name, [P, BANK], F32))

        probs = sb("probs", [P, 4, N])
        probs_T = sb("probs_T", [P, 2, 2, BANK])
        xc = sb("b_xc", [P, D])
        hT = sb("b_hT", [P, DC, P])
        chunk_min = sb("chunk_min", [P, 2, QUARTERS])
        head_min = sb("head_min", [P, HEADS])
        adj_copy = sb("adj_copy", [P, N], U8)
        prob_sum = sb("prob_sum", [P, HEADS])
        inv_sum = sb("inv_sum", [P, 2])
        inv_cols = sb("inv_cols", [P, 2, HD])
        inv_rows = sb("inv_rows", [P, 2, P])
        heads_T = sb("heads_T", [P, PAIRS, P])
        S = [ps(f"scores{i}") for i in range(3)]
        T = [ps(f"turn{i}") for i in range(2)]
        O = [ps(f"heads{i}") for i in range(2)]
        M = ps("misc")

        adj_loaded = sem("adj_loaded")
        sp_passed = sem("b_sp_passed")
        dve_passed = sem("b_dve_passed")
        mask_step = sem("mask_step")
        next_loaded = sem("next_loaded")
        counted = sem("counted")
        rows_summed = sem("rows_summed")
        centred = sem("b_centred")
        x_turned = sem("b_x_turned")
        relu_done = sem("b_relu_done")
        q_ready = sem("q_ready")
        q_high = sem("q_high")
        q_split = sem("q_split")
        q_stacked = [sem(f"q_stacked{p}") for p in range(PAIRS)]
        scores_ready = sem("scores_ready")
        scores_read = sem("scores_read")
        head_masked = sem("head_masked")
        probs_ready = sem("probs_ready")
        turned = [sem("even_turned"), sem("odd_turned")]
        copied = [sem("even_copied"), sem("odd_copied")]
        quarter_used = sem("quarter_used")
        inv_known = sem("inv_known")
        inv_ready = sem("inv_ready")
        inv_turned = sem("inv_turned")
        inv_copied = sem("inv_copied")
        pair_normed = sem("pair_normed")
        out_ready = sem("out_ready")
        x_added = sem("x_added")

        def chunk_bank(j):
            return S[j % 3]

        def over_tiles(eng, body):
            body(0, 0, False, True, True)
            with eng.Fori(0, TILES // 2 - 1) as i:
                for s in (1, 0):
                    body(2 * i + (2 - s), s, True, True, True)
            body(TILES - 1, 1, True, True, False)
            body(TILES, 0, True, False, False)

        with nc.Block() as block:

            @block.sync
            def _(sp):
                adj_rows = dram["adj"].rearrange("(t p) n -> t p n", p=P)

                def body(t, s, has_prev, has_cur, has_next):
                    if has_next:
                        wait_apart(sp, scores_read, CHUNKS * t, sp_passed)
                        sp.dma_start(mask[:, 1 - s, :], adj_rows[ds(t + 1, 1), :, :].rearrange("a p n -> (a p) n"))\
                            .then_inc(adj_loaded, 16)
                        for p in range(PAIRS):
                            wait_apart(sp, q_split, t + 1, sp_passed)
                            wait_apart(sp, scores_ready, CHUNKS * t + 2 * QUARTERS * (p + 1), sp_passed)
                            stack_queries(sp, q_hi, q_lo, q_stack, p, q_stacked[p])

                over_tiles(sp, body)
                sp.dma_start(w1[:, :, :], dram["L1_gnn_W"].rearrange("(c p) o -> p c o", p=P))\
                    .then_inc(next_loaded, 16)
                sp.dma_start(bias1[:, :], dram["L1_gnn_b"].rearrange("(a n) -> a n", a=1).broadcast_to([P, D]))\
                    .then_inc(next_loaded, 16)
                for n in range(2):
                    sp.wait_ge(scores_read, CHUNKS * (TILES - 1 + n))
                    sp.dma_start(mask[:, n, :], adj_rows[n, :, :]).then_inc(next_loaded, 16)
                sp.wait_ge(next_loaded, 16 * 4)

            @block.gpsimd
            def _(pool):
                def body(t, s, has_prev, has_cur, has_next):
                    if has_next:
                        pool.wait_ge(adj_loaded, 16 * (t + 1))
                        wait(pool, counted, t)
                        nc.gpsimd.tensor_tensor(col_count[:, :], mask[:, 1 - s, :], col_count[:, :], ALU.add)\
                            .then_inc(counted, 1)

                over_tiles(pool, body)
                pool.wait_ge(counted, TILES - 1)

            @block.vector
            def _(dve):
                def layer_norm(n):
                    own = x[:, ds(n, 1), :].rearrange("p a d -> p (a d)")
                    wait(dve, x_turned, n - 1)
                    nc.vector.tensor_scalar(xc[:, :], own, mv[:, ds(n, 1), 0], rstd[:, ds(n, 1)],
                                            ALU.subtract, ALU.mult).then_inc(centred, 1)

                def split_queries(n):
                    dve.wait_ge(q_high, n)
                    nc.vector.scalar_tensor_tensor(
                        out=q_lo[:, :, :], in0=M[:, :].rearrange("p (a n) -> p a n", a=PAIRS),
                        scalar=-SCORE_SCALE, in1=q_hi[:, :, :].bitcast(F32),
                        op0=ALU.mult, op1=ALU.subtract).then_inc(q_split, 1)

                def mask_scores(t, s, pair, j):
                    half, c = divmod(j, QUARTERS)
                    h = 2 * pair + half
                    i = h * QUARTERS + c
                    wait_apart(dve, scores_ready, CHUNKS * t + i + 1, dve_passed)
                    if c == 0:
                        wait_apart(dve, turned[half], QUARTERS * PAIRS * t + QUARTERS * (pair - 1), dve_passed)
                    nc.vector.tensor_tensor_reduce(
                        probs[:, h % 4, c * BANK:(c + 1) * BANK], chunk_bank(i)[:, :],
                        mask[:, s, c * BANK:(c + 1) * BANK], 1.0, HUGE, ALU.add, ALU.min,
                        chunk_min[:, half, c:c + 1]).then_inc(scores_read, 1)
                    if c == QUARTERS - 1:
                        dve.wait_ge(scores_read, CHUNKS * t + i + 1)
                        nc.vector.tensor_reduce(head_min[:, h:h + 1], chunk_min[:, half, :], AX.X, ALU.min)\
                            .then_inc(head_masked, 1)

                def body(t, s, has_prev, has_cur, has_next):
                    for pair in range(PAIRS):
                        g = PAIRS * t + pair
                        for k in range(QUARTERS):
                            if has_cur:
                                mask_scores(t, s, pair, 2 * k)
                                mask_scores(t, s, pair, 2 * k + 1)
                            if has_next and pair == 2 and k == 1:
                                split_queries(t + 1)
                            turn_prev = (has_cur or pair == 0) and (has_prev or pair >= 1)
                            if turn_prev:
                                q = QUARTERS * (g - 1) + k
                                dve.wait_ge(turned[1], q + 1)
                                wait(dve, quarter_used, q - 1)
                                nc.vector.tensor_copy(probs_T[:, k % 2, 1, :], T[1][:, :])\
                                    .then_inc(copied[1], 1)
                            if turn_prev and k == 0:
                                prev = (pair - 1) % PAIRS
                                dve.wait_ge(probs_ready, 2 * g)
                                wait(dve, inv_turned, g - 1)
                                nc.vector.reciprocal(inv_sum[:, :], prob_sum[:, 2 * prev:2 * prev + 2])\
                                    .then_inc(inv_known, 1)
                                dve.wait_ge(inv_known, g)
                                nc.vector.tensor_copy(inv_cols[:, :, :],
                                                      inv_sum[:, :].unsqueeze(2).to_broadcast([P, 2, HD]))\
                                    .then_inc(inv_ready, 1)
                            norm_prev = (has_cur or pair <= 1) and (has_prev or pair >= 2)
                            if norm_prev and k == 1:
                                prev = (pair - 2) % PAIRS
                                dve.wait_ge(quarter_used, QUARTERS * (g - 1))
                                dve.wait_ge(inv_copied, g - 1)
                                nc.vector.tensor_tensor(heads_T[:, prev, :], O[pair % 2][:, 0:P],
                                                        inv_rows[:, pair % 2, :], ALU.mult)\
                                    .then_inc(pair_normed, 1)
                            if has_next and pair == 1 and k == 2:
                                layer_norm(t + 1)
                            if has_prev and pair == 1 and k == 3:
                                dve.wait_ge(out_ready, t)
                                own = x[:, ds(t - 1, 1), :].rearrange("p a d -> p (a d)")
                                nc.vector.tensor_tensor(own, M[:, 0:D], own, ALU.add).then_inc(x_added, 1)
                            if has_next and pair == 2 and k == 2:
                                dve.wait_ge(counted, t + 1)
                                dve.wait_ge(rows_summed, t + 1)
                                mask_half(nc, mask[:, 1 - s, :], 0, mask_step)
                            if has_next and pair == 2 and k == 3:
                                mask_half(nc, mask[:, 1 - s, :], 1, mask_step)
                            if has_next and pair == 3 and k == 2:
                                mask_own(nc, dve, mask[:, 1 - s, ds(t + 1, P)], ident, mask_step, 4 * t)

                over_tiles(dve, body)
                dve.wait_ge(x_added, TILES)

            @block.scalar
            def _(act):
                def relu(n):
                    act.wait_ge(x_turned, n)
                    wait(act, q_ready, n - 1)
                    nc.scalar.activation(hT[:, :, :], M[:, 0:D].rearrange("p (c n) -> p c n", c=DC),
                                         ACT.Relu).then_inc(relu_done, 1)

                def round_queries(n):
                    act.wait_ge(q_ready, n)
                    for p in range(PAIRS):
                        wait(act, q_stacked[p], 128 * (n - 1))
                    nc.scalar.activation(q_hi[:, :, :], M[:, :].rearrange("p (a n) -> p a n", a=PAIRS),
                                         ACT.Copy, scale=-SCORE_SCALE).then_inc(q_high, 1)

                def sum_rows(n, s):
                    act.wait_ge(adj_loaded, 16 * n)
                    wait(act, rows_summed, n - 1)
                    nc.scalar.activation(adj_copy[:, :], mask[:, s, :], ACT.Copy,
                                         accum_out=row_sum[:, ds(n, 1)]).then_inc(rows_summed, 1)

                def body(t, s, has_prev, has_cur, has_next):
                    for pair in range(PAIRS):
                        g = PAIRS * t + pair
                        for k in range(QUARTERS):
                            if has_next and pair == 2 and k == 0:
                                relu(t + 1)
                            if has_next and pair == 2 and k == 1:
                                round_queries(t + 1)
                            turn_prev = (has_cur or pair == 0) and (has_prev or pair >= 1)
                            if turn_prev:
                                q = QUARTERS * (g - 1) + k
                                act.wait_ge(turned[0], q + 1)
                                wait(act, quarter_used, q - 1)
                                nc.scalar.activation(probs_T[:, k % 2, 0, :], T[0][:, :], ACT.Copy)\
                                    .then_inc(copied[0], 1)
                            if turn_prev and k == 1:
                                act.wait_ge(inv_turned, g)
                                wait(act, pair_normed, g - 2)
                                nc.scalar.activation(inv_rows[:, (pair - 1) % 2, :], M[:, 0:P], ACT.Copy)\
                                    .then_inc(inv_copied, 1)
                            if has_next and pair == 1 and k == 2:
                                sum_rows(t + 1, 1 - s)
                            if has_cur and k % 2 == 1:
                                h = 2 * pair + k // 2
                                act.wait_ge(head_masked, HEADS * t + h + 1)
                                nc.scalar.activation(probs[:, h % 4, :], probs[:, h % 4, :], ACT.Exp,
                                                     bias=head_min[:, h:h + 1], scale=-1.0,
                                                     accum_out=prob_sum[:, h:h + 1]).then_inc(probs_ready, 1)

                over_tiles(act, body)

            @block.tensor
            def _(pe):
                def turn_x(n):
                    pe.wait_ge(centred, n)
                    for d in range(DC):
                        last = nc.tensor.transpose(M[:, d * P:(d + 1) * P], xc[:, d * P:(d + 1) * P],
                                                   ident["i"][:, :])
                    last.then_inc(x_turned, 1)

                def project_queries(n):
                    pe.wait_ge(relu_done, n)
                    for p in range(PAIRS):
                        for d in range(DC):
                            last = nc.tensor.matmul(M[:, p * P:(p + 1) * P], w["q"][:, d, p * P:(p + 1) * P],
                                                    hT[:, d, :], start=(d == 0), stop=(d == DC - 1))
                    last.then_inc(q_ready, 1)

                def scores(t, pair, j):
                    half, c = divmod(j, QUARTERS)
                    h = 2 * pair + half
                    i = h * QUARTERS + c
                    if j == 0:
                        wait(pe, q_stacked[pair], 128 * t)
                    if i >= 3:
                        pe.wait_ge(scores_read, CHUNKS * t + i - 2)
                    else:
                        wait(pe, scores_read, CHUNKS * t - (1, 0, 2)[i])
                    keys = k_stack[:, h, c * BANK:(c + 1) * BANK]
                    for part in range(2):
                        last = nc.tensor.matmul(chunk_bank(i)[:, :], q_stack[:, h, part, :], keys,
                                                start=(part == 0), stop=(part == 1))
                    last.then_inc(scores_ready, 1)

                def turn_probs(pair, g, k):
                    for half in range(2):
                        slot = (2 * pair + half) % 4
                        if k == 0:
                            pe.wait_ge(probs_ready, 2 * g + half + 1)
                        wait(pe, copied[half], QUARTERS * g + k)
                        for b in range(BANK // P):
                            m = k * (BANK // P) + b
                            last = nc.tensor.transpose(T[half][:, b * P:(b + 1) * P],
                                                       probs[:, slot, m * P:(m + 1) * P], ident["i"][:, :])
                        last.then_inc(turned[half], 1)

                def weigh_values(pair, g, k):
                    for half in range(2):
                        pe.wait_ge(copied[half], QUARTERS * g + k + 1)
                    if k == 0:
                        wait(pe, pair_normed, g - 1)
                    for b in range(BANK // P):
                        m = k * (BANK // P) + b
                        for half in range(2):
                            h = 2 * pair + half
                            last = nc.tensor.matmul(O[pair % 2][half * HD:(half + 1) * HD, 0:P],
                                                    v[:, m, h * HD:(h + 1) * HD],
                                                    probs_T[:, k % 2, half, b * P:(b + 1) * P],
                                                    start=(m == 0), stop=(m == TILES - 1))
                    last.then_inc(quarter_used, 1)

                def body(t, s, has_prev, has_cur, has_next):
                    for pair in range(PAIRS):
                        g = PAIRS * t + pair
                        turn_prev = (has_cur or pair == 0) and (has_prev or pair >= 1)
                        last_prev = (has_cur or pair <= 1) and (has_prev or pair >= 2)
                        for k in range(QUARTERS):
                            if has_cur:
                                scores(t, pair, 2 * k)
                                scores(t, pair, 2 * k + 1)
                            if k == 0 and pair == 2 and has_next:
                                wait(pe, x_added, t)
                                pe.wait_ge(inv_copied, g - 1)
                                turn_x(t + 1)
                            if k == 0 and last_prev:
                                weigh_values((pair - 2) % PAIRS, g - 2, QUARTERS - 1)
                            if turn_prev:
                                turn_probs((pair - 1) % PAIRS, g - 1, k)
                            if k >= 1 and turn_prev:
                                weigh_values((pair - 1) % PAIRS, g - 1, k - 1)
                            if k == 1 and turn_prev:
                                pe.wait_ge(inv_ready, g)
                                wait(pe, inv_copied, g - 1)
                                if pair == 2 and has_next:
                                    pe.wait_ge(q_split, t + 1)
                                elif pair == 2:
                                    pe.wait_ge(x_added, t)
                                nc.tensor.transpose(M[:, 0:P], inv_cols[:, :, :].rearrange("p a n -> p (a n)"),
                                                    ident["i"][:, :]).then_inc(inv_turned, 1)
                            if k == 2 and pair == 1 and has_prev:
                                pe.wait_ge(pair_normed, g - 1)
                                wait(pe, inv_copied, g if has_cur else g - 1)
                                for p in range(PAIRS):
                                    last = nc.tensor.matmul(M[:, 0:D], heads_T[:, p, :], w["o"][:, p, :],
                                                            start=(p == 0), stop=(p == PAIRS - 1))
                                last.then_inc(out_ready, 1)
                            if k == 0 and pair == 2 and has_next:
                                project_queries(t + 1)

                over_tiles(pe, body)


def graph_layers(nc, x, adj, ident, eps, row_sum, col_count, w1, bias1, dram, out):
    with ExitStack() as ctx:
        def sb(name, shape, dt=F32):
            return ctx.enter_context(nc.sbuf_tensor(name, shape, dt))

        def sem(name):
            return ctx.enter_context(nc.semaphore(name))

        def ps(name):
            return ctx.enter_context(nc.psum_tensor(name, [P, BANK], F32))

        adj_T = sb("adj_T", [P, TILES, N], U8)
        block_T = sb("block_T", [P, 2, N], F32R)
        parts = [sb(f"parts{i}", [P, TILES, 2, D], F32R) for i in range(2)]
        xc = sb("c_xc", [P, 2, D])
        hT = sb("c_hT", [P, 2, DC, P])
        y = sb("y", [P, 2, DX])
        yr = sb("yr", [P, D])
        stats = sb("c_stats", [P, 6])
        mv = sb("c_mv", [P, 2, 2])
        std = sb("c_std", [P, 2])
        rstd = sb("c_rstd", [P, 2])
        deg1 = sb("deg1", [P, TILES])
        w2 = sb("w2", [P, DC, D])
        w3 = sb("w3", [P, DC, DX])
        bias = sb("bias", [P, 2, DX])
        gat_k = sb("gat_k", [P, DC, GAT_HEADS, D])
        ones = sb("ones", [P, P])
        ident_r = sb("ident_r", [P, P], F32R)
        ones_b = sb("ones_b", [P, 1], BF16)
        in_deg_inv = sb("in_deg_inv", [P, TILES])
        r = sb("r", [P, TILES])
        r_any = sb("r_any", [P, TILES])
        scores = sb("gat_scores", [P, TILES, GAT_HEADS])
        w_adj = sb("w_adj", [P, TILES, GAT_HEADS])
        w_all = sb("w_all", [P, TILES, GAT_HEADS])
        g_tmp = sb("g_tmp", [P, 4, TILES, GAT_HEADS])
        y_sum = sb("y_sum", [P, D])
        all_sum_T = sb("all_sum_T", [P, DC, P])
        all_k = sb("all_k", [P, GAT_HEADS, D])
        u = sb("u", [P, 2, D])
        acc = sb("acc", [P, 2, D])
        w2a = sb("w2a", [P, D])
        w2b = sb("w2b", [P, DC, P])
        w2b_T = sb("w2b_T", [P, D])
        wn_T = sb("wn_T", [P, DC, D])
        a_bc = sb("a_bc", [P, 2, GAT_HEADS, D])
        va = sb("va", [P, DC, GAT_HEADS])
        k_a = [all_k[:, :, :], a_bc[:, 1, :, :]]
        b_col = sb("b_col", [P, 1 + DC])
        b_bc = sb("b_bc", [P, 1 + DC, P])

        turn_ps = [ps("c_turn0"), ps("c_turn1")]
        sum_ps = [ps("sum0"), ps("sum1")]
        small_ps = ps("small")
        dense_ps = [ps("dense0"), ps("dense1")]
        z_ps = [[dense_ps[0], dense_ps[1]], [turn_ps[1], ps("z3")]]

        adj_banks = [sum_ps[0], sum_ps[1], turn_ps[1], z_ps[1][1]]

        w2_loaded = sem("w2_loaded")
        w3_loaded = sem("w3_loaded")
        sp_passed = sem("c_sp_passed")
        dve_passed = sem("c_dve_passed")
        adj_in = [[sem(f"adj_in{s}_half{half}") for half in range(2)] for s in range(2)]
        prep_pool = sem("prep_pool")
        prep_dve = sem("prep_dve")
        prep_pe = sem("prep_pe")
        prep_act = sem("prep_act")
        ln_step = sem("c_ln_step")
        stats_ready = sem("c_stats_ready")
        std_ready = sem("c_std_ready")
        rstd_ready = sem("c_rstd_ready")
        deg_ready = sem("deg_ready")
        deg_root = sem("deg_root")
        x_step = sem("x_step")
        centred = sem("c_centred")
        x_turned = sem("c_x_turned")
        h_ready = sem("h_ready")
        dense_ready = sem("dense_ready")
        y_step = sem("y_step")
        y_split = sem("y_split")
        y_summed = sem("y_summed")
        adj_turned = sem("adj_turned")
        adj_kept = sem("adj_kept")
        block_ready = sem("block_ready")
        sums_ready = sem("sums_ready")
        gat_step = sem("gat_step")
        gat_exp = sem("gat_exp")
        z_ready = sem("z_ready")
        z_step = sem("z_step")
        out_ready = sem("tile_out_ready")
        out_stored = [sem("out_stored0"), sem("out_stored1")]

        QB = BANK // P
        W2_LOADS = 5
        W3_LOADS = 2 * DC + 3
        YS = 3
        XS = 2

        def one(ap):
            return ap.rearrange("p a d -> p (a d)")

        def over_ticks(eng, tick, first=2, lead=0):
            def peeled(t):
                tick(t, t % 2, lambda lag: 0 <= t - lag < TILES)
            for t in range(first):
                peeled(t)
            with eng.Fori(first // 2, TILES // 2 - lead) as i:
                for s in range(2):
                    tick(2 * i + s, s, lambda lag: True)
            for t in range(TILES - 2 * lead, TILES + 2):
                peeled(t)

        with nc.Block() as block:

            @block.sync
            def _(sp):
                adj_rows = dram["adj"].rearrange("(t p) n -> t p n", p=P)

                def flat_bc(ap, n):
                    return ap.rearrange("(a n) -> a n", a=1).broadcast_to([P, n])

                def next_adj(t, s):
                    for half in range(2):
                        cols = slice(half * N // 2, (half + 1) * N // 2)
                        wait_apart(sp, adj_turned, QUARTERS * (t - 2) + 2 * (half + 1), sp_passed)
                        sp.dma_start(adj[:, s, cols], adj_rows[ds(t, 1), :, cols].rearrange("a p n -> (a p) n"))\
                            .then_inc(adj_in[s][half], 16)

                sp.dma_start(w2b[:, :, :], dram["L2_gnn_W2"].rearrange("(c p) m -> p c m", p=P))\
                    .then_inc(w2_loaded, 16)
                sp.dma_start(w2a[:, :], dram["L2_gnn_W1"]).then_inc(w2_loaded, 16)
                sp.dma_start(b_col[:, 0:1], dram["L2_gnn_b1"].rearrange("(p a) -> p a", a=1)).then_inc(w2_loaded, 16)
                sp.dma_start(bias[:, 0, 0:D], flat_bc(dram["L2_gnn_b2"], D)).then_inc(w2_loaded, 16)
                sp.dma_start(w3[:, :, 0:D], dram["L3_gnn_W_node"].rearrange("(c p) o -> p c o", p=P))\
                    .then_inc(w2_loaded, 16)
                next_adj(2, 0)
                next_adj(3, 1)
                for c in range(DC):
                    sp.dma_start(gat_k[:, c, :, :],
                                 dram["L3_gnn_K"][:, c * P:(c + 1) * P, :].rearrange("h p f -> p h f"))\
                        .then_inc(w3_loaded, 16)
                next_adj(4, 0)
                next_adj(5, 1)
                for i, name in enumerate(("L3_gnn_A_self", "L3_gnn_A_neigh")):
                    sp.dma_start(a_bc[:, i, :, :].rearrange("p h f -> p (h f)"),
                                 flat_bc(dram[name].rearrange("h f -> (h f)"), GAT_HEADS * D)).then_inc(w3_loaded, 16)
                for c in range(DC):
                    sp.dma_start(b_col[:, 1 + c:2 + c],
                                 dram["L3_gnn_b_node"][c * P:(c + 1) * P].rearrange("(p a) -> p a", a=1))\
                        .then_inc(w3_loaded, 16)
                sp.dma_start(bias[:, 1, 0:D], flat_bc(dram["L3_gnn_b_node"], D)).then_inc(w3_loaded, 16)
                with sp.Fori(3, TILES // 2) as i:
                    for s in range(2):
                        next_adj(2 * i + s, s)
                out_rows = out.rearrange("(t p) d -> t p d", p=P)

                def store(t, s):
                    wait_apart(sp, out_ready, t + 1, sp_passed)
                    sp.dma_start(out_rows[ds(t, 1), :, :].rearrange("a p d -> (a p) d"), acc[:, s, :])\
                        .then_inc(out_stored[s], 16)

                with sp.Fori(0, TILES // 2) as i:
                    for s in range(2):
                        store(2 * i + s, s)
                for s in range(2):
                    wait_apart(sp, out_stored[s], 16 * TILES // 2, sp_passed)

            @block.gpsimd
            def _(pool):
                nc.gpsimd.memset(ones[:, :], 1.0).then_inc(prep_pool, 1)
                nc.gpsimd.memset(ones_b[:, :], 1.0).then_inc(prep_pool, 1)
                nc.gpsimd.memset(y_sum[:, :], 0.0).then_inc(prep_pool, 1)
                pool.wait_ge(prep_pool, 3)
                pool.wait_ge(w2_loaded, 16 * W2_LOADS)
                nc.gpsimd.tensor_tensor(b_bc[:, 0, :], ones[:, :], b_col[:, 0:1].to_broadcast([P, P]), ALU.mult)\
                    .then_inc(prep_pool, 1)
                pool.wait_ge(w3_loaded, 16 * W3_LOADS)
                nc.gpsimd.tensor_tensor(a_bc[:, 0, :, :], a_bc[:, 0, :, :], a_bc[:, 1, :, :], ALU.add)\
                    .then_inc(prep_pool, 1)
                pool.wait_ge(prep_pool, 5)
                for c in range(DC):
                    nc.gpsimd.tensor_tensor(k_a[c], gat_k[:, c, :, :], a_bc[:, 0, :, :], ALU.mult)\
                        .then_inc(prep_pool, 1)
                for c in range(DC):
                    nc.gpsimd.tensor_tensor(b_bc[:, 1 + c, :], ones[:, :],
                                            b_col[:, 1 + c:2 + c].to_broadcast([P, P]), ALU.mult)\
                        .then_inc(prep_pool, 1)
                pool.wait_ge(prep_pool, 5 + 2 * DC)

                def add_y(t, s):
                    pool.wait_ge(y_step, YS * (2 * TILES + t) + 1)
                    wait(pool, y_summed, t)
                    nc.gpsimd.tensor_tensor(y_sum[:, :], y[:, s, 0:D], y_sum[:, :], ALU.add)\
                        .then_inc(y_summed, 1)

                add_y(0, 0)
                add_y(1, 1)
                with pool.Fori(1, TILES // 2) as i:
                    for s in range(2):
                        add_y(2 * i + s, s)

            @block.vector
            def _(dve):
                def statistics(n, t, s):
                    nc.vector.bn_stats(stats[:, :], one(x[:, ds(t, 1), :])).then_inc(ln_step, 1)
                    wait_apart(dve, ln_step, n + 1, dve_passed)
                    nc.vector.bn_aggr(mv[:, s, :], stats[:, :]).then_inc(stats_ready, 1)

                def center(n, t, s):
                    own = one(x[:, ds(t, 1), :])
                    dve.wait_ge(std_ready, n + 1)
                    nc.vector.reciprocal(rstd[:, s:s + 1], std[:, s:s + 1]).then_inc(rstd_ready, 1)
                    dve.wait_ge(rstd_ready, n + 1)
                    wait(dve, x_turned, n - 1)
                    nc.vector.tensor_scalar(xc[:, s, :], own, mv[:, s, 0:1], rstd[:, s:s + 1],
                                            ALU.subtract, ALU.mult).then_inc(centred, 1)

                def finish_y(layer, t, s):
                    n = (layer - 1) * TILES + t
                    width = DX if layer == 3 else D
                    dve.wait_ge(dense_ready, n + 1)
                    if layer == 3:
                        wait(dve, y_summed, t - 1)
                    nc.vector.tensor_tensor(y[:, s, 0:width], dense_ps[s][:, 0:width],
                                            bias1[:, :] if layer == 1 else bias[:, layer - 2, 0:width], ALU.add).then_inc(y_step, 1)
                    dve.wait_ge(y_step, YS * n + 1)
                    if layer == 2:
                        nc.vector.tensor_scalar(yr[:, :], y[:, s, 0:D], r[:, ds(t, 1)], None, ALU.mult)\
                            .then_inc(y_step, 1)
                        full = yr[:, :]
                    elif layer == 3:
                        nc.vector.tensor_copy(one(scores[:, ds(t, 1), :]), y[:, s, D:DX]).then_inc(y_step, 1)
                        full = y[:, s, 0:D]
                    else:
                        dve.sem_inc(y_step, 1)
                        full = y[:, s, 0:D]
                    dve.wait_ge(y_step, YS * n + 2)
                    to = parts[layer % 2]
                    hi = to[:, ds(t, 1), 0, :].rearrange("p a d -> p (a d)")
                    lo = to[:, ds(t, 1), 1, :].rearrange("p a d -> p (a d)")
                    nc.vector.tensor_copy(hi, full).then_inc(y_step, 1)
                    dve.wait_ge(y_step, YS * n + 3)
                    nc.vector.tensor_tensor(lo, full, hi.bitcast(F32), ALU.subtract).then_inc(y_split, 1)

                nc.vector.tensor_copy(ident_r[:, :], ident["i"][:, :]).then_inc(prep_dve, 1)
                nc.vector.tensor_scalar(deg1[:, :], row_sum[:, :], 1.0, 1.0 / HUGE, ALU.add, ALU.max)\
                    .then_inc(deg_ready, 1)

                def first_tick(t, s, live):
                    if isinstance(t, int) and t == 4:
                        dve.wait_ge(prep_pe, 3)
                        nc.vector.tensor_tensor(bias[:, 0, 0:D], small_ps[:, D:2 * D], bias[:, 0, 0:D], ALU.add)\
                            .then_inc(prep_dve, 1)
                    if isinstance(t, int) and t == TILES - 2:
                        dve.wait_ge(prep_pool, 5 + DC)
                        for c in range(DC):
                            nc.vector.tensor_reduce(va[:, c, :], k_a[c], AX.X, ALU.add).then_inc(prep_dve, 1)
                    if live(0):
                        center(t, t, s)
                    if live(-1):
                        statistics(t + 1, t + 1, 1 - s)
                    if live(2):
                        finish_y(1, t - 2, s)
                    if not isinstance(t, int):
                        return
                    if t == 0:
                        dve.wait_ge(deg_root, 1)
                        nc.vector.reciprocal(deg1[:, :], r_any[:, :]).then_inc(deg_ready, 1)
                        dve.wait_ge(deg_ready, 2)
                        nc.vector.scalar_tensor_tensor(out=r[:, :], in0=row_sum[:, :], scalar=-1.0, in1=deg1[:, :],
                                                       op0=ALU.is_gt, op1=ALU.mult).then_inc(prep_dve, 1)
                    if t == 1:
                        dve.wait_ge(prep_pe, 1)
                        nc.vector.reciprocal(in_deg_inv[:, :], small_ps[:, 0:TILES]).then_inc(prep_dve, 1)

                statistics(0, 0, 0)
                over_ticks(dve, first_tick, first=6, lead=1)
                dve.wait_ge(prep_pe, 6)
                nc.vector.tensor_copy(bias[:, 1, D:DX], small_ps[:, 0:GAT_HEADS]).then_inc(prep_dve, 1)
                nc.vector.tensor_copy(w3[:, :, D:DX], small_ps[:, 2 * GAT_HEADS:(2 + DC) * GAT_HEADS]
                                      .rearrange("p (c h) -> p c h", c=DC)).then_inc(prep_dve, 1)
                dve.wait_ge(prep_dve, 6 + DC)

                def layer_tick(layer):
                    def tick(t, s, live):
                        n = (layer - 1) * TILES + t
                        if live(0):
                            scale = in_deg_inv if layer == 1 else r
                            own = one(x[:, ds(t, 1), :])
                            dve.wait_ge(sums_ready, n + 1)
                            nc.vector.scalar_tensor_tensor(out=own, in0=sum_ps[s][:, 0:D], scalar=scale[:, ds(t, 1)],
                                                           in1=own, op0=ALU.mult, op1=ALU.add).then_inc(x_step, 1)
                            dve.wait_ge(x_step, XS * n + 1)
                            nc.vector.scalar_tensor_tensor(out=own, in0=sum_ps[s][:, D:2 * D],
                                                           scalar=scale[:, ds(t, 1)],
                                                           in1=own, op0=ALU.mult, op1=ALU.add).then_inc(x_step, 1)
                            wait_apart(dve, x_step, XS * n + 2, dve_passed)
                            statistics(n + TILES, t, s)
                        if live(2):
                            finish_y(layer + 1, t - 2, s)
                        if live(0):
                            center(n + TILES, t, s)
                    return tick

                over_ticks(dve, layer_tick(1))
                over_ticks(dve, layer_tick(2), first=4)

                def row_weights():
                    dve.wait_ge(y_split, 3 * TILES)
                    step = [0]

                    def link(ins):
                        step[0] += 1
                        ins.then_inc(gat_step, 1)
                        dve.wait_ge(gat_step, step[0])

                    deg = row_sum[:, :].unsqueeze(2).to_broadcast([P, TILES, GAT_HEADS])
                    lrelu, top, e_adj, e_all = (g_tmp[:, i, :, :] for i in range(4))
                    link(nc.vector.scalar_tensor_tensor(out=lrelu, in0=scores[:, :, :], scalar=ALPHA,
                                                        in1=scores[:, :, :], op0=ALU.mult, op1=ALU.max))
                    link(nc.vector.tensor_scalar(top, deg, 1.0, -NEG, ALU.min, ALU.mult))
                    link(nc.vector.scalar_tensor_tensor(out=top, in0=top, scalar=NEG, in1=lrelu,
                                                        op0=ALU.add, op1=ALU.add))
                    link(nc.vector.tensor_tensor(e_adj, lrelu, top, ALU.subtract))
                    link(nc.vector.tensor_scalar(e_adj, e_adj, 0.0, None, ALU.min))
                    link(nc.vector.scalar_tensor_tensor(out=e_all, in0=lrelu, scalar=NEG, in1=top,
                                                        op0=ALU.add, op1=ALU.subtract))
                    dve.wait_ge(gat_exp, 2)
                    link(nc.vector.tensor_scalar(lrelu, deg, -1.0, float(N), ALU.mult, ALU.add))
                    link(nc.vector.tensor_tensor(lrelu, lrelu, e_all, ALU.mult))
                    link(nc.vector.tensor_tensor(top, deg, e_adj, ALU.mult))
                    link(nc.vector.tensor_tensor(top, top, lrelu, ALU.add))
                    link(nc.vector.reciprocal(lrelu, top))
                    link(nc.vector.tensor_scalar(lrelu, lrelu, 1.0 / GAT_HEADS, None, ALU.mult))
                    link(nc.vector.tensor_tensor(e_adj, e_adj, e_all, ALU.subtract))
                    link(nc.vector.tensor_tensor(w_adj[:, :, :], e_adj, lrelu, ALU.mult))
                    link(nc.vector.tensor_tensor(w_all[:, :, :], e_all, lrelu, ALU.mult))

                def out_tick(t, s, live):
                    if live(0):
                        n = 2 * TILES + t
                        dve.wait_ge(sums_ready, n + 1)
                        wait(dve, x_turned, n + TILES - 1)
                        nc.vector.tensor_copy(u[:, s, :], sum_ps[s][:, 0:D]).then_inc(x_step, 1)
                        dve.wait_ge(x_step, XS * n + 1)
                        nc.vector.tensor_tensor(u[:, s, :], sum_ps[s][:, D:2 * D], u[:, s, :], ALU.add)\
                            .then_inc(x_step, 1)
                    if isinstance(t, int) and t == 1:
                        row_weights()
                    if isinstance(t, int) and t == 2:
                        dve.wait_ge(prep_act, 6)
                    if live(2):
                        o = t - 2
                        to = acc[:, s, :]
                        if isinstance(o, int):
                            wait(dve, out_stored[s], 16 * (o // 2))
                        else:
                            dve.wait_ge(out_stored[s], (o - s) * 8)
                        k = 0
                        for h in range(GAT_HEADS):
                            src = all_k[:, h, :]
                            wgt = w_all[:, ds(o, 1), h]
                            if h == 0:
                                nc.vector.tensor_scalar(to, src, wgt, None, ALU.mult).then_inc(z_step, 1)
                            else:
                                nc.vector.scalar_tensor_tensor(out=to, in0=src, scalar=wgt, in1=to,
                                                               op0=ALU.mult, op1=ALU.add).then_inc(z_step, 1)
                            k += 1
                            dve.wait_ge(z_step, 2 * GAT_HEADS * o + k)
                        dve.wait_ge(z_ready, o + 1)
                        for h in range(GAT_HEADS):
                            z = z_ps[s][h // 2][:, (h % 2) * D:(h % 2 + 1) * D]
                            nc.vector.scalar_tensor_tensor(out=to, in0=z, scalar=w_adj[:, ds(o, 1), h], in1=to,
                                                           op0=ALU.mult, op1=ALU.add).then_inc(z_step, 1)
                            k += 1
                            dve.wait_ge(z_step, 2 * GAT_HEADS * o + k)
                        nc.vector.scalar_tensor_tensor(out=to, in0=to, scalar=0.0, in1=one(x[:, ds(o, 1), :]),
                                                       op0=ALU.max, op1=ALU.add).then_inc(out_ready, 1)

                over_ticks(dve, out_tick, first=4)

            @block.scalar
            def _(act):
                def relu(n, s, func=ACT.Relu):
                    act.wait_ge(x_turned, n + 1)
                    if func == ACT.Relu:
                        wait(act, dense_ready, n - 1)
                    else:
                        act.wait_ge(dense_ready, 3 * TILES)
                        wait(act, z_ready, n - 1 - 3 * TILES)
                    nc.scalar.activation(hT[:, s, :, :], turn_ps[0][:, 0:D].rearrange("p (c n) -> p c n", c=DC),
                                         func).then_inc(h_ready, 1)

                def deviation(n, s):
                    act.wait_ge(stats_ready, n + 1)
                    nc.scalar.activation(std[:, s:s + 1], mv[:, s, 1:2], ACT.Sqrt, bias=eps[:, :])\
                        .then_inc(std_ready, 1)

                def widen(n, t, s):
                    wait(act, sums_ready, n - 1)
                    nc.scalar.activation(block_T[:, s, :], one(adj_T[:, ds(t, 1), :]), ACT.Copy)\
                        .then_inc(block_ready, 1)

                def keep(t, q):
                    act.wait_ge(adj_turned, QUARTERS * t + q + 1)
                    nc.scalar.activation(adj_T[:, ds(t, 1), q * BANK:(q + 1) * BANK].rearrange("p a n -> p (a n)"),
                                         adj_banks[q][:, :], ACT.Copy).then_inc(adj_kept, 1)

                def first_tick(t, s, live):
                    if isinstance(t, int) and t == 3:
                        act.wait_ge(prep_pe, 2)
                        nc.scalar.activation(w2b_T[:, :], small_ps[:, 0:D], ACT.Copy).then_inc(prep_act, 1)
                    if isinstance(t, int) and t == 5:
                        act.wait_ge(prep_pe, 4)
                        nc.scalar.activation(w2[:, :, :].rearrange("p c o -> p (c o)"), small_ps[:, :], ACT.Copy)\
                            .then_inc(prep_act, 1)
                    if isinstance(t, int) and t == TILES - 2:
                        act.wait_ge(prep_pe, 5)
                        nc.scalar.activation(wn_T[:, :, :].rearrange("p d o -> p (d o)"), small_ps[:, :], ACT.Copy)\
                            .then_inc(prep_act, 1)
                    if live(0):
                        keep(t, 0)
                        keep(t, 1)
                    if live(1):
                        relu(t - 1, 1 - s)
                    if live(-1):
                        deviation(t + 1, 1 - s)
                    if live(0):
                        keep(t, 2)
                        keep(t, 3)
                    if not isinstance(t, int):
                        return
                    if t == 0:
                        act.wait_ge(deg_ready, 1)
                        nc.scalar.activation(r_any[:, :], deg1[:, :], ACT.Sqrt).then_inc(deg_root, 1)
                    if t == TILES - 1:
                        act.wait_ge(adj_kept, QUARTERS)
                        widen(0, 0, 0)
                    if t == TILES:
                        widen(1, 1, 1)

                deviation(0, 0)
                over_ticks(act, first_tick, first=6, lead=1)

                def layer_tick(layer):
                    def tick(t, s, live):
                        n = (layer - 1) * TILES + t
                        if live(-1):
                            if live(1):
                                widen(n + 1, t + 1, 1 - s)
                        elif layer < 3 and t <= TILES:
                            widen(n + 1, t + 1 - TILES, 1 - s)
                        if live(1):
                            relu(n - 1 + TILES, 1 - s, ACT.Relu if layer < 3 else ACT.Copy)
                        if live(0) and layer < 3:
                            deviation(n + TILES, s)
                    return tick

                over_ticks(act, layer_tick(1), lead=1)
                over_ticks(act, layer_tick(2), lead=1)

                def last_tick(t, s, live):
                    layer_tick(3)(t, s, live)
                    if isinstance(t, int) and t == 0:
                        act.wait_ge(prep_pe, 7)
                        nc.scalar.activation(all_sum_T[:, :, :], small_ps[:, 0:D].rearrange("p (c n) -> p c n", c=DC),
                                             ACT.Copy).then_inc(prep_act, 1)
                    if isinstance(t, int) and t == 1:
                        act.wait_ge(gat_step, 6)
                        for i in (2, 3):
                            nc.scalar.activation(g_tmp[:, i, :, :], g_tmp[:, i, :, :], ACT.Exp).then_inc(gat_exp, 1)
                        act.wait_ge(prep_pe, 8)
                        for i in range(2):
                            nc.scalar.activation(all_k[:, 2 * i:2 * i + 2, :].rearrange("p h f -> p (h f)"),
                                                 dense_ps[i][:, :], ACT.Copy).then_inc(prep_act, 1)

                over_ticks(act, last_tick, first=4, lead=1)

            @block.tensor
            def _(pe):
                def turn(n, s, src):
                    pe.wait_ge(centred, n + 1) if src is xc else pe.wait_ge(x_step, XS * (n - TILES) + 2)
                    wait(pe, h_ready, n)
                    for d in range(DC):
                        last = nc.tensor.transpose(turn_ps[0][:, d * P:(d + 1) * P],
                                                   src[:, s, d * P:(d + 1) * P], ident["i"][:, :])
                    last.then_inc(x_turned, 1)

                def dense(layer, n, s):
                    pe.wait_ge(h_ready, n + 1)
                    wait(pe, y_step, YS * (n - 2) + 1)
                    weights, width = ((w1, D), (w2, D), (w3, DX))[layer - 1]
                    for d in range(DC):
                        last = nc.tensor.matmul(dense_ps[s][:, 0:width], hT[:, s, d, :], weights[:, d, :],
                                                start=(d == 0), stop=(d == DC - 1))
                    last.then_inc(dense_ready, 1)

                def sums(layer, n, t, s, nodes=range(TILES)):
                    src = parts[layer % 2]
                    if nodes[0] == 0:
                        pe.wait_ge(block_ready, n + 1)
                        wait(pe, x_step, XS * (n - 1))
                        if layer == 2:
                            nc.tensor.matmul(sum_ps[s][:, :], ident_r[:, :], src[:, ds(t, 1), :, :],
                                             start=True, stop=False)
                    for j in nodes:
                        last = nc.tensor.matmul(sum_ps[s][:, :], block_T[:, s, j * P:(j + 1) * P],
                                                src[:, j, :, :], start=(j == 0 and layer != 2),
                                                stop=(j == TILES - 1))
                    if nodes[-1] == TILES - 1:
                        last.then_inc(sums_ready, 1)

                def finish_layer(layer, t, turn_last, make_dense):
                    n = layer * TILES
                    most = TILES - 3
                    if t == TILES:
                        if layer == 0:
                            turn_last()
                        pe.wait_ge(y_split, n + most)
                        sums(layer + 1, n, 0, 0, range(0, TILES // 2))
                        make_dense()
                        sums(layer + 1, n, 0, 0, range(TILES // 2, most))
                        if layer > 0:
                            turn_last()
                        sums(layer + 1, n + 1, 1, 1, range(0, TILES // 4))
                    else:
                        make_dense()
                        sums(layer + 1, n + 1, 1, 1, range(TILES // 4, TILES // 2 + 2))
                        pe.wait_ge(y_split, n + TILES)
                        sums(layer + 1, n, 0, 0, range(most, TILES))
                        sums(layer + 1, n + 1, 1, 1, range(TILES // 2 + 2, TILES))

                def turn_adj(t, s, q):
                    wait(pe, adj_kept, QUARTERS * (t - 1) + q + 1)
                    for b in range(QB):
                        m = q * QB + b
                        last = nc.tensor.transpose(adj_banks[q][:, b * P:(b + 1) * P],
                                                   adj[:, s, m * P:(m + 1) * P], ident["i"][:, :])
                    last.then_inc(adj_turned, 1)

                def first_tick(t, s, live):
                    if not live(0):
                        finish_layer(0, t, lambda: turn(t - 1, 1 - s, xc), lambda: dense(1, t - 2, s))
                        return
                    came = (t - s) * 8
                    if not isinstance(t, int) or t >= 2:
                        pe.wait_ge(adj_in[s][0], came)
                    turn_adj(t, s, 0)
                    turn_adj(t, s, 1)
                    if live(1):
                        turn(t - 1, 1 - s, xc)
                    if not isinstance(t, int) or t >= 2:
                        pe.wait_ge(adj_in[s][1], came)
                    turn_adj(t, s, 2)
                    if live(2):
                        dense(1, t - 2, s)
                    turn_adj(t, s, 3)
                    if isinstance(t, int):
                        prepare(t)

                def prepare(t):
                    if t == 0:
                        pe.wait_ge(prep_pool, 3)
                        for c in range(TILES):
                            last = nc.tensor.matmul(small_ps[:, c:c + 1], col_count[:, c * P:(c + 1) * P],
                                                    ones_b[:, :], start=True, stop=True)
                        last.then_inc(prep_pe, 1)
                    if t == 2:
                        pe.wait_ge(w2_loaded, 16 * W2_LOADS)
                        pe.wait_ge(prep_dve, 3)
                        for c in range(DC):
                            last = nc.tensor.transpose(small_ps[:, c * P:(c + 1) * P], w2b[:, c, :], ident["i"][:, :])
                        last.then_inc(prep_pe, 1)
                    if t == 3:
                        pe.wait_ge(prep_pool, 4)
                        pe.wait_ge(prep_act, 1)
                        nc.tensor.matmul(small_ps[:, D:2 * D], b_bc[:, 0, :], w2b_T[:, :], start=True, stop=True)\
                            .then_inc(prep_pe, 1)
                    if t == 4:
                        pe.wait_ge(prep_dve, 4)
                        for c in range(DC):
                            last = nc.tensor.matmul(small_ps[:, c * D:(c + 1) * D], w2a[:, c * P:(c + 1) * P],
                                                    w2b_T[:, :], start=True, stop=True)
                        last.then_inc(prep_pe, 1)
                    if t == 5:
                        pe.wait_ge(prep_act, 2)
                        for d in range(DC):
                            for c in range(DC):
                                last = nc.tensor.transpose(small_ps[:, (d * DC + c) * P:(d * DC + c + 1) * P],
                                                           w3[:, c, d * P:(d + 1) * P], ident["i"][:, :])
                        last.then_inc(prep_pe, 1)
                    if t == TILES - 2:
                        pe.wait_ge(prep_dve, 4 + DC)
                        pe.wait_ge(prep_pool, 5 + 2 * DC)
                        pe.wait_ge(prep_act, 3)
                        for d in range(DC):
                            nc.tensor.matmul(small_ps[:, 0:GAT_HEADS], b_bc[:, 1 + d, :], va[:, d, :],
                                             start=(d == 0), stop=(d == DC - 1))
                        for c in range(DC):
                            for d in range(DC):
                                last = nc.tensor.matmul(small_ps[:, (2 + c) * GAT_HEADS:(3 + c) * GAT_HEADS],
                                                        wn_T[:, d, c * P:(c + 1) * P], va[:, d, :],
                                                        start=(d == 0), stop=(d == DC - 1))
                        last.then_inc(prep_pe, 1)

                over_ticks(pe, first_tick, first=6, lead=1)

                def layer_tick(layer):
                    def tick(t, s, live):
                        n = (layer - 1) * TILES + t

                        def turn_next():
                            turn(n - 1 + TILES, 1 - s, xc)

                        def make_dense():
                            dense(layer + 1, n - 2 + TILES, s)

                        if not live(0):
                            finish_layer(layer, t, turn_next, make_dense)
                            return
                        if live(2):
                            sums(layer, n, t, s)
                        if live(1):
                            turn_next()
                        if live(2):
                            make_dense()
                    return tick

                over_ticks(pe, layer_tick(1))
                pe.wait_ge(prep_dve, 6 + DC)
                over_ticks(pe, layer_tick(2))

                def out_tick(t, s, live):
                    n = 2 * TILES + t
                    if live(0) and live(2):
                        sums(3, n, t, s)
                    if isinstance(t, int) and t == 0:
                        pe.wait_ge(y_summed, TILES)
                        for c in range(DC):
                            last = nc.tensor.matmul(small_ps[:, c * P:(c + 1) * P], y_sum[:, c * P:(c + 1) * P],
                                                    ones[:, :], start=True, stop=True)
                        last.then_inc(prep_pe, 1)
                    if isinstance(t, int) and t == 1:
                        pe.wait_ge(prep_act, 4)
                        pe.wait_ge(y_step, YS * 3 * TILES)
                        for i in range(2):
                            for c in range(DC):
                                last = nc.tensor.matmul(dense_ps[i][:, :], all_sum_T[:, c, :],
                                                        gat_k[:, c, 2 * i:2 * i + 2, :],
                                                        start=(c == 0), stop=(c == DC - 1))
                        last.then_inc(prep_pe, 1)
                    if isinstance(t, int) and t == 2:
                        pe.wait_ge(prep_act, 6)
                    if live(1):
                        turn(n - 1 + TILES, 1 - s, u)
                    if live(2):
                        o = t - 2
                        pe.wait_ge(h_ready, n - 2 + TILES + 1)
                        wait(pe, z_step, 2 * GAT_HEADS * (o - 1))
                        for i in range(2):
                            for c in range(DC):
                                last = nc.tensor.matmul(z_ps[s][i][:, :], hT[:, s, c, :],
                                                        gat_k[:, c, 2 * i:2 * i + 2, :],
                                                        start=(c == 0), stop=(c == DC - 1))
                        last.then_inc(z_ready, 1)

                over_ticks(pe, out_tick, first=4)


def build(nc, dram, out):
    with ExitStack() as ctx:
        def sb(name, shape, dt=F32):
            return ctx.enter_context(nc.sbuf_tensor(name, shape, dt))

        x = sb("x", [P, TILES, D])
        ident = {name: sb("ident_" + name, [P, P]) for name in ("i", "not", "bias")}
        eps = sb("eps", [P, 1])
        col_count = sb("col_count", [P, N], BF16)
        row_sum = sb("row_sum", [P, TILES])
        mask = sb("mask", [P, 2, N])
        w1 = sb("w1", [P, DC, D])
        bias1 = sb("bias1", [P, D])
        with ExitStack() as heads:
            k_stack = heads.enter_context(nc.sbuf_tensor("k_stack", [P, HEADS, N], F32R))
            v = heads.enter_context(nc.sbuf_tensor("v", [P, TILES, HEADS * HD], F32))
            w = {"q": heads.enter_context(nc.sbuf_tensor("wq", [P, DC, HEADS * HD], F32)),
                 "o": heads.enter_context(nc.sbuf_tensor("wo", [P, PAIRS, D], F32))}
            mv = heads.enter_context(nc.sbuf_tensor("mean_var", [P, TILES, 2], F32))
            rstd = heads.enter_context(nc.sbuf_tensor("rstd", [P, TILES], F32))
            q_hi = heads.enter_context(nc.sbuf_tensor("q_hi", [P, PAIRS, P], F32R))
            q_lo = heads.enter_context(nc.sbuf_tensor("q_lo", [P, PAIRS, P], F32R))
            q_stack = heads.enter_context(nc.sbuf_tensor("q_stack", [P, HEADS, 2, P], F32R))
            project_keys_values(nc, x, mask, q_hi, q_lo, q_stack, k_stack, v, w, ident, eps, mv, rstd,
                                row_sum, col_count, dram)
            attend(nc, x, mask, q_hi, q_lo, q_stack, k_stack, v, w, ident, mv, rstd, row_sum, col_count,
                   w1, bias1, dram)
        graph_layers(nc, x, mask, ident, eps, row_sum, col_count, w1, bias1, dram, out)


_INS = ["x", "adj", "L0_gnn_Wks", "L0_gnn_Wqs", "L0_gnn_Wvs", "L0_gnn_Wo", "L1_gnn_W", "L1_gnn_b",
        "L2_gnn_W1", "L2_gnn_b1", "L2_gnn_W2", "L2_gnn_b2", "L3_gnn_W_node", "L3_gnn_b_node",
        "L3_gnn_K", "L3_gnn_A_self", "L3_gnn_A_neigh"]


def kernel(**inputs):
    import numpy as _np
    import concourse.bacc as _bacc
    from concourse import mybir as _mybir
    from concourse.bass_utils import run_bass_kernel_spmd as _run

    nc = _bacc.Bacc("TRN2", target_bir_lowering=False, num_devices=1)
    arrays, dram = {}, {}
    for name in _INS:
        a = _np.ascontiguousarray(inputs[name])
        arrays[f"in_{name}_dram"] = a
        dram[name] = nc.dram_tensor(f"in_{name}_dram", a.shape, _mybir.dt.from_np(a.dtype),
                                    kind="ExternalInput").ap()
    out = nc.dram_tensor("out_dram", (N, D), _mybir.dt.float32, kind="ExternalOutput").ap()
    build(nc, dram, out)
    r = _run(nc, [arrays], core_ids=[0])
    return r.results[0]["out_dram"]
```
